# Optimizing a Trainium2 kernel written in Bass

```python
import numpy as np
import jax
import jax.numpy as jnp

def _softmax(x, axis=-1):
    return jax.nn.softmax(x, axis=axis)

def _gelu(x):
    return jax.nn.gelu(x, approximate=True)

def _silu(x):
    return jax.nn.silu(x)

def _sigmoid(x):
    return jax.nn.sigmoid(x)

def _layernorm(x, axis=-1, eps=1e-05):
    m = jnp.mean(x, axis=axis, keepdims=True)
    v = jnp.var(x, axis=axis, keepdims=True)
    return (x - m) / jnp.sqrt(v + eps)

def _scatter_add(tgt, idx, src, axis=0):
    return tgt.at[idx].add(src)

def _segment_sum(src, seg, n):
    return jax.ops.segment_sum(src, seg, n)
kernel_name = 'mk_gnn_preln_d4_gnn_r32_821a44'

def setup_inputs(seed: int=0):
    np.random.seed(seed)
    _w = jnp.asarray

    def _rec_inputs():
        import jax
        import jax.numpy as jnp
        _gk = jax.random.key(seed)
        x = 0.0001712 + 1 * jax.random.normal(jax.random.fold_in(_gk, 1), (3125, 16), jnp.float32)
        _s = jax.random.randint(jax.random.fold_in(_gk, 2), (50000,), 0, 3125, jnp.int32)
        _d = jax.random.randint(jax.random.fold_in(_gk, 3), (50000,), 0, 3125, jnp.int32)
        _loop = jnp.arange(3125, dtype=jnp.int32)
        src = jnp.concatenate([_s, _d, _loop])
        dst = jnp.concatenate([_d, _s, _loop])
        _o = jnp.argsort(dst, stable=True)
        src = src[_o]
        dst = dst[_o]
        edge_attr_16 = -0.00010739 + 0.99994 * jax.random.normal(jax.random.fold_in(_gk, 12), (103125, 16), jnp.float32)
        edge_attr_3 = -1.09012e-05 + 0.99985 * jax.random.normal(jax.random.fold_in(_gk, 13), (103125, 3), jnp.float32)
        edge_attr_48 = -3.69585e-06 + 0.999911 * jax.random.normal(jax.random.fold_in(_gk, 14), (103125, 48), jnp.float32)
        edge_type_8 = jax.random.randint(jax.random.fold_in(_gk, 17), (103125,), 0, 8, jnp.int32)
        edge_weight = jax.random.uniform(jax.random.fold_in(_gk, 18), (103125,), jnp.float32, 0.0, 1)
        return (x, src, dst, edge_attr_16, edge_attr_3, edge_attr_48, edge_type_8, edge_weight)
    x, src, dst, edge_attr_16, edge_attr_3, edge_attr_48, edge_type_8, edge_weight = _rec_inputs()

    def _L0_gnn_setup():
        import jax, jax.numpy as jnp
        import numpy as np
        N_NODES = 50000
        N_EDGES = 25000
        NODE_DIM = 16
        EDGE_DIM = 16
        key = jax.random.key(seed)
        k1, k2, k3, k4 = jax.random.split(key, 4)
        node_features = jax.random.normal(k1, (N_NODES, NODE_DIM), dtype=jnp.float32)
        edge_features = jax.random.normal(k2, (N_EDGES, EDGE_DIM), dtype=jnp.float32)
        pair_indices = jax.random.randint(k3, (N_EDGES, 2), 0, N_NODES, dtype=jnp.int64)
        limit = float(np.sqrt(6.0 / (EDGE_DIM + NODE_DIM * NODE_DIM)))
        kernel = jax.random.uniform(k4, (EDGE_DIM, NODE_DIM * NODE_DIM), minval=-limit, maxval=limit, dtype=jnp.float32)
        bias = jnp.zeros((NODE_DIM * NODE_DIM,), dtype=jnp.float32)
        return {'node_features': node_features, 'edge_features': edge_features, 'pair_indices': pair_indices, 'kernel': kernel, 'bias': bias}
    _L0_gnn_all = _L0_gnn_setup()
    _L0_gnn_in = {k: v for k, v in _L0_gnn_all.items() if k in ('kernel', 'bias')}
    del _L0_gnn_all

    def _L1_gnn_setup():
        import jax, jax.numpy as jnp
        import numpy as np
        N_NODES = 3125
        N_EDGES = 31250
        MSG_DIM = 16
        HID_DIM = 16
        N_EDGE_TYPE = 8
        key = jax.random.key(seed)
        ks = jax.random.split(key, 9)
        features = jax.random.normal(ks[0], (N_NODES, HID_DIM), dtype=jnp.float32)
        edge_src = jax.random.randint(ks[1], (N_EDGES,), 0, N_NODES, dtype=jnp.int32)
        edge_dst = jax.random.randint(ks[2], (N_EDGES,), 0, N_NODES, dtype=jnp.int32)
        edge_type = jax.random.randint(ks[3], (N_EDGES,), 0, N_EDGE_TYPE, dtype=jnp.int32)
        edge_emb = jax.random.normal(ks[4], (N_EDGE_TYPE, MSG_DIM * HID_DIM), dtype=jnp.float32) * 0.1
        s = 1.0 / np.sqrt(HID_DIM)
        w_ih = jax.random.uniform(ks[5], (3 * HID_DIM, MSG_DIM), minval=-s, maxval=s, dtype=jnp.float32)
        w_hh = jax.random.uniform(ks[6], (3 * HID_DIM, HID_DIM), minval=-s, maxval=s, dtype=jnp.float32)
        b_ih = jax.random.uniform(ks[7], (3 * HID_DIM,), minval=-s, maxval=s, dtype=jnp.float32)
        b_hh = jax.random.uniform(ks[8], (3 * HID_DIM,), minval=-s, maxval=s, dtype=jnp.float32)
        return {'features': features, 'edge_src': edge_src, 'edge_dst': edge_dst, 'edge_type': edge_type, 'edge_emb': edge_emb, 'w_ih': w_ih, 'w_hh': w_hh, 'b_ih': b_ih, 'b_hh': b_hh}
    _L1_gnn_all = _L1_gnn_setup()
    _L1_gnn_in = {k: v for k, v in _L1_gnn_all.items() if k in ('edge_emb', 'w_ih', 'w_hh', 'b_ih', 'b_hh')}
    del _L1_gnn_all

    def _L2_gnn_setup():
        import jax, jax.numpy as jnp
        import numpy as np
        N_NODES = 3125
        N_EDGES = 100000
        DIM = 16
        B, K, C, D, E, H = (0.1, 5.0, 1.0, 5.0, 0.9, 0.1)
        E_ = E
        key = jax.random.key(seed)
        k1, k2, k3, k4 = jax.random.split(key, 4)
        x = jax.random.uniform(k1, (N_NODES, DIM), dtype=jnp.float32)
        edge_src = jax.random.randint(k2, (N_EDGES,), 0, N_NODES, dtype=jnp.int32)
        edge_dst = jax.random.randint(k3, (N_EDGES,), 0, N_NODES, dtype=jnp.int32)
        edge_vals = jax.random.uniform(k4, (N_EDGES,), dtype=jnp.float32)
        return {'x': x, 'edge_src': edge_src, 'edge_dst': edge_dst, 'edge_vals': edge_vals}
    _L2_gnn_all = _L2_gnn_setup()
    _L2_gnn_in = {k: v for k, v in _L2_gnn_all.items() if k in ()}
    del _L2_gnn_all

    def _L3_gnn_setup():
        import jax, jax.numpy as jnp
        import numpy as np
        NS, NV = (16, 4)
        EPS = 1e-05
        N_NODES, N_EDGES = (1250, 12500)

        def _bn_scalar(x, g, b):
            m = x.mean(0)
            v = ((x - m) ** 2).mean(0)
            return (x - m) / jnp.sqrt(v + EPS) * g + b

        def _seg_mean(x, idx, n):
            s = jax.ops.segment_sum(x, idx, num_segments=n)
            c = jax.ops.segment_sum(jnp.ones((idx.shape[0],), x.dtype), idx, num_segments=n)
            return s / jnp.maximum(c, 1.0)[:, None]

        def _edge_weights(edge_attr, w1, b1, w2, b2):
            h = jax.nn.relu(edge_attr @ w1 + b1)
            return h @ w2 + b2

        def _forward(node_attr, edge_attr, edge_vec, fc0_w1, fc0_b1, fc0_w2, fc0_b2, fc1_w1, fc1_b1, fc1_w2, fc1_b2, bn0_gs, bn0_bs, bn0_gv, bn1_gs, bn1_bs, edge_index):
            N = node_attr.shape[0]
            E = edge_attr.shape[0]
            src, dst = (edge_index[0], edge_index[1])
            rhat = edge_vec / (jnp.linalg.norm(edge_vec, axis=-1, keepdims=True) + 1e-12)
            sh1 = rhat * float(np.sqrt(3.0))
            w = _edge_weights(edge_attr, fc0_w1, fc0_b1, fc0_w2, fc0_b2)
            wa = w[:, :NS * NS].reshape(E, NS, NS)
            wb = w[:, NS * NS:].reshape(E, NS, NV)
            x = node_attr[dst]
            inv = float(1.0 / np.sqrt(NS))
            msg_s = jnp.einsum('ei,eij->ej', x, wa) * inv
            msg_v = jnp.einsum('ei,eij,ec->ejc', x, wb, sh1) * inv
            msg = jnp.concatenate([msg_s, msg_v.reshape(E, NV * 3)], axis=-1)
            out = _seg_mean(msg, src, N)
            s0 = _bn_scalar(out[:, :NS], bn0_gs, bn0_bs)
            v0 = out[:, NS:].reshape(N, NV, 3)
            vn = jnp.sqrt((v0 ** 2).mean(axis=(0, 2)) + EPS)
            v0 = v0 / vn[None, :, None] * bn0_gv[None, :, None]
            w = _edge_weights(edge_attr, fc1_w1, fc1_b1, fc1_w2, fc1_b2)
            wa = w[:, :NS * NS].reshape(E, NS, NS)
            wb = w[:, NS * NS:].reshape(E, NV, NS)
            s = s0[dst]
            v = v0[dst]
            path_a = jnp.einsum('ei,eij->ej', s, wa)
            path_b = jnp.einsum('eic,ec,eij->ej', v, sh1, wb) * float(1.0 / np.sqrt(3.0))
            msg = (path_a + path_b) * float(1.0 / np.sqrt(NS + NV))
            node1 = _seg_mean(msg, src, N)
            return _bn_scalar(node1, bn1_gs, bn1_bs)
        key = jax.random.key(seed)
        ks = jax.random.split(key, 8)
        d = 3 * NS
        wn = NS * NS + NS * NV
        g = lambda k, shape, sc: jax.random.normal(k, shape, jnp.float32) * sc
        return {'node_attr': g(ks[0], (N_NODES, NS), 1.0), 'edge_attr': g(ks[1], (N_EDGES, d), 1.0), 'edge_vec': g(ks[2], (N_EDGES, 3), 1.0), 'fc0_w1': g(ks[3], (d, d), d ** (-0.5)), 'fc0_b1': jnp.zeros((d,), jnp.float32), 'fc0_w2': g(ks[4], (d, wn), d ** (-0.5)), 'fc0_b2': jnp.zeros((wn,), jnp.float32), 'fc1_w1': g(ks[5], (d, d), d ** (-0.5)), 'fc1_b1': jnp.zeros((d,), jnp.float32), 'fc1_w2': g(ks[6], (d, wn), d ** (-0.5)), 'fc1_b2': jnp.zeros((wn,), jnp.float32), 'bn0_gs': jnp.ones((NS,), jnp.float32), 'bn0_bs': jnp.zeros((NS,), jnp.float32), 'bn0_gv': jnp.ones((NV,), jnp.float32), 'bn1_gs': jnp.ones((NS,), jnp.float32), 'bn1_bs': jnp.zeros((NS,), jnp.float32), 'edge_index': jax.random.randint(ks[7], (2, N_EDGES), 0, N_NODES)}
    _L3_gnn_all = _L3_gnn_setup()
    _L3_gnn_in = {k: v for k, v in _L3_gnn_all.items() if k in ('fc0_w1', 'fc0_b1', 'fc0_w2', 'fc0_b2', 'fc1_w1', 'fc1_b1', 'fc1_w2', 'fc1_b2', 'bn0_gs', 'bn0_bs', 'bn0_gv', 'bn1_gs', 'bn1_bs')}
    del _L3_gnn_all
    return {'x': x, 'src': src, 'dst': dst, 'edge_attr_16': edge_attr_16, 'edge_attr_3': edge_attr_3, 'edge_attr_48': edge_attr_48, 'edge_type_8': edge_type_8, 'edge_weight': edge_weight, 'L0_gnn_kernel': _L0_gnn_in['kernel'], 'L0_gnn_bias': _L0_gnn_in['bias'], 'L1_gnn_edge_emb': _L1_gnn_in['edge_emb'], 'L1_gnn_w_ih': _L1_gnn_in['w_ih'], 'L1_gnn_w_hh': _L1_gnn_in['w_hh'], 'L1_gnn_b_ih': _L1_gnn_in['b_ih'], 'L1_gnn_b_hh': _L1_gnn_in['b_hh'], 'L3_gnn_fc0_w1': _L3_gnn_in['fc0_w1'], 'L3_gnn_fc0_b1': _L3_gnn_in['fc0_b1'], 'L3_gnn_fc0_w2': _L3_gnn_in['fc0_w2'], 'L3_gnn_fc0_b2': _L3_gnn_in['fc0_b2'], 'L3_gnn_fc1_w1': _L3_gnn_in['fc1_w1'], 'L3_gnn_fc1_b1': _L3_gnn_in['fc1_b1'], 'L3_gnn_fc1_w2': _L3_gnn_in['fc1_w2'], 'L3_gnn_fc1_b2': _L3_gnn_in['fc1_b2'], 'L3_gnn_bn0_gs': _L3_gnn_in['bn0_gs'], 'L3_gnn_bn0_bs': _L3_gnn_in['bn0_bs'], 'L3_gnn_bn0_gv': _L3_gnn_in['bn0_gv'], 'L3_gnn_bn1_gs': _L3_gnn_in['bn1_gs'], 'L3_gnn_bn1_bs': _L3_gnn_in['bn1_bs']}

def reference(x, src, dst, edge_attr_16, edge_attr_3, edge_attr_48, edge_type_8, edge_weight, L0_gnn_kernel, L0_gnn_bias, L1_gnn_edge_emb, L1_gnn_w_ih, L1_gnn_w_hh, L1_gnn_b_ih, L1_gnn_b_hh, L3_gnn_fc0_w1, L3_gnn_fc0_b1, L3_gnn_fc0_w2, L3_gnn_fc0_b2, L3_gnn_fc1_w1, L3_gnn_fc1_b1, L3_gnn_fc1_w2, L3_gnn_fc1_b2, L3_gnn_bn0_gs, L3_gnn_bn0_bs, L3_gnn_bn0_gv, L3_gnn_bn1_gs, L3_gnn_bn1_bs):
    import jax
    import jax.numpy as jnp

    def _L0_gnn_ref(node_features, edge_features, pair_indices, kernel, bias):
        import jax, jax.numpy as jnp
        import numpy as np
        N_NODES = 50000
        N_EDGES = 25000
        NODE_DIM = 16
        EDGE_DIM = 16
        d = node_features.shape[-1]
        edge_mats = (edge_features @ kernel + bias).reshape(-1, d, d)
        neighbors = node_features[pair_indices[:, 1]]
        transformed = jnp.einsum('eij,ej->ei', edge_mats, neighbors)
        aggregated = jax.ops.segment_sum(transformed, pair_indices[:, 0], num_segments=node_features.shape[0])
        return aggregated

    def _L1_gnn_ref(features, edge_src, edge_dst, edge_type, edge_emb, w_ih, w_hh, b_ih, b_hh):
        import jax, jax.numpy as jnp
        import numpy as np
        N_NODES = 3125
        N_EDGES = 31250
        MSG_DIM = 16
        HID_DIM = 16
        N_EDGE_TYPE = 8
        n_nodes = features.shape[0]
        A = edge_emb[edge_type].reshape(-1, MSG_DIM, HID_DIM)
        h_src = features[edge_src]
        msg = jnp.einsum('emh,eh->em', A, h_src)
        m = jax.ops.segment_sum(msg, edge_dst, num_segments=n_nodes)
        gi = m @ w_ih.T + b_ih
        gh = features @ w_hh.T + b_hh
        i_r, i_z, i_n = jnp.split(gi, 3, axis=-1)
        h_r, h_z, h_n = jnp.split(gh, 3, axis=-1)
        r = jax.nn.sigmoid(i_r + h_r)
        z = jax.nn.sigmoid(i_z + h_z)
        n = jnp.tanh(i_n + r * h_n)
        h_new = (1.0 - z) * n + z * features
        return h_new

    def _L2_gnn_ref(x, edge_src, edge_dst, edge_vals):
        import jax, jax.numpy as jnp
        import numpy as np
        N_NODES = 3125
        N_EDGES = 100000
        DIM = 16
        B, K, C, D, E, H = (0.1, 5.0, 1.0, 5.0, 0.9, 0.1)
        E_ = E
        n = x.shape[0]
        f = B + x * (1.0 - x / K) * (x / C - 1.0)
        xi = x[edge_src]
        xj = x[edge_dst]
        msg = edge_vals[:, None] * xi * xj / (D + E_ * xi + H * xj)
        f = f + jax.ops.segment_sum(msg, edge_src, num_segments=n)
        return f

    def _L3_gnn_ref(node_attr, edge_attr, edge_vec, fc0_w1, fc0_b1, fc0_w2, fc0_b2, fc1_w1, fc1_b1, fc1_w2, fc1_b2, bn0_gs, bn0_bs, bn0_gv, bn1_gs, bn1_bs, edge_index):
        import jax, jax.numpy as jnp
        import numpy as np
        NS, NV = (16, 4)
        EPS = 1e-05
        N_NODES, N_EDGES = (1250, 12500)

        def _bn_scalar(x, g, b):
            m = x.mean(0)
            v = ((x - m) ** 2).mean(0)
            return (x - m) / jnp.sqrt(v + EPS) * g + b

        def _seg_mean(x, idx, n):
            s = jax.ops.segment_sum(x, idx, num_segments=n)
            c = jax.ops.segment_sum(jnp.ones((idx.shape[0],), x.dtype), idx, num_segments=n)
            return s / jnp.maximum(c, 1.0)[:, None]

        def _edge_weights(edge_attr, w1, b1, w2, b2):
            h = jax.nn.relu(edge_attr @ w1 + b1)
            return h @ w2 + b2

        def _forward(node_attr, edge_attr, edge_vec, fc0_w1, fc0_b1, fc0_w2, fc0_b2, fc1_w1, fc1_b1, fc1_w2, fc1_b2, bn0_gs, bn0_bs, bn0_gv, bn1_gs, bn1_bs, edge_index):
            N = node_attr.shape[0]
            E = edge_attr.shape[0]
            src, dst = (edge_index[0], edge_index[1])
            rhat = edge_vec / (jnp.linalg.norm(edge_vec, axis=-1, keepdims=True) + 1e-12)
            sh1 = rhat * float(np.sqrt(3.0))
            w = _edge_weights(edge_attr, fc0_w1, fc0_b1, fc0_w2, fc0_b2)
            wa = w[:, :NS * NS].reshape(E, NS, NS)
            wb = w[:, NS * NS:].reshape(E, NS, NV)
            x = node_attr[dst]
            inv = float(1.0 / np.sqrt(NS))
            msg_s = jnp.einsum('ei,eij->ej', x, wa) * inv
            msg_v = jnp.einsum('ei,eij,ec->ejc', x, wb, sh1) * inv
            msg = jnp.concatenate([msg_s, msg_v.reshape(E, NV * 3)], axis=-1)
            out = _seg_mean(msg, src, N)
            s0 = _bn_scalar(out[:, :NS], bn0_gs, bn0_bs)
            v0 = out[:, NS:].reshape(N, NV, 3)
            vn = jnp.sqrt((v0 ** 2).mean(axis=(0, 2)) + EPS)
            v0 = v0 / vn[None, :, None] * bn0_gv[None, :, None]
            w = _edge_weights(edge_attr, fc1_w1, fc1_b1, fc1_w2, fc1_b2)
            wa = w[:, :NS * NS].reshape(E, NS, NS)
            wb = w[:, NS * NS:].reshape(E, NV, NS)
            s = s0[dst]
            v = v0[dst]
            path_a = jnp.einsum('ei,eij->ej', s, wa)
            path_b = jnp.einsum('eic,ec,eij->ej', v, sh1, wb) * float(1.0 / np.sqrt(3.0))
            msg = (path_a + path_b) * float(1.0 / np.sqrt(NS + NV))
            node1 = _seg_mean(msg, src, N)
            return _bn_scalar(node1, bn1_gs, bn1_bs)
        return _forward(node_attr, edge_attr, edge_vec, fc0_w1, fc0_b1, fc0_w2, fc0_b2, fc1_w1, fc1_b1, fc1_w2, fc1_b2, bn0_gs, bn0_bs, bn0_gv, bn1_gs, bn1_bs, edge_index)
    edge_index = jnp.stack([src, dst])
    edge_index_t = jnp.stack([src, dst], axis=1)
    h = jnp.maximum(_layernorm(x, axis=-1), 0.0)
    x = x + _L0_gnn_ref(h, edge_attr_16, edge_index_t, L0_gnn_kernel, L0_gnn_bias)
    h = jnp.maximum(_layernorm(x, axis=-1), 0.0)
    x = x + _L1_gnn_ref(h, src, dst, edge_type_8, L1_gnn_edge_emb, L1_gnn_w_ih, L1_gnn_w_hh, L1_gnn_b_ih, L1_gnn_b_hh)
    h = jnp.maximum(_layernorm(x, axis=-1), 0.0)
    x = x + _L2_gnn_ref(h, src, dst, edge_weight)
    h = jnp.maximum(_layernorm(x, axis=-1), 0.0)
    x = x + _L3_gnn_ref(h, edge_attr_48, edge_attr_3, L3_gnn_fc0_w1, L3_gnn_fc0_b1, L3_gnn_fc0_w2, L3_gnn_fc0_b2, L3_gnn_fc1_w1, L3_gnn_fc1_b1, L3_gnn_fc1_w2, L3_gnn_fc1_b2, L3_gnn_bn0_gs, L3_gnn_bn0_bs, L3_gnn_bn0_gv, L3_gnn_bn1_gs, L3_gnn_bn1_bs, edge_index)
    return x

_drawn_inputs = setup_inputs


def setup_inputs(seed=0):
    import zlib

    import numpy as np

    out = dict(_drawn_inputs(seed))
    spreads = {'L0_gnn_bias': (0.0, 0.1),
     'L3_gnn_fc0_b1': (0.0, 0.522),
     'L3_gnn_fc0_b2': (0.0, 0.544),
     'L3_gnn_fc1_b1': (0.0, 0.755),
     'L3_gnn_fc1_b2': (0.0, 0.45),
     'L3_gnn_bn0_gs': (1.0, 0.6),
     'L3_gnn_bn0_bs': (0.0, 0.8),
     'L3_gnn_bn0_gv': (1.0, 0.6),
     'L3_gnn_bn1_gs': (1.0, 0.6),
     'L3_gnn_bn1_bs': (0.0, 0.616)}
    factors = {'edge_weight': 2.688, 'L1_gnn_b_ih': 5.932, 'L1_gnn_b_hh': 8.0, 'L1_gnn_w_hh': 2.696}
    for name, (base, spread) in spreads.items():
        noise = np.random.default_rng([zlib.crc32(name.encode()), seed]).standard_normal(out[name].shape)
        drawn = base * np.exp(spread * noise) if base else spread * noise
        out[name] = jnp.asarray(drawn.astype(out[name].dtype))
    for name, factor in factors.items():
        out[name] = (out[name] * factor).astype(out[name].dtype)
    return out
```

```python
from contextlib import ExitStack

import concourse.bass as bass
from concourse import mybir

F32 = mybir.dt.float32
F16 = mybir.dt.float16
BF16 = mybir.dt.bfloat16
I32 = mybir.dt.int32
ALU = mybir.AluOpType
ACT = mybir.ActivationFunctionType
AX = mybir.AxisListType

N = 3125
E = 103125
D = 16
TG = 14
NG = 58
T = TG * NG
NPAIR = TG // 2
NP = 98
NC = 4
NPAD = NC * NP * 8
LO = 391
NTYPE = 8
DA = 48
NS, NV = 16, 4
FA = NS + 3 * NV + 1
WN = (NS + NV) * NS
EPS = 1e-5
KB, KK, KC, KD, KE, KH = 0.1, 5.0, 1.0, 5.0, 0.9, 0.1
PADNODE = NPAD - 1
HC = 448
NH = TG * 128 // HC

PHASES = ("net", "gru", "react", "conv0", "conv1")
SUMF = dict(net=D, gru=D, react=D, conv0=FA, conv1=D)
HI = dict(net=8, gru=8, react=8, conv0=4, conv1=8)
IN = dict(net=D, conv0=NS, conv1=NS + NV)
OUTF = dict(net=D, conv0=NS + NV, conv1=NS)
GCOLS = dict(net=D, gru=D, react=D, conv0=D, conv1=32)

NORM = ["mean", "scale", "center", "square", "var", "std", "rstd", "norm", "relu"]
STEPS = {
    "start": NORM,
    "net": ["sums", "turned", "add"] + NORM + ["h turned", "h cols", "types 0", "types 0 out", "types 1",
                                               "types 1 out"],
    "gru": ["sums"] + [f"{s} {k}" for k in range(2) for s in ("gates", "gates in", "gates hid")]
    + ["rz", "sigmoid", "reset", "new in", "tanh", "diff", "update", "blend", "add"] + NORM,
    "react": ["sums", "turned", "f1", "f2", "f3", "f4", "f5", "add", "const"] + NORM,
    "conv0": ["sums", "turned", "node major", "count", "inv count", "quarter", "average", "average v", "sum s",
              "all s", "mean s", "centered", "masked", "squares", "squares v", "sum sq s", "sum sq v", "all sq",
              "var s", "var v", "std", "rstd", "gain", "scaled", "shift", "scaled v"],
    "conv1": ["sums", "turned", "average", "norm 20", "sum s", "all s", "mean s", "centered", "masked", "squares",
              "sum sq s", "all sq", "var s", "std", "rstd", "gain", "scaled", "shift", "add"],
}
STAGES = ["start", *PHASES]
FIRST_STEP = {s: sum(len(STEPS[x]) for x in STAGES[:k]) for k, s in enumerate(STAGES)}


def before(stage, name):
    return FIRST_STEP[stage] + STEPS[stage].index(name)


def ended(stage):
    return FIRST_STEP[stage] + len(STEPS[stage])


def gnn_kernel(nc, x, src, dst, etype, weight, vec, ea16, ea48, net_w, types_w, ih_w, hh_w, ih_b, hh_b,
               w1, w2, gs0, bs0, gv0, gs1, bs1, out):
    with ExitStack() as ctx:
        def sb(name, shape, dt):
            return ctx.enter_context(nc.sbuf_tensor(name, shape, dt))

        def sem(name):
            return ctx.enter_context(nc.semaphore(name))

        def bc(ap, *dims):
            return bass.AP(ap.tensor, ap.offset, [ap.ap[0], *[list(d) for d in dims]])

        table = {p: nc.dram_tensor(f"table_{p}", [NPAD * (NTYPE if p == "gru" else 1), GCOLS[p]], F32).ap()
                 for p in PHASES}

        acc = ctx.enter_context(nc.psum_tensor("acc", [128, 2, 512], F32))
        hidden = ctx.enter_context(nc.psum_tensor("hidden", [128, 2, 512], F32))
        wide = ctx.enter_context(nc.psum_tensor("wide", [128, 4, 512], F32))

        src_i = sb("src_i", [128, T], I32)
        dst_i = sb("dst_i", [128, T], I32)
        typ_i = sb("typ_i", [128, T], I32)
        bits = sb("bits", [128, T], I32)
        key_src8 = sb("key_src8", [128, T, 2], F32)
        key_src4 = sb("key_src4", [128, T, 2], F32)
        key_dst8 = sb("key_dst8", [128, T, 2], F32)
        wgt = sb("wgt", [128, T], F32)
        unit = sb("unit", [128, T, 3], F32)
        len_a = sb("len_a", [128, T], F32)
        len_b = sb("len_b", [128, T], F32)

        lo_vals = sb("lo_vals", [128, 2 * LO], F16)
        hi_vals8 = sb("hi_vals8", [128, 8, D], F16)
        hi_vals4 = sb("hi_vals4", [128, 4, FA], F16)
        zeros = sb("zeros", [128, LO + 1], BF16)
        ident = sb("ident", [128, 128], F32)
        ones = sb("ones", [128, 128], F32)
        mask = sb("mask", [NP, NC * 8], F32)
        eps = sb("eps", [128, 2], F32)
        net_sb = sb("net_sb", [128, D * D], F32)
        types_sb = sb("types_sb", [128, 8 * NTYPE * D], F32)
        ih_sb = sb("ih_sb", [128, 8 * 48], F32)
        hh_sb = sb("hh_sb", [128, 8 * 48], F32)
        gate_b = sb("gate_b", [1, 2, 8 * 48], F32)
        w1_sb = sb("w1_sb", [128, 2, 128], F32)
        w2_sb = sb("w2_sb", [128, 2, WN], F32)
        norms = sb("norms", [NP, 4 * NS + NV], F32)

        idx_a = sb("idx_a", [128, 2, TG], I32)
        idx_b = sb("idx_b", [128, 2, TG], I32)
        key = sb("key", [128, 2, TG, 2], F32)
        rows_a = sb("rows_a", [128, 2, TG, 32], F32)
        rows_b = sb("rows_b", [128, 2, TG, D], F32)
        scal = sb("scal", [128, 2, TG * 3], F32)
        ea = sb("ea", [128, 2, TG * 128], F32)
        hid = sb("hid", [128, 2, TG * 128], F32)
        prod = sb("prod", [128, 2, 2, WN], F32)
        msg = sb("msg", [128, TG, NV + FA], F32)
        vsh = sb("vsh", [128, TG * 12], F32)
        rest = sb("rest", [128, TG * FA], F32)
        parts = sb("parts", [128, 2, TG, 3 * 32], BF16)
        onehot = sb("onehot", [128, TG, 2 * LO], BF16)
        himask = sb("himask", [128, 4, 128], BF16)
        spread = sb("spread", [128, TG, 3 * 128], BF16)
        ra = sb("ra", [128, TG * D], F32)
        rb = sb("rb", [128, TG * D], F32)

        xs = sb("xs", [NP, NC * 8, D], F32)
        hs = sb("hs", [NP, NC * 8, D], F32)
        t0 = sb("t0", [NP, NC * 8, 32], F32)
        t1 = sb("t1", [NP, NC * 8, 32], F32)
        st = sb("st", [NP, 6, NC * 8], F32)
        hcols = sb("hcols", [128, NC * NP], F32)
        sums = sb("sums", [128, 2 * NC * NP], F32)
        gates = sb("gates", [NP, 2, NC * 8 * 48], F32)
        gi = gates[:, 0].rearrange("p (n f) -> p n f", f=48)
        gh = gates[:, 1].rearrange("p (n f) -> p n f", f=48)
        typed = gates[:].rearrange("p a b -> p (a b)")[:, 0:4 * 512].rearrange("p (q f) -> p q f", q=4)
        oa = sb("oa", [NP, NC * 8, FA], F32)
        bn = sb("bn", [NP, 12, NS + NV], F32)

        x_loaded = sem("x_loaded")
        consts_loaded = sem("consts_loaded")
        edges_loaded = sem("edges_loaded")
        pool_consts = sem("pool_consts")
        setup = sem("setup")
        lens = sem("lens")
        step = sem("step")
        tabled = {p: sem(f"tabled_{p}") for p in PHASES}
        idx_in = [sem(f"idx_in{u}") for u in range(2)]
        key_in = [sem(f"key_in{u}") for u in range(2)]
        ea_in = [sem(f"ea_in{u}") for u in range(2)]
        gathered = {p: [sem(f"gathered_{p}{u}") for u in range(2)] for p in PHASES}
        hid_mm = sem("hid_mm")
        hid_relu = sem("hid_relu")
        weights = sem("weights")
        mult = sem("mult")
        reduced = sem("reduced")
        spreadd = sem("spreadd")
        masked = sem("masked")
        summed = sem("summed")
        split = sem("split")
        formed = sem("formed")
        acc_open = sem("acc_open")
        acc_done = sem("acc_done")
        stored = sem("stored")
        rows_free = sem("rows_free")

        def earlier(phase, per_group, phases=PHASES):
            k = PHASES.index(phase)
            return sum((per_group[q] if isinstance(per_group, dict) else per_group) * NG
                       for q in phases if PHASES.index(q) < k)

        CONVS = ("net", "conv0", "conv1")
        FORM = dict(react=6, conv0=1, conv1=2)
        key_count = dict(net=16, gru=16, react=32, conv0=32, conv1=32)
        base_pair = {p: earlier(p, NPAIR) for p in PHASES}
        base_conv = {p: earlier(p, NPAIR, CONVS) for p in PHASES}
        base_split = {p: earlier(p, 4) for p in PHASES}
        base_key = {p: earlier(p, key_count) // 2 for p in PHASES}
        idx_count = dict(net=16, gru=16, react=32, conv0=16, conv1=16)
        base_idx = {p: earlier(p, idx_count) // 2 for p in PHASES}
        base_ea = {p: earlier(p, 16, CONVS) // 2 for p in PHASES}
        base_hid = {p: earlier(p, NH, CONVS[1:]) for p in PHASES}
        base_form = {p: earlier(p, FORM, tuple(FORM)) for p in PHASES}
        gather_count = {p: 16 * TG * (2 if p == "react" else 1) for p in PHASES}
        key_of = dict(net=key_src8, gru=key_dst8, react=key_src8, conv0=key_src4, conv1=key_src8)

        def group_loop(eng, body, last=NG):
            body(0, 0, 0)
            body(1, 1, 0)
            with eng.Fori(0, (last - 2) // 2) as i:
                body(i * 2 + 2, 0, i + 1)
                body(i * 2 + 3, 1, i + 1)

        N_CONST = 15
        N_SQUARED = 19
        N_SETUP = 22

        block = ctx.enter_context(nc.Block())

        @block.sync
        def _(sp):
            xv = x.rearrange("(c p h) f -> p c (h f)", c=NC, p=NP)
            sp.dma_start(xs[:].rearrange("p (c h) f -> p c (h f)", c=NC), xv).then_inc(x_loaded, 16)
            for to, frm in ((src_i, src), (dst_i, dst), (typ_i, etype), (wgt, weight)):
                sp.dma_start(to[:], frm).then_inc(edges_loaded, 16)
            sp.dma_start(unit[:].rearrange("p t c -> p (t c)"), vec).then_inc(edges_loaded, 16)
            for to, frm in ((net_sb[:], net_w), (types_sb[:], types_w), (ih_sb[:], ih_w), (hh_sb[:], hh_w),
                            (gate_b[:, 0], ih_b), (gate_b[:, 1], hh_b),
                            (w1_sb[:, 0], w1[0]), (w1_sb[:, 1], w1[1]), (w2_sb[:, 0], w2[0]), (w2_sb[:, 1], w2[1])):
                sp.dma_start(to, frm).then_inc(consts_loaded, 16)
            at = 0
            for v, n in ((gs0, NS), (gv0, NV), (bs0, NS), (gs1, NS), (bs1, NS)):
                sp.dma_start(norms[:, at:at + n], v.partition_broadcast(NP)).then_inc(consts_loaded, 16)
                at += n

            def table_out(p):
                if p == "gru":
                    rows = table[p].rearrange("(c p r) m -> c p (r m)", c=NC, p=NP)
                    for k in range(2):
                        sp.wait_ge(step, before("net", f"types {k} out") + 1)
                        sp.dma_start(rows[2 * k].rearrange("p (a f) -> p a f", a=2), typed[:, 0:2]).then_inc(tabled[p], 16)
                        sp.dma_start(rows[2 * k + 1].rearrange("p (a f) -> p a f", a=2), typed[:, 2:4]).then_inc(tabled[p], 16)
                else:
                    prev = STAGES[STAGES.index(p) - 1]
                    sp.wait_ge(step, ended(prev))
                    rows = table[p].rearrange("(c p h) f -> p c (h f)", c=NC, p=NP)
                    frm = t1 if p == "conv1" else hs
                    sp.dma_start(rows, frm[:].rearrange("p (c h) f -> p c (h f)", c=NC)).then_inc(tabled[p], 16)

            sp.wait_ge(setup, N_SETUP)
            for p in PHASES:
                table_out(p)

                def load(n, u, m, p=p):
                    cols = bass.ds(n * TG, TG)
                    first = isinstance(n, int)
                    ecols = bass.ds(n * (TG * 128), TG * 128)
                    if p == "net":
                        if not first:
                            sp.wait_ge(weights, n * NPAIR + (base_conv[p] - NPAIR))
                        sp.dma_start(ea[0:D, u], ea16[:, ecols]).then_inc(ea_in[u], 16)
                    if p in ("conv0", "conv1"):
                        if not first:
                            sp.wait_ge(hid_mm, n * NH + (base_hid[p] - NH))
                        sp.dma_start(ea[0:DA, u], ea48[:, ecols]).then_inc(ea_in[u], 16)
                    if not first:
                        sp.wait_ge(gathered[p][u], m * gather_count[p])
                    which = typ_i if p == "gru" else dst_i
                    sp.dma_start(idx_a[:, u], which[:, cols]).then_inc(idx_in[u], 16)
                    if p == "react":
                        sp.dma_start(idx_b[:, u], src_i[:, cols]).then_inc(idx_in[u], 16)
                    if not first:
                        sp.wait_ge(spreadd, n * NPAIR + (base_pair[p] - NPAIR))
                    sp.dma_start(key[:, u], key_of[p][:, cols, :]).then_inc(key_in[u], 16)
                    if p == "react":
                        sp.dma_start(scal[:, u, 0:TG], wgt[:, cols]).then_inc(key_in[u], 16)
                    if p in ("conv0", "conv1"):
                        sp.dma_start(scal[:, u].rearrange("p (t c) -> p t c", c=3), unit[:, cols, :]).then_inc(key_in[u], 16)

                group_loop(sp, load)
            sp.wait_ge(step, ended("conv1"))
            sp.dma_start(out.rearrange("(c p h) f -> p c (h f)", c=NC, p=NP),
                         xs[:].rearrange("p (c h) f -> p c (h f)", c=NC)).then_inc(stored, 16)
            sp.wait_ge(stored, 16)

        @block.gpsimd
        def _(pool):
            g = nc.gpsimd
            g.iota(lo_vals[:], [[1, 2 * LO]], base=0, channel_multiplier=0,
                   allow_small_or_imprecise_dtypes=True).then_inc(pool_consts, 1)
            g.iota(hi_vals8[:], [[1, 8], [0, D]], base=0, channel_multiplier=0,
                   allow_small_or_imprecise_dtypes=True).then_inc(pool_consts, 1)
            g.iota(hi_vals4[:], [[1, 4], [0, FA]], base=0, channel_multiplier=0,
                   allow_small_or_imprecise_dtypes=True).then_inc(pool_consts, 1)
            g.memset(ones[:], 1.0).then_inc(pool_consts, 1)
            pool.wait_ge(pool_consts, 4)
            g.affine_select(out=ident[:], in_=ones[:], compare_op=ALU.is_equal, fill=0.0, base=0,
                            pattern=[[-1, 128]], channel_multiplier=1).then_inc(pool_consts, 1)
            g.affine_select(out=mask[:].rearrange("p (c h) -> p c h", c=NC),
                            in_=ones[0:NP, 0:NC * 8].rearrange("p (c h) -> p c h", c=NC),
                            compare_op=ALU.is_ge, fill=0.0, base=N - 1,
                            pattern=[[-8 * NP, NC], [-1, 8]], channel_multiplier=-8).then_inc(pool_consts, 1)

            for p in PHASES:
                pool.wait_ge(tabled[p], 64 if p == "gru" else 16)

                def gather(n, u, m, p=p):
                    pool.wait_ge(idx_in[u], m * idx_count[p] + (base_idx[p] + idx_count[p]))
                    if not (isinstance(n, int) and n < 2):
                        if p in CONVS:
                            pool.wait_ge(mult, n * NPAIR + (base_conv[p] - NPAIR))
                        elif p == "react":
                            pool.wait_ge(formed, n * FORM[p] + (base_form[p] - FORM[p]))
                        else:
                            pool.wait_ge(split, n * 4 + (base_split[p] - 4))
                    pool.sem_inc(rows_free, 1)
                    for t in range(TG):
                        g.indirect_dma_start(out=rows_a[:, u, t, 0:GCOLS[p]], out_offset=None, in_=table[p],
                                             in_offset=bass.IndirectOffsetOnAxis(ap=idx_a[:, u, t:t + 1], axis=0)
                                             ).then_inc(gathered[p][u], 16)
                        if p == "react":
                            g.indirect_dma_start(out=rows_b[:, u, t, :], out_offset=None, in_=table[p],
                                                 in_offset=bass.IndirectOffsetOnAxis(ap=idx_b[:, u, t:t + 1], axis=0)
                                                 ).then_inc(gathered[p][u], 16)

                group_loop(pool, gather)

        @block.scalar
        def _(act):
            a = nc.scalar

            def at(stage, name):
                act.wait_ge(step, before(stage, name))

            def std(stage):
                at(stage, "std")
                a.activation(st[:, 2], st[:, 1], ACT.Sqrt, bias=eps[0:NP, 0:1], scale=1.0 / D).then_inc(step, 1)

            act.wait_ge(setup, N_SQUARED)
            a.activation(len_b[:], len_a[:], ACT.Sqrt, bias=eps[:, 1:2]).then_inc(lens, 1)
            std("start")

            for p in PHASES:
                if p in CONVS[1:]:
                    def relu(n, u, m, p=p):
                        if not (isinstance(n, int) and n < 2):
                            act.wait_ge(weights, n * NPAIR + (base_conv[p] - NPAIR))
                        for c in range(NH):
                            act.wait_ge(hid_mm, n * NH + (base_hid[p] + c + 1))
                            a.activation(hid[:, u, c * HC:(c + 1) * HC], hidden[:, c % 2, 0:HC],
                                         ACT.Relu).then_inc(hid_relu, 1)

                    group_loop(act, relu)
                at(p, "sums")
                act.wait_ge(acc_done, PHASES.index(p) + 1)
                if p == "conv0":
                    a.activation(sums[0:4 * FA, 0:2 * LO].rearrange("p (a b) -> p a b", a=2), acc[0:4 * FA, :, 0:LO],
                                 ACT.Copy).then_inc(step, 1)
                    at(p, "std")
                    a.activation(bn[:, 5], bn[:, 4], ACT.Sqrt, bias=eps[0:NP, 0:1]).then_inc(step, 1)
                else:
                    a.activation(sums[:, 0:LO + 1], acc[:, 0, 0:LO + 1], ACT.Copy).then_inc(step, 1)
                if p == "net":
                    std(p)
                    at(p, "h cols")
                    a.activation(hcols[:], hidden[:, 0, 0:NC * NP], ACT.Copy).then_inc(step, 1)
                    at(p, "types 0 out")
                    a.activation(typed, wide[0:NP], ACT.Copy).then_inc(step, 1)
                    at(p, "types 1 out")
                    act.wait_ge(tabled["gru"], 32)
                    a.activation(typed, wide[0:NP], ACT.Copy).then_inc(step, 1)
                if p == "gru":
                    for k in range(2):
                        at(p, f"gates in {k}")
                        a.activation(gi[:, 16 * k:16 * k + 16].rearrange("p (a h) f -> p a (h f)", a=2),
                                     wide[0:NP, 0:4:2, 0:384], ACT.Copy).then_inc(step, 1)
                        at(p, f"gates hid {k}")
                        a.activation(gh[:, 16 * k:16 * k + 16].rearrange("p (a h) f -> p a (h f)", a=2),
                                     wide[0:NP, 1:4:2, 0:384], ACT.Copy).then_inc(step, 1)
                    at(p, "sigmoid")
                    a.activation(t0[:], t0[:], ACT.Sigmoid).then_inc(step, 1)
                    at(p, "tanh")
                    a.activation(t1[:, :, 0:D], t1[:, :, 0:D], ACT.Tanh).then_inc(step, 1)
                if p in ("gru", "react"):
                    std(p)
                if p == "conv1":
                    at(p, "std")
                    a.activation(bn[:, 5, 0:NS], bn[:, 4, 0:NS], ACT.Sqrt, bias=eps[0:NP, 0:1]).then_inc(step, 1)

        @block.tensor
        def _(pe):
            m = nc.tensor

            def at(stage, name):
                pe.wait_ge(step, before(stage, name))

            pe.wait_ge(pool_consts, 6)
            pe.wait_ge(setup, N_SETUP)
            pe.wait_ge(consts_loaded, 16 * N_CONST)
            for k, p in enumerate(PHASES):
                H, F = HI[p], SUMF[p]
                NB = 2 if p == "conv0" else 1
                W = dict(net=net_sb[:], conv0=w2_sb[:, 0], conv1=w2_sb[:, 1]).get(p)
                nw = IN[p] * OUTF[p] if p in CONVS else 0
                pe.wait_ge(step, ended(STAGES[k]))
                for b in range(NB):
                    mm = m.matmul(acc[0:H * F, b, 0:LO + 1], zeros[:, 0:H * F], zeros[:], start=True, stop=False)
                mm.then_inc(acc_open, 1)

                def hid_chunk(n, u, c, mth, p=p):
                    if c == 0:
                        pe.wait_ge(ea_in[u], mth * 16 + (base_ea[p] + 16))
                    if not (isinstance(n, int) and n == 0 and c < 2):
                        pe.wait_ge(hid_relu, n * NH + (base_hid[p] + c - 1))
                    m.matmul(hidden[:, c % 2, 0:HC], w1_sb[:, CONVS.index(p) - 1],
                             ea[:, u, c * HC:(c + 1) * HC], start=True, stop=True).then_inc(hid_mm, 1)

                def conv_pair(n, u, j, mth, p=p, W=W, nw=nw):
                    if p == "net":
                        if j == 0:
                            pe.wait_ge(ea_in[u], mth * 16 + (base_ea[p] + 16))
                        lhs = ea
                    else:
                        lhs = hid
                        c = ((2 * j + 2) * 128 - 1) // HC
                        pe.wait_ge(hid_relu, n * NH + (base_hid[p] + c + 1))
                    if not (isinstance(n, int) and n == 0 and j < 2):
                        pe.wait_ge(mult, n * NPAIR + (base_conv[p] + j - 1))
                    for s in range(2):
                        col = (2 * j + s) * 128
                        mm = m.matmul(wide[:, 2 * ((u + j) % 2) + s, 0:nw], lhs[:, u, col:col + 128], W,
                                      start=True, stop=True)
                    mm.then_inc(weights, 1)

                def sum_pair(n, j, p=p, H=H, F=F, NB=NB):
                    pe.wait_ge(spreadd, n * NPAIR + (base_pair[p] + j + 1))
                    for t in (2 * j, 2 * j + 1):
                        for s in range(3):
                            for b in range(NB):
                                mm = m.matmul(acc[0:H * F, b, 0:LO], spread[:, t, s * H * F:(s + 1) * H * F],
                                              onehot[:, t, b * LO:(b + 1) * LO], start=False, stop=False)
                    mm.then_inc(summed, 1)

                def body(n, u, mth, new=True, ahead=True, p=p):
                    for j in range(NPAIR):
                        if p in CONVS[1:] and ahead and j < NH:
                            hid_chunk(n + 1, 1 - u, j, mth + u)
                        if p in CONVS and new and j + 2 < NPAIR:
                            conv_pair(n, u, j + 2, mth)
                        if p in CONVS and ahead and j + 2 >= NPAIR:
                            conv_pair(n + 1, 1 - u, j + 2 - NPAIR, mth + u)
                        if not (isinstance(n, int) and n == 0):
                            sum_pair(n - 1, j)

                if p in CONVS[1:]:
                    for c in range(NH):
                        hid_chunk(0, 0, c, 0)
                if p in CONVS:
                    conv_pair(0, 0, 0, 0)
                    conv_pair(0, 0, 1, 0)
                group_loop(pe, body, NG - 2)
                body(NG - 2, 0, NG // 2 - 1)
                body(NG - 1, 1, NG // 2 - 1, ahead=False)
                body(NG, 0, NG // 2, new=False, ahead=False)
                for b in range(NB):
                    mm = m.matmul(acc[0:H * F, b, 0:LO + 1], zeros[:, 0:H * F], zeros[:], start=False, stop=True)
                mm.then_inc(acc_done, 1)

                if p in ("net", "react", "conv1"):
                    at(p, "turned")
                    for c in range(NC):
                        mm = m.transpose(wide[0:NP, 0, c * 128:(c + 1) * 128], sums[:, c * NP:(c + 1) * NP], ident[:])
                    mm.then_inc(step, 1)
                if p == "net":
                    at(p, "h turned")
                    for c in range(NC):
                        mm = m.transpose(hidden[:, 0, c * NP:(c + 1) * NP],
                                         hs[:, 8 * c:8 * c + 8].rearrange("p h f -> p (h f)"), ident[0:NP, 0:NP])
                    mm.then_inc(step, 1)
                    for k2 in range(2):
                        at(p, f"types {k2}")
                        for q in range(4):
                            c = 2 * k2 + q // 2
                            mm = m.matmul(wide[0:NP, q, :], hcols[:, c * NP:(c + 1) * NP],
                                          types_sb[:, (q % 2) * 512:(q % 2 + 1) * 512], start=True, stop=True)
                        mm.then_inc(step, 1)
                if p == "gru":
                    for k2 in range(2):
                        at(p, f"gates {k2}")
                        for q in range(4):
                            c = 2 * k2 + q // 2
                            frm, w = (hcols, hh_sb) if q % 2 else (sums, ih_sb)
                            m.matmul(wide[0:NP, q, 0:384], frm[:, c * NP:(c + 1) * NP], w[:], start=True, stop=False)
                            mm = m.matmul(wide[0:NP, q, 0:384], ones[0:1, 0:NP], gate_b[:, q % 2], start=False,
                                          stop=True)
                        mm.then_inc(step, 1)
                if p == "conv0":
                    at(p, "turned")
                    for q in range(8):
                        c, b = q // 2, q % 2
                        mm = m.transpose(wide[0:NP, q // 4, (q % 4) * 4 * FA:(q % 4 + 1) * 4 * FA],
                                         sums[0:4 * FA, bass.ds(2 * c * NP + b, NP, step=2)], ident[0:4 * FA, 0:4 * FA])
                    mm.then_inc(step, 1)
                if p in ("conv0", "conv1"):
                    at(p, "all s")
                    m.matmul(hidden[0:NP, 0, 0:NS], ones[0:NP, 0:NP], bn[:, 0, 0:NS], start=True, stop=True).then_inc(step, 1)
                    at(p, "all sq")
                    w = NS + NV if p == "conv0" else NS
                    m.matmul(hidden[0:NP, 1, 0:w], ones[0:NP, 0:NP], bn[:, 2, 0:w], start=True, stop=True).then_inc(step, 1)

        @block.vector
        def _(dve):
            v = nc.vector

            def at(stage, name):
                dve.wait_ge(step, before(stage, name))

            n_set = [0]

            def then(ins):
                n_set[0] += 1
                ins.then_inc(setup, 1)
                dve.wait_ge(setup, n_set[0])

            def norm(stage):
                at(stage, "mean")
                v.tensor_reduce(st[:, 0], xs[:], AX.X, ALU.add).then_inc(step, 1)
                at(stage, "scale")
                v.tensor_scalar(st[:, 3], st[:, 0], 1.0 / D, None, ALU.mult).then_inc(step, 1)
                at(stage, "center")
                v.tensor_tensor(t0[:, :, 0:D], xs[:], bc(st[:, 3], [1, NC * 8], [0, D]), ALU.subtract).then_inc(step, 1)
                at(stage, "square")
                v.tensor_tensor(t1[:, :, 0:D], t0[:, :, 0:D], t0[:, :, 0:D], ALU.mult).then_inc(step, 1)
                at(stage, "var")
                v.tensor_reduce(st[:, 1], t1[:, :, 0:D], AX.X, ALU.add).then_inc(step, 1)
                at(stage, "rstd")
                v.reciprocal(st[:, 4], st[:, 2]).then_inc(step, 1)
                at(stage, "norm")
                v.tensor_tensor(t1[:, :, 0:D], t0[:, :, 0:D], bc(st[:, 4], [1, NC * 8], [0, D]), ALU.mult).then_inc(step, 1)
                at(stage, "relu")
                v.tensor_scalar(hs[:], t1[:, :, 0:D], 0.0, None, ALU.max).then_inc(step, 1)

            v.memset(eps[:, 1:2], 0.0)
            v.memset(zeros[:], 0.0)
            v.memset(sums[:], 0.0)
            v.memset(t1[:], 0.0)
            v.memset(ea[:], 1.0)
            v.memset(msg[:], 1.0)
            then(v.memset(eps[:, 0:1], EPS))
            dve.wait_ge(edges_loaded, 16 * 5)
            for idx, keys, shift in ((src_i, key_src8, 3), (src_i, key_src4, 2), (dst_i, key_dst8, 3)):
                then(v.tensor_scalar(bits[:], idx[:], shift, None, ALU.arith_shift_right))
                then(v.tensor_copy(keys[:, :, 0], bits[:]))
                then(v.tensor_scalar(bits[:], idx[:], (1 << shift) - 1, None, ALU.bitwise_and))
                then(v.tensor_copy(keys[:, :, 1], bits[:]))
            then(v.scalar_tensor_tensor(out=typ_i[:], in0=src_i[:], scalar=float(NTYPE), in1=typ_i[:],
                                        op0=ALU.mult, op1=ALU.add))
            then(v.tensor_tensor(len_b[:], unit[:, :, 1], unit[:, :, 1], ALU.mult))
            then(v.tensor_tensor(len_a[:], unit[:, :, 0], unit[:, :, 0], ALU.mult))
            then(v.tensor_tensor(len_a[:], len_a[:], len_b[:], ALU.add))
            then(v.tensor_tensor(len_b[:], unit[:, :, 2], unit[:, :, 2], ALU.mult))
            then(v.tensor_tensor(len_a[:], len_a[:], len_b[:], ALU.add))
            assert n_set[0] == N_SQUARED
            dve.wait_ge(lens, 1)
            then(v.tensor_scalar(len_a[:], len_b[:], 1e-12, None, ALU.add))
            then(v.reciprocal(len_b[:], len_a[:]))
            then(v.tensor_tensor(unit[:], unit[:], bc(len_b[:], [1, T], [0, 3]), ALU.mult))
            assert n_set[0] == N_SETUP
            dve.wait_ge(x_loaded, 16)
            norm("start")
            dve.wait_ge(pool_consts, 6)
            dve.wait_ge(consts_loaded, 16 * N_CONST)

            for k, p in enumerate(PHASES):
                H, F = HI[p], SUMF[p]
                I, O = IN.get(p), OUTF.get(p)
                lo_n = 2 * LO if p == "conv0" else LO
                hi_vals = hi_vals4 if p == "conv0" else hi_vals8
                first_in = 12 if p == "conv1" else 0

                def form(n, u, m, p=p):
                    dve.wait_ge(key_in[u], m * key_count[p] + (base_key[p] + key_count[p]))
                    dve.wait_ge(gathered[p][u], m * gather_count[p] + gather_count[p])
                    done = [0]

                    def formed_by(ins):
                        done[0] += 1
                        ins.then_inc(formed, 1)
                        dve.wait_ge(formed, n * FORM[p] + (base_form[p] + done[0]))

                    if p == "react":
                        xi = rows_b[:, u].rearrange("p t f -> p (t f)")
                        xj = rows_a[:, u, :, 0:D]
                        wg = scal[:, u, 0:TG]
                        three = lambda ap: ap.rearrange("p (t f) -> p t f", f=D)
                        formed_by(v.tensor_tensor(three(ra[:]), three(xi), xj, ALU.mult))
                        formed_by(v.tensor_tensor(three(ra[:]), three(ra[:]), bc(wg, [1, TG], [0, D]), ALU.mult))
                        formed_by(v.tensor_scalar(three(rb[:]), xj, KH, KD, ALU.mult, ALU.add))
                        formed_by(v.scalar_tensor_tensor(out=rb[:], in0=xi, scalar=KE, in1=rb[:], op0=ALU.mult,
                                                         op1=ALU.add))
                        formed_by(v.reciprocal(rb[:], rb[:]))
                        formed_by(v.tensor_tensor(msg[:, :, 0:D], three(ra[:]), three(rb[:]), ALU.mult))
                    if p == "conv1":
                        vs = vsh[:].rearrange("p (t i c) -> p t i c", t=TG, c=3)
                        formed_by(v.tensor_tensor(vs, rows_a[:, u, :, 0:12].rearrange("p t (i c) -> p t i c", c=3),
                                                  bc(scal[:, u], [3, TG], [0, NV], [1, 3]), ALU.mult))
                        formed_by(v.tensor_reduce(rows_a[:, u, :, 28:32], vs, AX.X, ALU.add))

                def multiply(n, u, j, p=p, I=I, O=O, first_in=first_in):
                    dve.wait_ge(weights, n * NPAIR + (base_conv[p] + j + 1))
                    if not (isinstance(n, int) and n == 0 and j < 2):
                        dve.wait_ge(reduced, n * NPAIR + (base_conv[p] + j - 1))
                    q = (u + j) % 2
                    v.tensor_tensor(prod[:, q, :, 0:I * O].rearrange("p s (o i) -> p s o i", i=I),
                                    wide[:, 2 * q:2 * q + 2, 0:I * O].rearrange("p s (o i) -> p s o i", i=I),
                                    bc(rows_a[:, u, 2 * j, first_in:first_in + I], [32, 2], [0, O], [1, I]),
                                    ALU.mult).then_inc(mult, 1)

                def reduce(n, u, j, p=p, I=I, O=O):
                    dve.wait_ge(mult, n * NPAIR + (base_conv[p] + j + 1))
                    q = (u + j) % 2
                    v.tensor_reduce(msg[:, 2 * j:2 * j + 2, 0:O],
                                    prod[:, q, :, 0:I * O].rearrange("p s (o i) -> p s o i", i=I),
                                    AX.X, ALU.add).then_inc(reduced, 1)

                def spread_pair(n, u, j, p=p, H=H, F=F, lo_n=lo_n, hi_vals=hi_vals):
                    if not (isinstance(n, int) and n == 0):
                        dve.wait_ge(summed, n * NPAIR + (base_pair[p] + j + 1 - NPAIR))
                    for t in (2 * j, 2 * j + 1):
                        h = (2 * u + t) % 4
                        v.tensor_scalar(onehot[:, t, 0:lo_n], lo_vals[:, 0:lo_n], key[:, u, t, 0:1], None, ALU.is_equal)
                        hm = v.tensor_scalar(himask[:, h, 0:H * F], hi_vals[:].rearrange("p h f -> p (h f)"),
                                             key[:, u, t, 1:2], None, ALU.is_equal)
                    hm.then_inc(masked, 1)
                    dve.wait_ge(masked, n * NPAIR + (base_pair[p] + j + 1))
                    for t in (2 * j, 2 * j + 1):
                        h = (2 * u + t) % 4
                        sp_ = v.tensor_tensor(spread[:, t, 0:3 * H * F].rearrange("p (s h f) -> p s h f", s=3, h=H),
                                              bc(parts[:, u, t, 0:1], [F, 3], [0, H], [1, F]),
                                              bc(himask[:, h, 0:1], [0, 3], [F, H], [1, F]), ALU.mult)
                    sp_.then_inc(spreadd, 1)

                def split_group(n, u, p=p, F=F):
                    def part(i):
                        return parts[:, u, :, i * F:(i + 1) * F]

                    def left():
                        return rest[:, 0:TG * F].rearrange("p (t f) -> p t f", f=F)

                    value = dict(gru=rows_a[:, u, :, 0:F], conv0=msg[:, :, NV:NV + FA]).get(p, msg[:, :, 0:F])
                    b = base_split[p]
                    v.tensor_copy(part(0), value).then_inc(split, 1)
                    dve.wait_ge(split, n * 4 + (b + 1))
                    v.tensor_tensor(left(), value, part(0), ALU.subtract).then_inc(split, 1)
                    dve.wait_ge(split, n * 4 + (b + 2))
                    v.tensor_copy(part(1), left()).then_inc(split, 1)
                    dve.wait_ge(split, n * 4 + (b + 3))
                    v.tensor_tensor(part(2), left(), part(1), ALU.subtract).then_inc(split, 1)
                    dve.wait_ge(split, n * 4 + (b + 4))

                def body(n, u, m, new=True, p=p, form=form, multiply=multiply, reduce=reduce, spread_pair=spread_pair,
                         split_group=split_group):
                    old = not (isinstance(n, int) and n == 0)
                    if new:
                        form(n, u, m)
                    for j in range(NPAIR):
                        if new and p in CONVS:
                            multiply(n, u, j)
                        if old:
                            spread_pair(n - 1, 1 - u, j)
                        if new and p in CONVS:
                            reduce(n, u, j)
                    if not new:
                        return
                    if p in CONVS:
                        dve.wait_ge(reduced, n * NPAIR + (base_conv[p] + NPAIR))
                    if p == "conv0":
                        v.tensor_tensor(msg[:, :, NV + NS:NV + NS + 12].rearrange("p t (j c) -> p t j c", c=3),
                                        bc(msg[:, 0, 0:NV], [NV + FA, TG], [1, NV], [0, 3]),
                                        bc(scal[:, u], [3, TG], [0, NV], [1, 3]), ALU.mult).then_inc(formed, 1)
                        dve.wait_ge(formed, n * FORM[p] + (base_form[p] + 1))
                    split_group(n, u)

                group_loop(dve, body)
                body(NG, 0, 0, new=False)

                turned = wide[0:NP, 0].rearrange("p (n f) -> p n f", f=D)
                T0, T1 = t0[:, :, 0:D], t1[:, :, 0:D]
                nodes = lambda ap: bc(ap, [1, NC * 8], [0, D])
                feats = lambda ap, w=NS: bc(ap, [0, NC * 8], [1, w])
                if p == "net":
                    at(p, "add")
                    v.tensor_tensor(xs[:], xs[:], turned, ALU.add).then_inc(step, 1)
                    norm(p)
                if p == "gru":
                    at(p, "rz")
                    v.tensor_tensor(t0[:], gi[:, :, 0:32], gh[:, :, 0:32], ALU.add).then_inc(step, 1)
                    at(p, "reset")
                    v.tensor_tensor(T1, T0, gh[:, :, 32:48], ALU.mult).then_inc(step, 1)
                    at(p, "new in")
                    v.tensor_tensor(T1, T1, gi[:, :, 32:48], ALU.add).then_inc(step, 1)
                    at(p, "diff")
                    v.tensor_tensor(gi[:, :, 0:16], hs[:], T1, ALU.subtract).then_inc(step, 1)
                    at(p, "update")
                    v.tensor_tensor(gi[:, :, 0:16], gi[:, :, 0:16], t0[:, :, 16:32], ALU.mult).then_inc(step, 1)
                    at(p, "blend")
                    v.tensor_tensor(T1, T1, gi[:, :, 0:16], ALU.add).then_inc(step, 1)
                    at(p, "add")
                    v.tensor_tensor(xs[:], xs[:], T1, ALU.add).then_inc(step, 1)
                    norm(p)
                if p == "react":
                    at(p, "f1")
                    v.tensor_scalar(T0, hs[:], -1.0 / KK, 1.0, ALU.mult, ALU.add).then_inc(step, 1)
                    at(p, "f2")
                    v.tensor_scalar(T1, hs[:], 1.0 / KC, -1.0, ALU.mult, ALU.add).then_inc(step, 1)
                    at(p, "f3")
                    v.tensor_tensor(T0, T0, hs[:], ALU.mult).then_inc(step, 1)
                    at(p, "f4")
                    v.tensor_tensor(T0, T0, T1, ALU.mult).then_inc(step, 1)
                    at(p, "f5")
                    v.tensor_tensor(xs[:], xs[:], T0, ALU.add).then_inc(step, 1)
                    at(p, "add")
                    v.tensor_tensor(xs[:], xs[:], turned, ALU.add).then_inc(step, 1)
                    at(p, "const")
                    v.tensor_scalar(xs[:], xs[:], KB, None, ALU.add).then_inc(step, 1)
                    norm(p)
                if p == "conv0":
                    S, V = oa[:, :, 0:NS], oa[:, :, NS:NS + 12]
                    at(p, "node major")
                    v.tensor_copy(oa[:].rearrange("p (b n) f -> p b (n f)", b=2),
                                  wide[0:NP, 0:2, 0:16 * FA]).then_inc(step, 1)
                    at(p, "count")
                    v.tensor_scalar(st[:, 0], oa[:, :, FA - 1], 1.0, None, ALU.max).then_inc(step, 1)
                    at(p, "inv count")
                    v.reciprocal(st[:, 5], st[:, 0]).then_inc(step, 1)
                    at(p, "quarter")
                    v.tensor_scalar(st[:, 1], st[:, 5], NS ** -0.5, None, ALU.mult).then_inc(step, 1)
                    at(p, "average")
                    v.tensor_tensor(oa[:, :, 0:28], oa[:, :, 0:28], bc(st[:, 1], [1, NC * 8], [0, 28]),
                                    ALU.mult).then_inc(step, 1)
                    at(p, "average v")
                    v.tensor_scalar(V, V, 3.0 ** 0.5, None, ALU.mult).then_inc(step, 1)
                    at(p, "sum s")
                    v.tensor_reduce(bn[:, 0, 0:NS], bc(oa[:, 0, 0:1], [1, NS], [FA, NC * 8]), AX.X,
                                    ALU.add).then_inc(step, 1)
                if p == "conv1":
                    at(p, "average")
                    v.tensor_tensor(T0, turned, nodes(st[:, 5]), ALU.mult).then_inc(step, 1)
                    at(p, "norm 20")
                    v.tensor_scalar(T0, T0, (NS + NV) ** -0.5, None, ALU.mult).then_inc(step, 1)
                    at(p, "sum s")
                    v.tensor_reduce(bn[:, 0, 0:NS], bc(t0[:, 0, 0:1], [1, NS], [32, NC * 8]), AX.X,
                                    ALU.add).then_inc(step, 1)
                    S = T0
                if p in ("conv0", "conv1"):
                    at(p, "mean s")
                    v.tensor_scalar(bn[:, 1, 0:NS], hidden[0:NP, 0, 0:NS], 1.0 / N, None, ALU.mult).then_inc(step, 1)
                    at(p, "centered")
                    v.tensor_tensor(T0, S, feats(bn[:, 1, 0:NS]), ALU.subtract).then_inc(step, 1)
                    at(p, "masked")
                    v.tensor_tensor(T0, T0, nodes(mask[:]), ALU.mult).then_inc(step, 1)
                    at(p, "squares")
                    v.tensor_tensor(T1, T0, T0, ALU.mult).then_inc(step, 1)
                    if p == "conv0":
                        at(p, "squares v")
                        v.tensor_tensor(t1[:, :, NS:NS + 12], V, V, ALU.mult).then_inc(step, 1)
                    at(p, "sum sq s")
                    v.tensor_reduce(bn[:, 2, 0:NS], bc(t1[:, 0, 0:1], [1, NS], [32, NC * 8]), AX.X,
                                    ALU.add).then_inc(step, 1)
                    if p == "conv0":
                        at(p, "sum sq v")
                        v.tensor_reduce(bn[:, 2, NS:NS + NV], bc(t1[:, 0, NS:NS + 1], [3, NV], [32, NC * 8], [1, 3]),
                                        AX.XY, ALU.add).then_inc(step, 1)
                    at(p, "var s")
                    v.tensor_scalar(bn[:, 4, 0:NS], hidden[0:NP, 1, 0:NS], 1.0 / N, None, ALU.mult).then_inc(step, 1)
                    if p == "conv0":
                        at(p, "var v")
                        v.tensor_scalar(bn[:, 4, NS:], hidden[0:NP, 1, NS:NS + NV], 1.0 / (3 * N), None,
                                        ALU.mult).then_inc(step, 1)
                    w = NS + NV if p == "conv0" else NS
                    g0 = 0 if p == "conv0" else 2 * NS + NV
                    b0 = g0 + w
                    at(p, "rstd")
                    v.reciprocal(bn[:, 6, 0:w], bn[:, 5, 0:w]).then_inc(step, 1)
                    at(p, "gain")
                    v.tensor_tensor(bn[:, 7, 0:w], bn[:, 6, 0:w], norms[:, g0:g0 + w], ALU.mult).then_inc(step, 1)
                    at(p, "scaled")
                    v.tensor_tensor(T0, T0, feats(bn[:, 7, 0:NS]), ALU.mult).then_inc(step, 1)
                    at(p, "shift")
                    to = t1[:, :, 12:28] if p == "conv0" else T1
                    v.tensor_tensor(to, T0, feats(norms[:, b0:b0 + NS]), ALU.add).then_inc(step, 1)
                    if p == "conv0":
                        at(p, "scaled v")
                        v.tensor_tensor(t1[:, :, 0:12].rearrange("p n (j c) -> p n j c", c=3),
                                        V.rearrange("p n (j c) -> p n j c", c=3),
                                        bc(bn[:, 7, NS:NS + NV], [0, NC * 8], [1, NV], [0, 3]), ALU.mult).then_inc(step, 1)
                    else:
                        at(p, "add")
                        v.tensor_tensor(xs[:], xs[:], T1, ALU.add).then_inc(step, 1)


def kernel(**inputs):
    import numpy as np
    import concourse.bacc as bacc
    from concourse.bass_utils import run_bass_kernel_spmd

    a = {k: np.asarray(v) for k, v in inputs.items()}

    def edges(v, fill):
        full = np.full((128 * T,) + v.shape[1:], fill, v.dtype)
        full[:E] = v
        return full.reshape((128, T) + v.shape[1:])

    def columns(v):
        return np.ascontiguousarray(edges(v, 0).transpose(2, 1, 0)).reshape(v.shape[1], T * 128)

    def diagonal(w):
        r, c = w.shape
        full = np.zeros((8, r, 8, c), w.dtype)
        for h in range(8):
            full[h, :, h, :] = w
        return full.reshape(8 * r, 8 * c)

    def with_bias(w, b):
        full = np.zeros((128, w.shape[1]), w.dtype)
        full[:len(w)] = w
        full[len(w)] = b
        return full

    def hidden_weights(w, b):
        full = np.zeros((128, 128), w.dtype)
        full[:, :DA] = with_bias(w, b)
        full[DA, DA] = 1
        return full

    def out_major(w, i, o):
        return w.reshape(w.shape[0], i, o).transpose(0, 2, 1).reshape(w.shape[0], i * o)

    x = np.zeros((NPAD, D), a["x"].dtype)
    x[:N] = a["x"]
    f0 = with_bias(a["L3_gnn_fc0_w2"], a["L3_gnn_fc0_b2"])
    f1 = with_bias(a["L3_gnn_fc1_w2"], a["L3_gnn_fc1_b2"])
    emb = a["L1_gnn_edge_emb"].reshape(NTYPE, D, D).transpose(2, 0, 1).reshape(D, NTYPE * D)
    arrays = {
        "x": x,
        "src": edges(a["src"], PADNODE),
        "dst": edges(a["dst"], PADNODE),
        "etype": edges(a["edge_type_8"], 0),
        "weight": edges(a["edge_weight"], 0),
        "vec": edges(a["edge_attr_3"], 0).reshape(128, T * 3),
        "ea16": columns(a["edge_attr_16"]),
        "ea48": columns(a["edge_attr_48"]),
        "net_w": with_bias(a["L0_gnn_kernel"], a["L0_gnn_bias"]),
        "types_w": diagonal(emb),
        "ih_w": diagonal(a["L1_gnn_w_ih"].T),
        "hh_w": diagonal(a["L1_gnn_w_hh"].T),
        "ih_b": np.tile(a["L1_gnn_b_ih"], 8)[None, :],
        "hh_b": np.tile(a["L1_gnn_b_hh"], 8)[None, :],
        "w1": np.stack([hidden_weights(a[f"L3_gnn_fc{k}_w1"], a[f"L3_gnn_fc{k}_b1"]) for k in range(2)]),
        "w2": np.stack([np.concatenate([out_major(f0[:, NS * NS:], NS, NV), out_major(f0[:, :NS * NS], NS, NS)], 1),
                        out_major(f1, NS + NV, NS)]),
        "gs0": a["L3_gnn_bn0_gs"], "bs0": a["L3_gnn_bn0_bs"], "gv0": a["L3_gnn_bn0_gv"],
        "gs1": a["L3_gnn_bn1_gs"], "bs1": a["L3_gnn_bn1_bs"],
    }
    nc = bacc.Bacc("TRN2", target_bir_lowering=False, num_devices=1)
    feed, args = {}, []
    for name, v in arrays.items():
        v = np.ascontiguousarray(v)
        feed[f"in_{name}"] = v
        args.append(nc.dram_tensor(f"in_{name}", v.shape, mybir.dt.from_np(v.dtype), kind="ExternalInput").ap())
    args.append(nc.dram_tensor("out_x", (NPAD, D), F32, kind="ExternalOutput").ap())
    gnn_kernel(nc, *args)
    r = run_bass_kernel_spmd(nc, [feed], core_ids=[0])
    return r.results[0]["out_x"][:N]
```

```python
from contextlib import ExitStack

import concourse.bass as bass
from concourse import mybir

F32 = mybir.dt.float32
F16 = mybir.dt.float16
BF16 = mybir.dt.bfloat16
I32 = mybir.dt.int32
ALU = mybir.AluOpType
ACT = mybir.ActivationFunctionType
AX = mybir.AxisListType

N = 3125
E = 103125
D = 16
TG = 14
NG = 58
T = TG * NG
NPAIR = TG // 2
NP = 98
NC = 4
NPAD = NC * NP * 8
LO = 391
NTYPE = 8
DA = 48
NS, NV = 16, 4
FA = NS + 3 * NV + 1
WN = (NS + NV) * NS
EPS = 1e-5
KB, KK, KC, KD, KE, KH = 0.1, 5.0, 1.0, 5.0, 0.9, 0.1
PADNODE = NPAD - 1
HC = 448
NH = TG * 128 // HC

PHASES = ("net", "gru", "react", "conv0", "conv1")
CONVS = ("net", "conv0", "conv1")
ACT_LO = ("net", "react", "conv1")
LOOK = (0, 4, 8, 12, TG)
NL = len(LOOK) - 1
SUMF = dict(net=D, gru=D, react=D, conv0=FA, conv1=D)
HI = dict(net=8, gru=8, react=8, conv0=4, conv1=8)
IN = dict(net=D, conv0=NS, conv1=NS + NV)
OUTF = dict(net=D, conv0=NS + NV, conv1=NS)
GCOLS = dict(net=D, gru=D, react=D, conv0=D, conv1=32)

NORM = ["mean", "scale", "center", "square", "var", "std", "rstd", "norm", "relu"]
STEPS = {
    "start": NORM,
    "net": ["sums", "turned", "add"] + NORM + ["h turned", "h cols", "types 0", "types 0 out", "types 1",
                                               "types 1 out"],
    "gru": ["sums"] + [f"{s} {k}" for k in range(2) for s in ("gates", "gates in", "gates hid")]
    + ["rz", "sigmoid", "reset", "new in", "tanh", "diff", "update", "blend", "add"] + NORM
    + ["part 0", "left 0", "part 1", "part 2"],
    "react": ["sums", "turned", "f1", "f2", "f3", "f4", "f5", "add", "const", "row of ones"] + NORM,
    "conv0": ["sums", "turned", "node major", "count", "inv count", "quarter", "average", "average v", "sum s",
              "all s", "mean s", "centered", "masked", "squares", "squares v", "sum sq s", "sum sq v", "all sq",
              "var s", "var v", "std", "rstd", "gain", "scaled", "shift", "scaled v"],
    "conv1": ["sums", "turned", "average", "norm 20", "sum s", "all s", "mean s", "centered", "masked", "squares",
              "sum sq s", "all sq", "var s", "std", "rstd", "gain", "scaled", "shift", "add"],
}
STAGES = ["start", *PHASES]
FIRST_STEP = {s: sum(len(STEPS[x]) for x in STAGES[:k]) for k, s in enumerate(STAGES)}


def before(stage, name):
    return FIRST_STEP[stage] + STEPS[stage].index(name)


def ended(stage):
    return FIRST_STEP[stage] + len(STEPS[stage])


def gnn_kernel(nc, x, src, dst, etype, weight, vec, ea16, ea48, net_w, types_w, ih_w, hh_w, ih_b, hh_b,
               w1, w2, src_rows, gs0, bs0, gv0, gs1, bs1, out):
    with ExitStack() as ctx:
        def sb(name, shape, dt):
            return ctx.enter_context(nc.sbuf_tensor(name, shape, dt))

        def sem(name):
            return ctx.enter_context(nc.semaphore(name))

        def bc(ap, *dims):
            return bass.AP(ap.tensor, ap.offset, [ap.ap[0], *[list(d) for d in dims]])

        table = {p: nc.dram_tensor(f"table_{p}", [NPAD * (NTYPE if p == "gru" else 1), GCOLS[p]], F32).ap()
                 for p in PHASES}

        lo_rows = nc.dram_tensor("lo_rows", [128, T], F16).ap()
        hi_rows = nc.dram_tensor("hi_rows", [128, T], F16).ap()

        acc = ctx.enter_context(nc.psum_tensor("acc", [128, 2, 512], F32))
        hidden = ctx.enter_context(nc.psum_tensor("hidden", [128, 2, 512], F32))
        wide = ctx.enter_context(nc.psum_tensor("wide", [128, 4, 512], F32))

        src_i = sb("src_i", [128, T], I32)
        dst_i = sb("dst_i", [128, T], I32)
        typ_i = sb("typ_i", [128, T], I32)
        bits = sb("bits", [128, T], I32)
        key_src8 = sb("key_src8", [128, T, 2], F32)
        key_src4 = sb("key_src4", [128, T, 2], F32)
        key_dst8 = sb("key_dst8", [128, T, 2], F32)
        wgt = sb("wgt", [128, T], F32)
        unit = sb("unit", [128, T, 3], F32)
        len_a = sb("len_a", [128, T], F32)
        len_b = sb("len_b", [128, T], F32)

        lo_vals = sb("lo_vals", [128, 2 * LO], F16)
        hi_vals8 = sb("hi_vals8", [128, 8, D], F16)
        hi_vals4 = sb("hi_vals4", [128, 4, FA], F16)
        zeros = sb("zeros", [128, LO + 1], BF16)
        ident = sb("ident", [128, 128], F32)
        ones = sb("ones", [128, 128], F32)
        mask = sb("mask", [NP, NC * 8], F32)
        eps = sb("eps", [128, 2], F32)
        part_i = sb("part_i", [128, 2], I32)
        part_hi = sb("part_hi", [128, 1], F32)
        part_lo = sb("part_lo", [NP, NC], F32)
        choose = sb("choose", [128, D], F32)
        net_sb = sb("net_sb", [128, D * D], F32)
        types_sb = sb("types_sb", [128, 8 * NTYPE * D], F32)
        ih_sb = sb("ih_sb", [128, 8 * 48], F32)
        hh_sb = sb("hh_sb", [128, 8 * 48], F32)
        gate_b = sb("gate_b", [1, 2, 8 * 48], F32)
        w1_sb = sb("w1_sb", [128, 2, 128], F32)
        w2_sb = sb("w2_sb", [128, 2, WN], F32)
        norms = sb("norms", [NP, 4 * NS + NV], F32)

        idx_a = sb("idx_a", [128, 2, TG], I32)
        key = sb("key", [128, 2, TG, 2], F32)
        rows_a = sb("rows_a", [128, 2, TG, 32], F32)
        scal = sb("scal", [128, 2, TG * 3], F32)
        ea = sb("ea", [128, 2, TG * 128], F32)
        hid = sb("hid", [128, 2, TG * 128], F32)
        prod = sb("prod", [128, 2, 2, WN], F32)
        msg = sb("msg", [128, TG, NV + FA], F32)
        vsh = sb("vsh", [128, TG * 12], F32)
        rest = sb("rest", [128, TG * FA], F32)
        away = sb("away", [128, 4, LO + 1], BF16)
        parts = sb("parts", [128, 2, TG, 3 * 32], BF16)
        onehot = sb("onehot", [128, TG, 2 * LO], BF16)
        himask = sb("himask", [128, 4, 128], BF16)
        spread = sb("spread", [128, TG, 3 * 128], BF16)
        lo_t = sb("lo_t", [NP, 2, TG * 128], F16)
        hi_t = sb("hi_t", [128, 2, TG * 128], F16)
        h_parts = sb("h_parts", [NP, 3, NC * 128], BF16)
        ra = sb("ra", [128, TG * D], F32)
        rb = sb("rb", [128, TG * D], F32)

        onehot_t = [b[:].rearrange("p u f -> p (u f)").bitcast(BF16)[0:NP, :].rearrange("p (c e) -> p c e", c=NC)
                    for b in (hid, ea)]
        picked_rows = prod[:].rearrange("p a b f -> p (a b f)")[:, 0:1024].rearrange("p (b e) -> p b e", b=2)
        scratch = onehot[:].rearrange("p t f -> p (t f)")
        rows_i = scratch[:, 0:2 * T].bitcast(I32)
        rows_bits = scratch[:, 2 * T:4 * T].bitcast(I32)
        rows_lo = scratch[:, 4 * T:5 * T].bitcast(F16)
        rows_hi = scratch[:, 5 * T:6 * T].bitcast(F16)

        xs = sb("xs", [NP, NC * 8, D], F32)
        hs = sb("hs", [NP, NC * 8, D], F32)
        t0 = sb("t0", [NP, NC * 8, 32], F32)
        t1 = sb("t1", [NP, NC * 8, 32], F32)
        st = sb("st", [NP, 6, NC * 8], F32)
        hcols = sb("hcols", [128, NC * NP], F32)
        sums = sb("sums", [128, 2 * NC * NP], F32)
        gates = sb("gates", [NP, 2, NC * 8 * 48], F32)
        gi = gates[:, 0].rearrange("p (n f) -> p n f", f=48)
        gh = gates[:, 1].rearrange("p (n f) -> p n f", f=48)
        typed = gates[:].rearrange("p a b -> p (a b)")[:, 0:4 * 512].rearrange("p (q f) -> p q f", q=4)
        oa = sb("oa", [NP, NC * 8, FA], F32)
        bn = sb("bn", [NP, 12, NS + NV], F32)

        x_loaded = sem("x_loaded")
        consts_loaded = sem("consts_loaded")
        edges_loaded = sem("edges_loaded")
        pool_consts = sem("pool_consts")
        setup = sem("setup")
        lens = sem("lens")
        step = sem("step")
        tabled = {p: sem(f"tabled_{p}") for p in PHASES}
        idx_in = [sem(f"idx_in{u}") for u in range(2)]
        key_in = [sem(f"key_in{u}") for u in range(2)]
        scal_in = [sem(f"scal_in{u}") for u in range(2)]
        rows_keys = sem("rows_keys")
        look_in = [sem(f"look_in{u}") for u in range(2)]
        ea_in = [sem(f"ea_in{u}") for u in range(2)]
        gathered = {p: [sem(f"gathered_{p}{u}") for u in range(2)] for p in PHASES}
        hid_mm = sem("hid_mm")
        hid_relu = sem("hid_relu")
        weights = sem("weights")
        mult = sem("mult")
        reduced = sem("reduced")
        spreadd = sem("spreadd")
        masked = sem("masked")
        summed = sem("summed")
        split = sem("split")
        formed = sem("formed")
        acc_open = sem("acc_open")
        acc_done = sem("acc_done")
        stored = sem("stored")
        apart = sem("apart")
        lo_ready = sem("lo_ready")
        turned_lo = sem("turned_lo")
        looked = sem("looked")
        picked = sem("picked")
        chosen = sem("chosen")
        slot_free = sem("slot_free")
        rows_free = sem("rows_free")

        def earlier(phase, per_group, phases=PHASES):
            k = PHASES.index(phase)
            return sum((per_group[q] if isinstance(per_group, dict) else per_group) * NG
                       for q in phases if PHASES.index(q) < k)

        FORM = dict(react=6, conv0=1, conv1=2)
        scal_count = dict(react=16, conv0=16, conv1=16)
        base_scal = {p: earlier(p, 16, tuple(scal_count)) // 2 for p in PHASES}
        base_lo = {p: earlier(p, NPAIR, ACT_LO) for p in PHASES}
        base_pair = {p: earlier(p, NPAIR) for p in PHASES}
        base_conv = {p: earlier(p, NPAIR, CONVS) for p in PHASES}
        base_split = {p: earlier(p, 4) for p in PHASES}
        base_key = {p: earlier(p, 16) // 2 for p in PHASES}
        base_idx = {p: earlier(p, 16) // 2 for p in PHASES}
        base_ea = {p: earlier(p, 16, CONVS) // 2 for p in PHASES}
        base_hid = {p: earlier(p, NH, CONVS[1:]) for p in PHASES}
        base_form = {p: earlier(p, FORM, tuple(FORM)) for p in PHASES}
        gather_count = 16 * TG
        key_of = dict(net=key_src8, gru=key_dst8, react=key_src8, conv0=key_src4, conv1=key_src8)

        def group_loop(eng, body, last=NG, first=2):
            for n in range(first):
                body(n, n % 2, n // 2)
            with eng.Fori(0, (last - first) // 2) as i:
                body(i * 2 + first, 0, i + first // 2)
                body(i * 2 + (first + 1), 1, i + first // 2)

        N_CONST = 15
        N_ROWS = 7
        N_SQUARED = N_ROWS + 19
        N_SETUP = N_SQUARED + 3

        block = ctx.enter_context(nc.Block())

        @block.sync
        def _(sp):
            xv = x.rearrange("(c p h) f -> p c (h f)", c=NC, p=NP)
            sp.dma_start(xs[:].rearrange("p (c h) f -> p c (h f)", c=NC), xv).then_inc(x_loaded, 16)
            sp.dma_start(rows_i, src_rows).then_inc(edges_loaded, 16)
            for to, frm in ((src_i, src), (dst_i, dst), (typ_i, etype), (wgt, weight)):
                sp.dma_start(to[:], frm).then_inc(edges_loaded, 16)
            sp.dma_start(unit[:].rearrange("p t c -> p (t c)"), vec).then_inc(edges_loaded, 16)
            for to, frm in ((net_sb[:], net_w), (types_sb[:], types_w), (ih_sb[:], ih_w), (hh_sb[:], hh_w),
                            (gate_b[:, 0], ih_b), (gate_b[:, 1], hh_b),
                            (w1_sb[:, 0], w1[0]), (w1_sb[:, 1], w1[1]), (w2_sb[:, 0], w2[0]), (w2_sb[:, 1], w2[1])):
                sp.dma_start(to, frm).then_inc(consts_loaded, 16)
            at = 0
            for v, n in ((gs0, NS), (gv0, NV), (bs0, NS), (gs1, NS), (bs1, NS)):
                sp.dma_start(norms[:, at:at + n], v.partition_broadcast(NP)).then_inc(consts_loaded, 16)
                at += n

            sp.wait_ge(setup, N_ROWS)
            sp.dma_start(lo_rows, rows_lo).then_inc(rows_keys, 16)
            sp.dma_start(hi_rows, rows_hi).then_inc(rows_keys, 16)

            def table_out(p):
                if p == "gru":
                    rows = table[p].rearrange("(c p r) m -> c p (r m)", c=NC, p=NP)
                    for k in range(2):
                        sp.wait_ge(step, before("net", f"types {k} out") + 1)
                        sp.dma_start(rows[2 * k].rearrange("p (a f) -> p a f", a=2), typed[:, 0:2]).then_inc(tabled[p], 16)
                        sp.dma_start(rows[2 * k + 1].rearrange("p (a f) -> p a f", a=2), typed[:, 2:4]).then_inc(tabled[p], 16)
                else:
                    prev = STAGES[STAGES.index(p) - 1]
                    sp.wait_ge(step, ended(prev))
                    rows = table[p].rearrange("(c p h) f -> p c (h f)", c=NC, p=NP)
                    frm = t1 if p == "conv1" else hs
                    sp.dma_start(rows, frm[:].rearrange("p (c h) f -> p c (h f)", c=NC)).then_inc(tabled[p], 16)

            sp.wait_ge(setup, N_SETUP)
            sp.wait_ge(rows_keys, 32)
            for p in PHASES:
                table_out(p)

                def load(n, u, m, look=True, p=p):
                    cols = bass.ds(n * TG, TG)
                    first = isinstance(n, int) and n < 2
                    ecols = bass.ds(n * (TG * 128), TG * 128)
                    if p == "net":
                        if not first:
                            sp.wait_ge(weights, n * NPAIR + (base_conv[p] - NPAIR))
                            sp.sem_inc(slot_free, 1)
                        sp.dma_start(ea[0:D, u], ea16[:, ecols]).then_inc(ea_in[u], 16)
                    if p in ("conv0", "conv1"):
                        if not first:
                            sp.wait_ge(hid_mm, n * NH + (base_hid[p] - NH))
                            sp.sem_inc(slot_free, 1)
                        sp.dma_start(ea[0:DA, u], ea48[:, ecols]).then_inc(ea_in[u], 16)
                    if not first:
                        sp.wait_ge(gathered[p][u], m * gather_count)
                        sp.sem_inc(slot_free, 1)
                    which = typ_i if p == "gru" else dst_i
                    sp.dma_start(idx_a[:, u], which[:, cols]).then_inc(idx_in[u], 16)
                    if p in scal_count:
                        if not first:
                            sp.wait_ge(split, n * 4 + (base_split[p] - 4))
                            sp.sem_inc(slot_free, 1)
                        if p == "react":
                            sp.dma_start(scal[:, u, 0:TG], wgt[:, cols]).then_inc(scal_in[u], 16)
                        else:
                            sp.dma_start(scal[:, u].rearrange("p (t c) -> p t c", c=3),
                                         unit[:, cols, :]).then_inc(scal_in[u], 16)
                    if not (isinstance(n, int) and n == 0):
                        load_key(n - 1, 1 - u)
                    if p == "react" and look:
                        sp.wait_ge(picked, n * NL + NL)
                        sp.sem_inc(slot_free, 1)
                        look_load(n + 2, u)

                def load_key(n, u, p=p):
                    if not (isinstance(n, int) and n < 2):
                        sp.wait_ge(summed, n * NPAIR + (base_pair[p] - NPAIR))
                        sp.sem_inc(slot_free, 1)
                    sp.dma_start(key[:, u], key_of[p][:, bass.ds(n * TG, TG), :]).then_inc(key_in[u], 16)

                def look_load(n, u):
                    ecols = bass.ds(n * (TG * 128), TG * 128)
                    sp.dma_start(lo_t[:, u], lo_rows.rearrange("q t -> (q t)")[ecols].partition_broadcast(NP)
                                 ).then_inc(look_in[u], 16)
                    sp.dma_start(hi_t[:, u], hi_rows.rearrange("q t -> (q t)")[ecols].partition_broadcast(128)
                                 ).then_inc(look_in[u], 16)

                if p == "react":
                    look_load(0, 0)
                    look_load(1, 1)
                group_loop(sp, load, NG - 2, first=4)
                load(NG - 2, 0, NG // 2 - 1, look=False)
                load(NG - 1, 1, NG // 2 - 1, look=False)
                load_key(NG - 1, 1)
            sp.wait_ge(step, ended("conv1"))
            sp.dma_start(out.rearrange("(c p h) f -> p c (h f)", c=NC, p=NP),
                         xs[:].rearrange("p (c h) f -> p c (h f)", c=NC)).then_inc(stored, 16)
            sp.wait_ge(stored, 16)

        @block.gpsimd
        def _(pool):
            g = nc.gpsimd
            g.iota(lo_vals[:], [[1, 2 * LO]], base=0, channel_multiplier=0,
                   allow_small_or_imprecise_dtypes=True).then_inc(pool_consts, 1)
            g.iota(hi_vals8[:], [[1, 8], [0, D]], base=0, channel_multiplier=0,
                   allow_small_or_imprecise_dtypes=True).then_inc(pool_consts, 1)
            g.iota(hi_vals4[:], [[1, 4], [0, FA]], base=0, channel_multiplier=0,
                   allow_small_or_imprecise_dtypes=True).then_inc(pool_consts, 1)
            g.iota(part_i[:, 0:1], [[0, 1]], base=0, channel_multiplier=1).then_inc(pool_consts, 1)
            g.iota(part_lo[:], [[NP, NC]], base=0, channel_multiplier=1,
                   allow_small_or_imprecise_dtypes=True).then_inc(pool_consts, 1)
            g.memset(ones[:], 1.0).then_inc(pool_consts, 1)
            pool.wait_ge(pool_consts, 6)
            g.affine_select(out=ident[:], in_=ones[:], compare_op=ALU.is_equal, fill=0.0, base=0,
                            pattern=[[-1, 128]], channel_multiplier=1).then_inc(pool_consts, 1)
            g.affine_select(out=mask[:].rearrange("p (c h) -> p c h", c=NC),
                            in_=ones[0:NP, 0:NC * 8].rearrange("p (c h) -> p c h", c=NC),
                            compare_op=ALU.is_ge, fill=0.0, base=N - 1,
                            pattern=[[-8 * NP, NC], [-1, 8]], channel_multiplier=-8).then_inc(pool_consts, 1)

            for p in PHASES:
                pool.wait_ge(tabled[p], 64 if p == "gru" else 16)

                def gather(n, u, m, p=p):
                    pool.wait_ge(idx_in[u], m * 16 + (base_idx[p] + 16))
                    if not (isinstance(n, int) and n < 2):
                        if p in CONVS:
                            pool.wait_ge(mult, n * NPAIR + (base_conv[p] - NPAIR))
                        elif p == "react":
                            pool.wait_ge(formed, n * FORM[p] + (base_form[p] - FORM[p]))
                        else:
                            pool.wait_ge(split, n * 4 + (base_split[p] - 4))
                    pool.sem_inc(rows_free, 1)
                    for t in range(TG):
                        g.indirect_dma_start(out=rows_a[:, u, t, 0:GCOLS[p]], out_offset=None, in_=table[p],
                                             in_offset=bass.IndirectOffsetOnAxis(ap=idx_a[:, u, t:t + 1], axis=0)
                                             ).then_inc(gathered[p][u], 16)

                group_loop(pool, gather)

        @block.scalar
        def _(act):
            a = nc.scalar

            def at(stage, name):
                act.wait_ge(step, before(stage, name))

            def std(stage):
                at(stage, "std")
                a.activation(st[:, 2], st[:, 1], ACT.Sqrt, bias=eps[0:NP, 0:1], scale=1.0 / D).then_inc(step, 1)

            act.wait_ge(setup, N_SQUARED)
            a.activation(len_b[:], len_a[:], ACT.Sqrt, bias=eps[:, 1:2]).then_inc(lens, 1)
            std("start")

            act.wait_ge(pool_consts, 8)
            for p in PHASES:
                def relu(n, u, c, p=p):
                    if c == 0 and not (isinstance(n, int) and n < 2):
                        act.wait_ge(weights, n * NPAIR + (base_conv[p] - NPAIR))
                    act.wait_ge(hid_mm, n * NH + (base_hid[p] + c + 1))
                    a.activation(hid[:, u, c * HC:(c + 1) * HC], hidden[:, c % 2, 0:HC],
                                 ACT.Relu).then_inc(hid_relu, 1)

                def distance(n, u, j, p=p):
                    if not (isinstance(n, int) and n == 0 and j < 2):
                        act.wait_ge(lo_ready, n * NPAIR + (base_lo[p] + j - 1))
                    for t in (2 * j, 2 * j + 1):
                        i = a.activation(away[:, (2 * u + t) % 4, 0:LO], lo_vals[:, 0:LO], ACT.Abs, bias=key[:, u, t, 0:1],
                                         scale=-1.0)
                    i.then_inc(apart, 1)

                def nearest(n, u, j, p=p):
                    act.wait_ge(apart, n * NPAIR + (base_lo[p] + j + 1))
                    if not (isinstance(n, int) and n == 0):
                        act.wait_ge(summed, n * NPAIR + (base_pair[p] + j + 1 - NPAIR))
                    for t in (2 * j, 2 * j + 1):
                        i = a.activation(onehot[:, t, 0:LO], away[:, (2 * u + t) % 4, 0:LO], ACT.Relu, bias=ones[:, 0:1],
                                         scale=-1.0)
                    i.then_inc(lo_ready, 1)

                def body(n, u, m, ahead=True, p=p):
                    old = p in ACT_LO and not (isinstance(n, int) and n == 0)
                    if old:
                        act.wait_ge(key_in[1 - u], (m - 1 + u) * 16 + (base_key[p] + 16))
                        distance(n - 1, 1 - u, 0)
                    for j in range(NPAIR):
                        if old:
                            if j + 1 < NPAIR:
                                distance(n - 1, 1 - u, j + 1)
                            nearest(n - 1, 1 - u, j)
                        if p in CONVS[1:] and ahead and j < NH:
                            relu(n + 1, 1 - u, j)

                if p in CONVS[1:]:
                    for c in range(NH):
                        relu(0, 0, c)
                if p != "gru":
                    group_loop(act, body, NG - 2)
                    body(NG - 2, 0, NG // 2 - 1)
                    body(NG - 1, 1, NG // 2 - 1, ahead=False)
                    body(NG, 0, NG // 2, ahead=False)
                at(p, "sums")
                act.wait_ge(acc_done, PHASES.index(p) + 1)
                if p == "conv0":
                    a.activation(sums[0:4 * FA, 0:2 * LO].rearrange("p (a b) -> p a b", a=2), acc[0:4 * FA, :, 0:LO],
                                 ACT.Copy).then_inc(step, 1)
                    at(p, "std")
                    a.activation(bn[:, 5], bn[:, 4], ACT.Sqrt, bias=eps[0:NP, 0:1]).then_inc(step, 1)
                else:
                    a.activation(sums[:, 0:LO + 1], acc[:, 0, 0:LO + 1], ACT.Copy).then_inc(step, 1)
                if p == "net":
                    std(p)
                    at(p, "h cols")
                    a.activation(hcols[:], hidden[:, 0, 0:NC * NP], ACT.Copy).then_inc(step, 1)
                    at(p, "types 0 out")
                    a.activation(typed, wide[0:NP], ACT.Copy).then_inc(step, 1)
                    at(p, "types 1 out")
                    act.wait_ge(tabled["gru"], 32)
                    a.activation(typed, wide[0:NP], ACT.Copy).then_inc(step, 1)
                if p == "gru":
                    for k in range(2):
                        at(p, f"gates in {k}")
                        a.activation(gi[:, 16 * k:16 * k + 16].rearrange("p (a h) f -> p a (h f)", a=2),
                                     wide[0:NP, 0:4:2, 0:384], ACT.Copy).then_inc(step, 1)
                        at(p, f"gates hid {k}")
                        a.activation(gh[:, 16 * k:16 * k + 16].rearrange("p (a h) f -> p a (h f)", a=2),
                                     wide[0:NP, 1:4:2, 0:384], ACT.Copy).then_inc(step, 1)
                    at(p, "sigmoid")
                    a.activation(t0[:], t0[:], ACT.Sigmoid).then_inc(step, 1)
                    at(p, "tanh")
                    a.activation(t1[:, :, 0:D], t1[:, :, 0:D], ACT.Tanh).then_inc(step, 1)
                if p in ("gru", "react"):
                    std(p)
                if p == "conv1":
                    at(p, "std")
                    a.activation(bn[:, 5, 0:NS], bn[:, 4, 0:NS], ACT.Sqrt, bias=eps[0:NP, 0:1]).then_inc(step, 1)

        @block.tensor
        def _(pe):
            m = nc.tensor

            def at(stage, name):
                pe.wait_ge(step, before(stage, name))

            pe.wait_ge(pool_consts, 8)
            pe.wait_ge(setup, N_SETUP)
            pe.wait_ge(consts_loaded, 16 * N_CONST)
            for k, p in enumerate(PHASES):
                H, F = HI[p], SUMF[p]
                NB = 2 if p == "conv0" else 1
                W = dict(net=net_sb[:], conv0=w2_sb[:, 0], conv1=w2_sb[:, 1]).get(p)
                nw = IN[p] * OUTF[p] if p in CONVS else 0
                pe.wait_ge(step, ended(STAGES[k]))
                for b in range(NB):
                    mm = m.matmul(acc[0:H * F, b, 0:LO + 1], zeros[:, 0:H * F], zeros[:], start=True, stop=False)
                mm.then_inc(acc_open, 1)

                def hid_chunk(n, u, c, mth, p=p):
                    if c == 0:
                        pe.wait_ge(ea_in[u], mth * 16 + (base_ea[p] + 16))
                    if not (isinstance(n, int) and n == 0 and c < 2):
                        pe.wait_ge(hid_relu, n * NH + (base_hid[p] + c - 1))
                    m.matmul(hidden[:, c % 2, 0:HC], w1_sb[:, CONVS.index(p) - 1],
                             ea[:, u, c * HC:(c + 1) * HC], start=True, stop=True).then_inc(hid_mm, 1)

                def conv_pair(n, u, j, mth, p=p, W=W, nw=nw):
                    if p == "net":
                        if j == 0:
                            pe.wait_ge(ea_in[u], mth * 16 + (base_ea[p] + 16))
                        lhs = ea
                    else:
                        lhs = hid
                        c = ((2 * j + 2) * 128 - 1) // HC
                        pe.wait_ge(hid_relu, n * NH + (base_hid[p] + c + 1))
                    if not (isinstance(n, int) and n == 0 and j < 2):
                        pe.wait_ge(mult, n * NPAIR + (base_conv[p] + j - 1))
                    for s in range(2):
                        col = (2 * j + s) * 128
                        mm = m.matmul(wide[:, 2 * ((u + j) % 2) + s, 0:nw], lhs[:, u, col:col + 128], W,
                                      start=True, stop=True)
                    mm.then_inc(weights, 1)

                def sum_pair(n, j, p=p, H=H, F=F, NB=NB):
                    pe.wait_ge(spreadd, n * NPAIR + (base_pair[p] + j + 1))
                    if p in ACT_LO:
                        pe.wait_ge(lo_ready, n * NPAIR + (base_lo[p] + j + 1))
                    for t in (2 * j, 2 * j + 1):
                        for s in range(3):
                            for b in range(NB):
                                mm = m.matmul(acc[0:H * F, b, 0:LO], spread[:, t, s * H * F:(s + 1) * H * F],
                                              onehot[:, t, b * LO:(b + 1) * LO], start=False, stop=False)
                    mm.then_inc(summed, 1)

                def look_up(n, u, b):
                    if b == 0:
                        pe.wait_ge(turned_lo, n + 1)
                    if not (isinstance(n, int) and n == 0 and b < 2):
                        pe.wait_ge(picked, n * NL + (b - 1))
                    c0, c1 = LOOK[b] * 128, LOOK[b + 1] * 128
                    for s in range(3):
                        for c in range(NC):
                            mm = m.matmul(hidden[:, b % 2, 0:c1 - c0], h_parts[:, s, c * 128:(c + 1) * 128],
                                          onehot_t[u][:, c, c0:c1], start=(s == 0 and c == 0),
                                          stop=(s == 2 and c == NC - 1))
                    mm.then_inc(looked, 1)

                def choose_rows(n, u, b):
                    pe.wait_ge(picked, n * NL + (b + 1))
                    if b == 0 and not (isinstance(n, int) and n < 2):
                        pe.wait_ge(formed, n * FORM["react"] + (base_form["react"] - FORM["react"]))
                    for t in range(LOOK[b], LOOK[b + 1]):
                        c = (t - LOOK[b]) * 128
                        mm = m.matmul(wide[:, u, t * D:(t + 1) * D], picked_rows[:, b % 2, c:c + 128], choose[:],
                                      start=True, stop=True)
                    mm.then_inc(chosen, 1)

                def body(n, u, mth, new=True, ahead=True, p=p):
                    for j in range(NPAIR):
                        if p in CONVS[1:] and ahead and j < NH:
                            hid_chunk(n + 1, 1 - u, j, mth + u)
                        if p in CONVS and new and j + 2 < NPAIR:
                            conv_pair(n, u, j + 2, mth)
                        if p in CONVS and ahead and j + 2 >= NPAIR:
                            conv_pair(n + 1, 1 - u, j + 2 - NPAIR, mth + u)
                        if p == "react" and ahead:
                            if j in (0, 1, 3, 4):
                                look_up(n + 1, 1 - u, (0, 1, None, 2, 3)[j])
                            if j in (2, 3, 5, 6):
                                choose_rows(n + 1, 1 - u, (None, None, 0, 1, None, 2, 3)[j])
                        if not (isinstance(n, int) and n == 0):
                            sum_pair(n - 1, j)

                if p in CONVS[1:]:
                    for c in range(NH):
                        hid_chunk(0, 0, c, 0)
                if p in CONVS:
                    conv_pair(0, 0, 0, 0)
                    conv_pair(0, 0, 1, 0)
                if p == "react":
                    for b in range(NL):
                        look_up(0, 0, b)
                        choose_rows(0, 0, b)
                group_loop(pe, body, NG - 2)
                body(NG - 2, 0, NG // 2 - 1)
                body(NG - 1, 1, NG // 2 - 1, ahead=False)
                body(NG, 0, NG // 2, new=False, ahead=False)
                for b in range(NB):
                    mm = m.matmul(acc[0:H * F, b, 0:LO + 1], zeros[:, 0:H * F], zeros[:], start=False, stop=True)
                mm.then_inc(acc_done, 1)

                if p in ("net", "react", "conv1"):
                    at(p, "turned")
                    for c in range(NC):
                        mm = m.transpose(wide[0:NP, 0, c * 128:(c + 1) * 128], sums[:, c * NP:(c + 1) * NP], ident[:])
                    mm.then_inc(step, 1)
                if p == "net":
                    at(p, "h turned")
                    for c in range(NC):
                        mm = m.transpose(hidden[:, 0, c * NP:(c + 1) * NP],
                                         hs[:, 8 * c:8 * c + 8].rearrange("p h f -> p (h f)"), ident[0:NP, 0:NP])
                    mm.then_inc(step, 1)
                    for k2 in range(2):
                        at(p, f"types {k2}")
                        for q in range(4):
                            c = 2 * k2 + q // 2
                            mm = m.matmul(wide[0:NP, q, :], hcols[:, c * NP:(c + 1) * NP],
                                          types_sb[:, (q % 2) * 512:(q % 2 + 1) * 512], start=True, stop=True)
                        mm.then_inc(step, 1)
                if p == "gru":
                    for k2 in range(2):
                        at(p, f"gates {k2}")
                        for q in range(4):
                            c = 2 * k2 + q // 2
                            frm, w = (hcols, hh_sb) if q % 2 else (sums, ih_sb)
                            m.matmul(wide[0:NP, q, 0:384], frm[:, c * NP:(c + 1) * NP], w[:], start=True, stop=False)
                            mm = m.matmul(wide[0:NP, q, 0:384], ones[0:1, 0:NP], gate_b[:, q % 2], start=False,
                                          stop=True)
                        mm.then_inc(step, 1)
                if p == "conv0":
                    at(p, "turned")
                    for q in range(8):
                        c, b = q // 2, q % 2
                        mm = m.transpose(wide[0:NP, q // 4, (q % 4) * 4 * FA:(q % 4 + 1) * 4 * FA],
                                         sums[0:4 * FA, bass.ds(2 * c * NP + b, NP, step=2)], ident[0:4 * FA, 0:4 * FA])
                    mm.then_inc(step, 1)
                if p in ("conv0", "conv1"):
                    at(p, "all s")
                    m.matmul(hidden[0:NP, 0, 0:NS], ones[0:NP, 0:NP], bn[:, 0, 0:NS], start=True, stop=True).then_inc(step, 1)
                    at(p, "all sq")
                    w = NS + NV if p == "conv0" else NS
                    m.matmul(hidden[0:NP, 1, 0:w], ones[0:NP, 0:NP], bn[:, 2, 0:w], start=True, stop=True).then_inc(step, 1)

        @block.vector
        def _(dve):
            v = nc.vector

            def at(stage, name):
                dve.wait_ge(step, before(stage, name))

            n_set = [0]

            def then(ins):
                n_set[0] += 1
                ins.then_inc(setup, 1)
                dve.wait_ge(setup, n_set[0])

            def norm(stage):
                at(stage, "mean")
                v.tensor_reduce(st[:, 0], xs[:], AX.X, ALU.add).then_inc(step, 1)
                at(stage, "scale")
                v.tensor_scalar(st[:, 3], st[:, 0], 1.0 / D, None, ALU.mult).then_inc(step, 1)
                at(stage, "center")
                v.tensor_tensor(t0[:, :, 0:D], xs[:], bc(st[:, 3], [1, NC * 8], [0, D]), ALU.subtract).then_inc(step, 1)
                at(stage, "square")
                v.tensor_tensor(t1[:, :, 0:D], t0[:, :, 0:D], t0[:, :, 0:D], ALU.mult).then_inc(step, 1)
                at(stage, "var")
                v.tensor_reduce(st[:, 1], t1[:, :, 0:D], AX.X, ALU.add).then_inc(step, 1)
                at(stage, "rstd")
                v.reciprocal(st[:, 4], st[:, 2]).then_inc(step, 1)
                at(stage, "norm")
                v.tensor_tensor(t1[:, :, 0:D], t0[:, :, 0:D], bc(st[:, 4], [1, NC * 8], [0, D]), ALU.mult).then_inc(step, 1)
                at(stage, "relu")
                v.tensor_scalar(hs[:], t1[:, :, 0:D], 0.0, None, ALU.max).then_inc(step, 1)

            v.memset(eps[:, 1:2], 0.0)
            v.memset(zeros[:], 0.0)
            v.memset(sums[:], 0.0)
            v.memset(t1[:], 0.0)
            v.memset(ea[:], 1.0)
            v.memset(msg[:], 1.0)
            then(v.memset(eps[:, 0:1], EPS))
            dve.wait_ge(edges_loaded, 16 * 6)
            then(v.tensor_scalar(rows_bits, rows_i, 3, None, ALU.arith_shift_right))
            then(v.tensor_copy(rows_lo, rows_bits))
            then(v.tensor_scalar(rows_bits, rows_i, 7, None, ALU.bitwise_and))
            then(v.tensor_copy(rows_hi, rows_bits))
            dve.wait_ge(pool_consts, 8)
            then(v.tensor_scalar(part_i[:, 1:2], part_i[:, 0:1], 4, None, ALU.arith_shift_right))
            then(v.tensor_copy(part_hi[:], part_i[:, 1:2]))
            assert n_set[0] == N_ROWS
            then(v.tensor_reduce(choose[:], bc(ident[:, 0:1], [1, D], [D, 8]), AX.X, ALU.add))
            for idx, keys, shift in ((src_i, key_src8, 3), (src_i, key_src4, 2), (dst_i, key_dst8, 3)):
                then(v.tensor_scalar(bits[:], idx[:], shift, None, ALU.arith_shift_right))
                then(v.tensor_copy(keys[:, :, 0], bits[:]))
                then(v.tensor_scalar(bits[:], idx[:], (1 << shift) - 1, None, ALU.bitwise_and))
                then(v.tensor_copy(keys[:, :, 1], bits[:]))
            then(v.scalar_tensor_tensor(out=typ_i[:], in0=src_i[:], scalar=float(NTYPE), in1=typ_i[:],
                                        op0=ALU.mult, op1=ALU.add))
            then(v.tensor_tensor(len_b[:], unit[:, :, 1], unit[:, :, 1], ALU.mult))
            then(v.tensor_tensor(len_a[:], unit[:, :, 0], unit[:, :, 0], ALU.mult))
            then(v.tensor_tensor(len_a[:], len_a[:], len_b[:], ALU.add))
            then(v.tensor_tensor(len_b[:], unit[:, :, 2], unit[:, :, 2], ALU.mult))
            then(v.tensor_tensor(len_a[:], len_a[:], len_b[:], ALU.add))
            assert n_set[0] == N_SQUARED
            dve.wait_ge(lens, 1)
            then(v.tensor_scalar(len_a[:], len_b[:], 1e-12, None, ALU.add))
            then(v.reciprocal(len_b[:], len_a[:]))
            then(v.tensor_tensor(unit[:], unit[:], bc(len_b[:], [1, T], [0, 3]), ALU.mult))
            assert n_set[0] == N_SETUP
            dve.wait_ge(x_loaded, 16)
            norm("start")
            dve.wait_ge(consts_loaded, 16 * N_CONST)

            for k, p in enumerate(PHASES):
                H, F = HI[p], SUMF[p]
                I, O = IN.get(p), OUTF.get(p)
                lo_n = 2 * LO if p == "conv0" else LO
                hi_vals = hi_vals4 if p == "conv0" else hi_vals8
                first_in = 12 if p == "conv1" else 0

                def form(n, u, m, p=p):
                    if p in scal_count:
                        dve.wait_ge(scal_in[u], m * 16 + (base_scal[p] + 16))
                    if p == "react":
                        dve.wait_ge(chosen, n * NL + NL)
                    dve.wait_ge(gathered[p][u], m * gather_count + gather_count)
                    done = [0]

                    def formed_by(ins):
                        done[0] += 1
                        ins.then_inc(formed, 1)
                        dve.wait_ge(formed, n * FORM[p] + (base_form[p] + done[0]))

                    if p == "react":
                        xi = wide[:, u, 0:TG * D]
                        xj = rows_a[:, u, :, 0:D]
                        wg = scal[:, u, 0:TG]
                        three = lambda ap: ap.rearrange("p (t f) -> p t f", f=D)
                        formed_by(v.tensor_tensor(three(ra[:]), three(xi), xj, ALU.mult))
                        formed_by(v.tensor_tensor(three(ra[:]), three(ra[:]), bc(wg, [1, TG], [0, D]), ALU.mult))
                        formed_by(v.tensor_scalar(three(rb[:]), xj, KH, KD, ALU.mult, ALU.add))
                        formed_by(v.scalar_tensor_tensor(out=rb[:], in0=xi, scalar=KE, in1=rb[:], op0=ALU.mult,
                                                         op1=ALU.add))
                        formed_by(v.reciprocal(rb[:], rb[:]))
                        formed_by(v.tensor_tensor(msg[:, :, 0:D], three(ra[:]), three(rb[:]), ALU.mult))
                    if p == "conv1":
                        vs = vsh[:].rearrange("p (t i c) -> p t i c", t=TG, c=3)
                        formed_by(v.tensor_tensor(vs, rows_a[:, u, :, 0:12].rearrange("p t (i c) -> p t i c", c=3),
                                                  bc(scal[:, u], [3, TG], [0, NV], [1, 3]), ALU.mult))
                        formed_by(v.tensor_reduce(rows_a[:, u, :, 28:32], vs, AX.X, ALU.add))

                def multiply(n, u, j, p=p, I=I, O=O, first_in=first_in):
                    dve.wait_ge(weights, n * NPAIR + (base_conv[p] + j + 1))
                    if not (isinstance(n, int) and n == 0 and j < 2):
                        dve.wait_ge(reduced, n * NPAIR + (base_conv[p] + j - 1))
                    q = (u + j) % 2
                    v.tensor_tensor(prod[:, q, :, 0:I * O].rearrange("p s (o i) -> p s o i", i=I),
                                    wide[:, 2 * q:2 * q + 2, 0:I * O].rearrange("p s (o i) -> p s o i", i=I),
                                    bc(rows_a[:, u, 2 * j, first_in:first_in + I], [32, 2], [0, O], [1, I]),
                                    ALU.mult).then_inc(mult, 1)

                def reduce(n, u, j, p=p, I=I, O=O):
                    dve.wait_ge(mult, n * NPAIR + (base_conv[p] + j + 1))
                    q = (u + j) % 2
                    v.tensor_reduce(msg[:, 2 * j:2 * j + 2, 0:O],
                                    prod[:, q, :, 0:I * O].rearrange("p s (o i) -> p s o i", i=I),
                                    AX.X, ALU.add).then_inc(reduced, 1)

                def spread_pair(n, u, j, p=p, H=H, F=F, lo_n=lo_n, hi_vals=hi_vals):
                    if not (isinstance(n, int) and n == 0):
                        dve.wait_ge(summed, n * NPAIR + (base_pair[p] + j + 1 - NPAIR))
                    for t in (2 * j, 2 * j + 1):
                        hm = v.tensor_scalar(himask[:, (2 * u + t) % 4, 0:H * F], hi_vals[:].rearrange("p h f -> p (h f)"),
                                             key[:, u, t, 1:2], None, ALU.is_equal)
                    hm.then_inc(masked, 1)
                    if p not in ACT_LO:
                        for t in (2 * j, 2 * j + 1):
                            v.tensor_scalar(onehot[:, t, 0:lo_n], lo_vals[:, 0:lo_n], key[:, u, t, 0:1], None,
                                            ALU.is_equal)
                    dve.wait_ge(masked, n * NPAIR + (base_pair[p] + j + 1))
                    for t in (2 * j, 2 * j + 1):
                        h = (2 * u + t) % 4
                        sp_ = v.tensor_tensor(spread[:, t, 0:3 * H * F].rearrange("p (s h f) -> p s h f", s=3, h=H),
                                              bc(parts[:, u, t, 0:1], [F, 3], [0, H], [1, F]),
                                              bc(himask[:, h, 0:1], [0, 3], [F, H], [1, F]), ALU.mult)
                    sp_.then_inc(spreadd, 1)

                def split_group(n, u, p=p, F=F):
                    def part(i):
                        return parts[:, u, :, i * F:(i + 1) * F]

                    def left():
                        return rest[:, 0:TG * F].rearrange("p (t f) -> p t f", f=F)

                    value = dict(gru=rows_a[:, u, :, 0:F], conv0=msg[:, :, NV:NV + FA]).get(p, msg[:, :, 0:F])
                    b = base_split[p]
                    v.tensor_copy(part(0), value).then_inc(split, 1)
                    dve.wait_ge(split, n * 4 + (b + 1))
                    v.tensor_tensor(left(), value, part(0), ALU.subtract).then_inc(split, 1)
                    dve.wait_ge(split, n * 4 + (b + 2))
                    v.tensor_copy(part(1), left()).then_inc(split, 1)
                    dve.wait_ge(split, n * 4 + (b + 3))
                    v.tensor_tensor(part(2), left(), part(1), ALU.subtract).then_inc(split, 1)
                    dve.wait_ge(split, n * 4 + (b + 4))

                def turn_lo(n, u, c):
                    if c == 0:
                        dve.wait_ge(look_in[u], (n // 2 if isinstance(n, int) else mm_of[0]) * 32 + 32)
                        if not (isinstance(n, int) and n < 2):
                            dve.wait_ge(looked, n * NL - NL)
                    i = v.tensor_scalar(onehot_t[u][:, c], lo_t[:, u], part_lo[:, c:c + 1], None, ALU.is_equal)
                    if c == NC - 1:
                        i.then_inc(turned_lo, 1)

                mm_of = [None]

                def pick(n, u, b):
                    dve.wait_ge(looked, n * NL + (b + 1))
                    if not (isinstance(n, int) and n == 0 and b < 2):
                        dve.wait_ge(chosen, n * NL + (b - 1))
                    c0, c1 = LOOK[b] * 128, LOOK[b + 1] * 128
                    v.scalar_tensor_tensor(out=picked_rows[:, b % 2, 0:c1 - c0], in0=hi_t[:, u, c0:c1],
                                           scalar=part_hi[:], in1=hidden[:, b % 2, 0:c1 - c0], op0=ALU.is_equal,
                                           op1=ALU.mult).then_inc(picked, 1)

                def body(n, u, m, new=True, ahead=True, two_ahead=True, p=p, form=form, multiply=multiply, reduce=reduce, spread_pair=spread_pair,
                         split_group=split_group):
                    old = not (isinstance(n, int) and n == 0)
                    if new:
                        form(n, u, m)
                    if old:
                        dve.wait_ge(key_in[1 - u], (m - 1 + u) * 16 + (base_key[p] + 16))
                    mm_of[0] = m + 1
                    for j in range(NPAIR):
                        if p == "react" and two_ahead and j in (2, 3, 4, 5):
                            turn_lo(n + 2, u, j - 2)
                        if p == "react" and ahead and j in (1, 2, 4, 5):
                            pick(n + 1, 1 - u, (None, 0, 1, None, 2, 3)[j])
                        if new and p in CONVS:
                            multiply(n, u, j)
                        if old:
                            spread_pair(n - 1, 1 - u, j)
                        if new and p in CONVS:
                            reduce(n, u, j)
                    if not new:
                        return
                    if p in CONVS:
                        dve.wait_ge(reduced, n * NPAIR + (base_conv[p] + NPAIR))
                    if p == "conv0":
                        v.tensor_tensor(msg[:, :, NV + NS:NV + NS + 12].rearrange("p t (j c) -> p t j c", c=3),
                                        bc(msg[:, 0, 0:NV], [NV + FA, TG], [1, NV], [0, 3]),
                                        bc(scal[:, u], [3, TG], [0, NV], [1, 3]), ALU.mult).then_inc(formed, 1)
                        dve.wait_ge(formed, n * FORM[p] + (base_form[p] + 1))
                    split_group(n, u)

                if p == "react":
                    for n in range(2):
                        for c in range(NC):
                            turn_lo(n, n, c)
                    for b in range(NL):
                        pick(0, 0, b)
                group_loop(dve, body, NG - 2)
                body(NG - 2, 0, NG // 2 - 1, two_ahead=False)
                body(NG - 1, 1, NG // 2 - 1, ahead=False, two_ahead=False)
                body(NG, 0, NG // 2, new=False, ahead=False, two_ahead=False)

                turned = wide[0:NP, 0].rearrange("p (n f) -> p n f", f=D)
                T0, T1 = t0[:, :, 0:D], t1[:, :, 0:D]
                nodes = lambda ap: bc(ap, [1, NC * 8], [0, D])
                feats = lambda ap, w=NS: bc(ap, [0, NC * 8], [1, w])
                if p == "net":
                    at(p, "add")
                    v.tensor_tensor(xs[:], xs[:], turned, ALU.add).then_inc(step, 1)
                    norm(p)
                if p == "gru":
                    at(p, "rz")
                    v.tensor_tensor(t0[:], gi[:, :, 0:32], gh[:, :, 0:32], ALU.add).then_inc(step, 1)
                    at(p, "reset")
                    v.tensor_tensor(T1, T0, gh[:, :, 32:48], ALU.mult).then_inc(step, 1)
                    at(p, "new in")
                    v.tensor_tensor(T1, T1, gi[:, :, 32:48], ALU.add).then_inc(step, 1)
                    at(p, "diff")
                    v.tensor_tensor(gi[:, :, 0:16], hs[:], T1, ALU.subtract).then_inc(step, 1)
                    at(p, "update")
                    v.tensor_tensor(gi[:, :, 0:16], gi[:, :, 0:16], t0[:, :, 16:32], ALU.mult).then_inc(step, 1)
                    at(p, "blend")
                    v.tensor_tensor(T1, T1, gi[:, :, 0:16], ALU.add).then_inc(step, 1)
                    at(p, "add")
                    v.tensor_tensor(xs[:], xs[:], T1, ALU.add).then_inc(step, 1)
                    norm(p)
                    hp = lambda i: h_parts[:, i].rearrange("p (n f) -> p n f", f=D)
                    at(p, "part 0")
                    v.tensor_copy(hp(0), hs[:]).then_inc(step, 1)
                    at(p, "left 0")
                    v.tensor_tensor(T0, hs[:], hp(0), ALU.subtract).then_inc(step, 1)
                    at(p, "part 1")
                    v.tensor_copy(hp(1), T0).then_inc(step, 1)
                    at(p, "part 2")
                    v.tensor_tensor(hp(2), T0, hp(1), ALU.subtract).then_inc(step, 1)
                if p == "react":
                    at(p, "f1")
                    v.tensor_scalar(T0, hs[:], -1.0 / KK, 1.0, ALU.mult, ALU.add).then_inc(step, 1)
                    at(p, "f2")
                    v.tensor_scalar(T1, hs[:], 1.0 / KC, -1.0, ALU.mult, ALU.add).then_inc(step, 1)
                    at(p, "f3")
                    v.tensor_tensor(T0, T0, hs[:], ALU.mult).then_inc(step, 1)
                    at(p, "f4")
                    v.tensor_tensor(T0, T0, T1, ALU.mult).then_inc(step, 1)
                    at(p, "f5")
                    v.tensor_tensor(xs[:], xs[:], T0, ALU.add).then_inc(step, 1)
                    at(p, "add")
                    v.tensor_tensor(xs[:], xs[:], turned, ALU.add).then_inc(step, 1)
                    at(p, "const")
                    v.tensor_scalar(xs[:], xs[:], KB, None, ALU.add).then_inc(step, 1)
                    at(p, "row of ones")
                    v.memset(ea[:], 1.0).then_inc(step, 1)
                    norm(p)
                if p == "conv0":
                    S, V = oa[:, :, 0:NS], oa[:, :, NS:NS + 12]
                    at(p, "node major")
                    v.tensor_copy(oa[:].rearrange("p (b n) f -> p b (n f)", b=2),
                                  wide[0:NP, 0:2, 0:16 * FA]).then_inc(step, 1)
                    at(p, "count")
                    v.tensor_scalar(st[:, 0], oa[:, :, FA - 1], 1.0, None, ALU.max).then_inc(step, 1)
                    at(p, "inv count")
                    v.reciprocal(st[:, 5], st[:, 0]).then_inc(step, 1)
                    at(p, "quarter")
                    v.tensor_scalar(st[:, 1], st[:, 5], NS ** -0.5, None, ALU.mult).then_inc(step, 1)
                    at(p, "average")
                    v.tensor_tensor(oa[:, :, 0:28], oa[:, :, 0:28], bc(st[:, 1], [1, NC * 8], [0, 28]),
                                    ALU.mult).then_inc(step, 1)
                    at(p, "average v")
                    v.tensor_scalar(V, V, 3.0 ** 0.5, None, ALU.mult).then_inc(step, 1)
                    at(p, "sum s")
                    v.tensor_reduce(bn[:, 0, 0:NS], bc(oa[:, 0, 0:1], [1, NS], [FA, NC * 8]), AX.X,
                                    ALU.add).then_inc(step, 1)
                if p == "conv1":
                    at(p, "average")
                    v.tensor_tensor(T0, turned, nodes(st[:, 5]), ALU.mult).then_inc(step, 1)
                    at(p, "norm 20")
                    v.tensor_scalar(T0, T0, (NS + NV) ** -0.5, None, ALU.mult).then_inc(step, 1)
                    at(p, "sum s")
                    v.tensor_reduce(bn[:, 0, 0:NS], bc(t0[:, 0, 0:1], [1, NS], [32, NC * 8]), AX.X,
                                    ALU.add).then_inc(step, 1)
                    S = T0
                if p in ("conv0", "conv1"):
                    at(p, "mean s")
                    v.tensor_scalar(bn[:, 1, 0:NS], hidden[0:NP, 0, 0:NS], 1.0 / N, None, ALU.mult).then_inc(step, 1)
                    at(p, "centered")
                    v.tensor_tensor(T0, S, feats(bn[:, 1, 0:NS]), ALU.subtract).then_inc(step, 1)
                    at(p, "masked")
                    v.tensor_tensor(T0, T0, nodes(mask[:]), ALU.mult).then_inc(step, 1)
                    at(p, "squares")
                    v.tensor_tensor(T1, T0, T0, ALU.mult).then_inc(step, 1)
                    if p == "conv0":
                        at(p, "squares v")
                        v.tensor_tensor(t1[:, :, NS:NS + 12], V, V, ALU.mult).then_inc(step, 1)
                    at(p, "sum sq s")
                    v.tensor_reduce(bn[:, 2, 0:NS], bc(t1[:, 0, 0:1], [1, NS], [32, NC * 8]), AX.X,
                                    ALU.add).then_inc(step, 1)
                    if p == "conv0":
                        at(p, "sum sq v")
                        v.tensor_reduce(bn[:, 2, NS:NS + NV], bc(t1[:, 0, NS:NS + 1], [3, NV], [32, NC * 8], [1, 3]),
                                        AX.XY, ALU.add).then_inc(step, 1)
                    at(p, "var s")
                    v.tensor_scalar(bn[:, 4, 0:NS], hidden[0:NP, 1, 0:NS], 1.0 / N, None, ALU.mult).then_inc(step, 1)
                    if p == "conv0":
                        at(p, "var v")
                        v.tensor_scalar(bn[:, 4, NS:], hidden[0:NP, 1, NS:NS + NV], 1.0 / (3 * N), None,
                                        ALU.mult).then_inc(step, 1)
                    w = NS + NV if p == "conv0" else NS
                    g0 = 0 if p == "conv0" else 2 * NS + NV
                    b0 = g0 + w
                    at(p, "rstd")
                    v.reciprocal(bn[:, 6, 0:w], bn[:, 5, 0:w]).then_inc(step, 1)
                    at(p, "gain")
                    v.tensor_tensor(bn[:, 7, 0:w], bn[:, 6, 0:w], norms[:, g0:g0 + w], ALU.mult).then_inc(step, 1)
                    at(p, "scaled")
                    v.tensor_tensor(T0, T0, feats(bn[:, 7, 0:NS]), ALU.mult).then_inc(step, 1)
                    at(p, "shift")
                    to = t1[:, :, 12:28] if p == "conv0" else T1
                    v.tensor_tensor(to, T0, feats(norms[:, b0:b0 + NS]), ALU.add).then_inc(step, 1)
                    if p == "conv0":
                        at(p, "scaled v")
                        v.tensor_tensor(t1[:, :, 0:12].rearrange("p n (j c) -> p n j c", c=3),
                                        V.rearrange("p n (j c) -> p n j c", c=3),
                                        bc(bn[:, 7, NS:NS + NV], [0, NC * 8], [1, NV], [0, 3]), ALU.mult).then_inc(step, 1)
                    else:
                        at(p, "add")
                        v.tensor_tensor(xs[:], xs[:], T1, ALU.add).then_inc(step, 1)


def kernel(**inputs):
    import numpy as np
    import concourse.bacc as bacc
    from concourse.bass_utils import run_bass_kernel_spmd

    a = {k: np.asarray(v) for k, v in inputs.items()}

    def edges(v, fill):
        full = np.full((128 * T,) + v.shape[1:], fill, v.dtype)
        full[:E] = v
        return full.reshape((128, T) + v.shape[1:])

    def columns(v):
        return np.ascontiguousarray(edges(v, 0).transpose(2, 1, 0)).reshape(v.shape[1], T * 128)

    def diagonal(w):
        r, c = w.shape
        full = np.zeros((8, r, 8, c), w.dtype)
        for h in range(8):
            full[h, :, h, :] = w
        return full.reshape(8 * r, 8 * c)

    def with_bias(w, b):
        full = np.zeros((128, w.shape[1]), w.dtype)
        full[:len(w)] = w
        full[len(w)] = b
        return full

    def hidden_weights(w, b):
        full = np.zeros((128, 128), w.dtype)
        full[:, :DA] = with_bias(w, b)
        full[DA, DA] = 1
        return full

    def out_major(w, i, o):
        return w.reshape(w.shape[0], i, o).transpose(0, 2, 1).reshape(w.shape[0], i * o)

    x = np.zeros((NPAD, D), a["x"].dtype)
    x[:N] = a["x"]
    f0 = with_bias(a["L3_gnn_fc0_w2"], a["L3_gnn_fc0_b2"])
    f1 = with_bias(a["L3_gnn_fc1_w2"], a["L3_gnn_fc1_b2"])
    emb = a["L1_gnn_edge_emb"].reshape(NTYPE, D, D).transpose(2, 0, 1).reshape(D, NTYPE * D)
    arrays = {
        "x": x,
        "src": edges(a["src"], PADNODE),
        "dst": edges(a["dst"], PADNODE),
        "etype": edges(a["edge_type_8"], 0),
        "weight": edges(a["edge_weight"], 0),
        "vec": edges(a["edge_attr_3"], 0).reshape(128, T * 3),
        "ea16": columns(a["edge_attr_16"]),
        "ea48": columns(a["edge_attr_48"]),
        "net_w": with_bias(a["L0_gnn_kernel"], a["L0_gnn_bias"]),
        "types_w": diagonal(emb),
        "ih_w": diagonal(a["L1_gnn_w_ih"].T),
        "hh_w": diagonal(a["L1_gnn_w_hh"].T),
        "ih_b": np.tile(a["L1_gnn_b_ih"], 8)[None, :],
        "hh_b": np.tile(a["L1_gnn_b_hh"], 8)[None, :],
        "w1": np.stack([hidden_weights(a[f"L3_gnn_fc{k}_w1"], a[f"L3_gnn_fc{k}_b1"]) for k in range(2)]),
        "w2": np.stack([np.concatenate([out_major(f0[:, NS * NS:], NS, NV), out_major(f0[:, :NS * NS], NS, NS)], 1),
                        out_major(f1, NS + NV, NS)]),
        "src_rows": edges(a["src"], PADNODE).T.reshape(128, T),
        "gs0": a["L3_gnn_bn0_gs"], "bs0": a["L3_gnn_bn0_bs"], "gv0": a["L3_gnn_bn0_gv"],
        "gs1": a["L3_gnn_bn1_gs"], "bs1": a["L3_gnn_bn1_bs"],
    }
    nc = bacc.Bacc("TRN2", target_bir_lowering=False, num_devices=1)
    feed, args = {}, []
    for name, v in arrays.items():
        v = np.ascontiguousarray(v)
        feed[f"in_{name}"] = v
        args.append(nc.dram_tensor(f"in_{name}", v.shape, mybir.dt.from_np(v.dtype), kind="ExternalInput").ap())
    args.append(nc.dram_tensor("out_x", (NPAD, D), F32, kind="ExternalOutput").ap())
    gnn_kernel(nc, *args)
    r = run_bass_kernel_spmd(nc, [feed], core_ids=[0])
    return r.results[0]["out_x"][:N]
```

```python
from contextlib import ExitStack

import concourse.bass as bass
from concourse import mybir

F32 = mybir.dt.float32
F16 = mybir.dt.float16
BF16 = mybir.dt.bfloat16
I32 = mybir.dt.int32
ALU = mybir.AluOpType
ACT = mybir.ActivationFunctionType
AX = mybir.AxisListType

N = 3125
E = 103125
D = 16
TG = 14
NG = 58
T = TG * NG
NPAIR = TG // 2
NP = 98
NC = 4
NPAD = NC * NP * 8
LO = -(-N // 8)
NTYPE = 8
DA = 48
NS, NV = 16, 4
FA = NS + 3 * NV + 1
WN = (NS + NV) * NS
EPS = 1e-5
KB, KK, KC, KD, KE, KH = 0.1, 5.0, 1.0, 5.0, 0.9, 0.1
PADNODE = NPAD - 1
HT = TG // 2
HC = 448
NH = HT * 128 // HC

PHASES = ("net", "gru", "react", "conv0", "conv1")
CONVS = ("net", "conv0", "conv1")
DVE_LO = dict(gru=range(0, TG, 4), conv0=range(0, TG, 2))
LOOK_FROM = dict(gru=TG - 4, react=0)
LOOK = dict(gru=(0, 4), react=(0, 4, 8, 12, 13))
NL = {p: len(LOOK[p]) - 1 for p in LOOK}
LG = LOOK["gru"][-1]
LT = LOOK["react"][-1]
MASKS = ("net", "conv1")
LC = 3
LREST = NPAD // 8 - 128 * LC
HALVES = dict(net=((0, 8), (8, TG)), conv0=((0, 8), (8, TG)), conv1=((0, 8), (8, TG)),
              gru=((0, TG),), react=((0, TG),))
SUMF = dict(net=D, gru=D, react=D, conv0=FA, conv1=D)
HI = dict(net=8, gru=8, react=8, conv0=4, conv1=8)
IN = dict(net=D, conv0=NS, conv1=NS + NV)
OUTF = dict(net=D, conv0=NS + NV, conv1=NS)
GCOLS = dict(net=D, gru=D, react=D, conv0=D, conv1=32)

NORM = ["mean", "scale", "center", "square", "var", "std", "rstd", "norm", "relu"]
STEPS = {
    "start": NORM,
    "net": ["sums", "turned", "add"] + NORM + ["h turned", "h cols", "types 0", "types 0 out", "types 1",
                                               "types 1 out"],
    "gru": ["gates hid", "gates hid out", "sums", "gates in",
            "rz", "sigmoid", "reset", "new in", "tanh", "diff", "update", "blend", "add"] + NORM,
    "react": ["f1", "f2", "f3", "f4", "f5", "const", "sums", "turned", "add"] + NORM,
    "conv0": ["sums", "turned", "node major", "count", "inv count", "quarter", "average", "average v", "sum s",
              "all s", "mean s", "centered", "masked", "squares", "squares v", "sum sq s", "sum sq v", "all sq",
              "var s", "var v", "std", "rstd", "gain", "scaled", "shift", "scaled v"],
    "conv1": ["sums", "turned", "average", "norm 20", "sum s", "all s", "mean s", "centered", "masked", "squares",
              "sum sq s", "all sq", "var s", "std", "rstd", "gain", "scaled", "shift", "add"],
}
STAGES = ["start", *PHASES]
FIRST_STEP = {s: sum(len(STEPS[x]) for x in STAGES[:k]) for k, s in enumerate(STAGES)}


def before(stage, name):
    return FIRST_STEP[stage] + STEPS[stage].index(name)


def ended(stage):
    return FIRST_STEP[stage] + len(STEPS[stage])


def gnn_kernel(nc, x, src, dst, etype, weight, vec, ea16, ea48, net_w, types_w, ih_w, hh_w, ih_b, hh_b,
               w1, w2, by_type, src_rows, gs0, bs0, gv0, gs1, bs1, out):
    with ExitStack() as ctx:
        def sb(name, shape, dt):
            return ctx.enter_context(nc.sbuf_tensor(name, shape, dt))

        def sem(name):
            return ctx.enter_context(nc.semaphore(name))

        def bc(ap, *dims):
            return bass.AP(ap.tensor, ap.offset, [ap.ap[0], *[list(d) for d in dims]])

        table = {p: nc.dram_tensor(f"table_{p}", [NPAD * (NTYPE if p == "gru" else 1), GCOLS[p]], F32).ap()
                 for p in PHASES}

        lo_rows = nc.dram_tensor("lo_rows", [128, T], F16).ap()
        hi_rows = nc.dram_tensor("hi_rows", [128, T], F16).ap()
        masks_kept = nc.dram_tensor("masks_kept", [128, T * 128], BF16).ap()

        acc = ctx.enter_context(nc.psum_tensor("acc", [128, 2, 512], F32))
        hidden = ctx.enter_context(nc.psum_tensor("hidden", [128, 2, 512], F32))
        wide = ctx.enter_context(nc.psum_tensor("wide", [128, 4, 512], F32))

        src_i = sb("src_i", [128, T], I32)
        dst_i = sb("dst_i", [128, T], I32)
        typ_i = sb("typ_i", [128, T], I32)
        bits = sb("bits", [128, T], I32)
        key_src8 = sb("key_src8", [128, T, 2], F32)
        key_src4 = sb("key_src4", [128, T, 2], F32)
        key_dst8 = sb("key_dst8", [128, T, 2], F32)
        wgt = sb("wgt", [128, T], F32)
        unit = sb("unit", [128, T, 3], F32)
        len_a = sb("len_a", [128, T], F32)
        len_b = sb("len_b", [128, T], F32)

        lo_vals = sb("lo_vals", [128, 2 * LO], F16)
        hi_vals8 = sb("hi_vals8", [128, 8, D], F16)
        hi_vals4 = sb("hi_vals4", [128, 4, FA], F16)
        zeros = sb("zeros", [128, LO + 1], BF16)
        ident = sb("ident", [128, 128], F32)
        ones = sb("ones", [128, 128], F32)
        mask = sb("mask", [NP, NC * 8], F32)
        eps = sb("eps", [128, 2], F32)
        part_i = sb("part_i", [128, 2], I32)
        part_hi = sb("part_hi", [128, 1], F32)
        part_lo = sb("part_lo", [128, LC + 1], F32)
        choose = sb("choose", [128, D], F32)
        net_sb = sb("net_sb", [128, D * D], F32)
        types_sb = sb("types_sb", [128, 8 * NTYPE * D], F32)
        ih_sb = sb("ih_sb", [128, 8 * 48], F32)
        hh_sb = sb("hh_sb", [128, 8 * 48], F32)
        gate_b = sb("gate_b", [1, 2, 8 * 48], F32)
        w1_sb = sb("w1_sb", [128, 2, 128], F32)
        w2_sb = sb("w2_sb", [128, 2, 2, WN], F32)
        norms = sb("norms", [NP, 4 * NS + NV], F32)

        idx_a = sb("idx_a", [128, 2, TG], I32)
        by_type_sb = sb("by_type_sb", [128, D * NTYPE], F32)
        type_vals = sb("type_vals", [128, D, NTYPE], F16)
        idx_b = sb("idx_b", [128, 2, TG - LT], I32)
        rows_b = sb("rows_b", [128, 2, TG - LT, D], F32)
        key = sb("key", [128, 2, TG, 2], F32)
        rows_a = sb("rows_a", [128, 2, TG, 32], F32)
        scal = sb("scal", [128, 2, TG * 3], F32)
        ea = sb("ea", [128, 2, TG * 128], F32)
        hid = sb("hid", [128, 2, TG * 128], F32)
        prod = sb("prod", [128, 2, 2, WN], F32)
        msg = sb("msg", [128, TG, NV + FA], F32)
        vsh = sb("vsh", [128, TG * 12], F32)
        rest = sb("rest", [128, TG * FA], F32)
        away = sb("away", [128, 4, LO + 1], BF16)
        parts = sb("parts", [128, 2, TG * 3 * 32], BF16)
        onehot = sb("onehot", [128, TG, 2 * LO], BF16)
        himask = sb("himask", [128, 4, 128], BF16)
        spread = sb("spread", [128, TG * 3 * 128], BF16)
        lo_t = sb("lo_t", [128, 2, TG * 128], F16)
        hi_t = sb("hi_t", [128, 2, TG * 128], F16)
        h_parts = sb("h_parts", [128, 3, (LC + 1) * 128], BF16)
        h_rest = sb("h_rest", [128, 128], BF16)
        rb = sb("rb", [128, TG * D], F32)

        onehot_t = [b[:].rearrange("p u f -> p (u f)").bitcast(BF16).rearrange("p (c e) -> p c e", c=LC + 1)
                    for b in (hid, ea)]
        h_by_lo = len_b[:, 0:(LC + 1) * 128]
        by_type_masked = len_a[:, 0:LG * D * NTYPE].rearrange("p (t m k) -> p t m k", t=LG, m=D)
        typ_f = bits[:].bitcast(F32)
        group_masks = hi_t[:].bitcast(BF16)
        ra = prod[:].rearrange("p a b f -> p (a b f)")[:, 1024:1024 + TG * D]
        picked_rows = prod[:].rearrange("p a b f -> p (a b f)")[:, 0:1024].rearrange("p (b e) -> p b e", b=2)
        scratch = onehot[:].rearrange("p t f -> p (t f)")
        rows_i = scratch[:, 0:2 * T].bitcast(I32)
        rows_bits = scratch[:, 2 * T:4 * T].bitcast(I32)
        rows_lo = scratch[:, 4 * T:5 * T].bitcast(F16)
        rows_hi = scratch[:, 5 * T:6 * T].bitcast(F16)

        xs = sb("xs", [NP, NC * 8, D], F32)
        hs = sb("hs", [NP, NC * 8, D], F32)
        t0 = sb("t0", [NP, NC * 8, 32], F32)
        t1 = sb("t1", [NP, NC * 8, 32], F32)
        st = sb("st", [NP, 6, NC * 8], F32)
        hcols = sb("hcols", [128, NC * NP], F32)
        sums = sb("sums", [128, 2 * NC * NP], F32)
        h_left = sums[:, 0:(LC + 1) * 128]
        gates = sb("gates", [NP, 2, NC * 8 * 48], F32)
        gi = gates[:, 0].rearrange("p (n f) -> p n f", f=48)
        gh = gates[:, 1].rearrange("p (n f) -> p n f", f=48)
        typed = gates[:].rearrange("p a b -> p (a b)")[:, 0:4 * 512].rearrange("p (q f) -> p q f", q=4)
        oa = sb("oa", [NP, NC * 8, FA], F32)
        bn = sb("bn", [NP, 12, NS + NV], F32)

        x_loaded = sem("x_loaded")
        consts_loaded = sem("consts_loaded")
        edges_loaded = sem("edges_loaded")
        pool_consts = sem("pool_consts")
        setup = sem("setup")
        lens = sem("lens")
        step = sem("step")
        tabled = {p: sem(f"tabled_{p}") for p in PHASES}
        idx_in = [sem(f"idx_in{u}") for u in range(2)]
        key_in = [sem(f"key_in{u}") for u in range(2)]
        scal_in = [sem(f"scal_in{u}") for u in range(2)]
        rows_keys = sem("rows_keys")
        ones_row = sem("ones_row")
        h_out = sem("h_out")
        h_in = sem("h_in")
        h_split = sem("h_split")
        lo_in = [sem(f"lo_in{u}") for u in range(2)]
        hi_in = [sem(f"hi_in{u}") for u in range(2)]
        mask_out = [sem(f"mask_out{u}") for u in range(2)]
        mask_in = [sem(f"mask_in{u}") for u in range(2)]
        ea_in = [sem(f"ea_in{u}") for u in range(2)]
        gathered = {p: [sem(f"gathered_{p}{u}") for u in range(2)] for p in PHASES}
        hid_mm = sem("hid_mm")
        hid_relu = sem("hid_relu")
        weights = sem("weights")
        mult = sem("mult")
        reduced = sem("reduced")
        spreadd = sem("spreadd")
        masked = sem("masked")
        summed = sem("summed")
        split = sem("split")
        formed = sem("formed")
        acc_done = sem("acc_done")
        stored = sem("stored")
        apart = sem("apart")
        lo_ready = sem("lo_ready")
        turned_lo = sem("turned_lo")
        looked = sem("looked")
        picked = sem("picked")
        chosen = sem("chosen")
        slot_free = sem("slot_free")
        rows_free = sem("rows_free")

        def earlier(phase, per_group, phases=PHASES):
            k = PHASES.index(phase)
            return sum((per_group[q] if isinstance(per_group, dict) else per_group) * NG
                       for q in phases if PHASES.index(q) < k)

        FORM = dict(gru=2, react=6, conv0=2, conv1=2)
        SPLIT = {p: 4 * len(HALVES[p]) for p in PHASES}
        scal_count = dict(gru=16, react=16, conv0=16, conv1=16)
        base_scal = {p: earlier(p, 16, tuple(scal_count)) // 2 for p in PHASES}
        base_pair = {p: earlier(p, NPAIR) for p in PHASES}
        base_conv = {p: earlier(p, NPAIR, CONVS) for p in PHASES}
        base_split = {p: earlier(p, SPLIT) for p in PHASES}
        base_key = {p: earlier(p, 16) // 2 for p in PHASES}
        idx_count = {p: 32 if p == "react" else 16 for p in PHASES}
        base_idx = {p: earlier(p, idx_count) // 2 for p in PHASES}
        ea_count = dict(net=16, conv0=32, conv1=32)
        base_ea = {p: earlier(p, ea_count, CONVS) // 2 for p in PHASES}
        base_hid = {p: earlier(p, NH, CONVS[1:]) for p in PHASES}
        base_form = {p: earlier(p, FORM, tuple(FORM)) for p in PHASES}
        gather_count = {p: 16 * (TG + dict(gru=-LG, react=TG - LT).get(p, 0)) for p in PHASES}
        base_look = dict(gru=0, react=NL["gru"] * NG)
        base_turn = dict(gru=0, react=NG)
        key_of = dict(net=key_src8, gru=key_dst8, react=key_src8, conv0=key_src4, conv1=key_src8)

        def group_loop(eng, body, last=NG, first=2, done=0):
            for n in range(done, first):
                body(n, n % 2, n // 2)
            with eng.Fori(0, (last - first) // 2) as i:
                body(i * 2 + first, 0, i + first // 2)
                body(i * 2 + (first + 1), 1, i + first // 2)

        N_CONST = 16
        N_ROWS = 10
        N_SQUARED = N_ROWS + 20
        N_SETUP = N_SQUARED + 4

        block = ctx.enter_context(nc.Block())

        @block.sync
        def _(sp):
            xv = x.rearrange("(c p h) f -> p c (h f)", c=NC, p=NP)
            sp.dma_start(xs[:].rearrange("p (c h) f -> p c (h f)", c=NC), xv).then_inc(x_loaded, 16)
            sp.dma_start(rows_i, src_rows).then_inc(edges_loaded, 16)
            for to, frm in ((src_i, src), (dst_i, dst), (typ_i, etype), (wgt, weight)):
                sp.dma_start(to[:], frm).then_inc(edges_loaded, 16)
            sp.dma_start(unit[:].rearrange("p t c -> p (t c)"), vec).then_inc(edges_loaded, 16)
            for to, frm in ((net_sb[:], net_w), (types_sb[:], types_w), (ih_sb[:], ih_w), (hh_sb[:], hh_w),
                            (gate_b[:, 0], ih_b), (gate_b[:, 1], hh_b),
                            (w1_sb[:, 0], w1[0]), (w1_sb[:, 1], w1[1]), (w2_sb[:, 0], w2[0]), (w2_sb[:, 1], w2[1]),
                            (by_type_sb[:], by_type)):
                sp.dma_start(to, frm).then_inc(consts_loaded, 16)
            at = 0
            for v, n in ((gs0, NS), (gv0, NV), (bs0, NS), (gs1, NS), (bs1, NS)):
                sp.dma_start(norms[:, at:at + n], v.partition_broadcast(NP)).then_inc(consts_loaded, 16)
                at += n

            def table_out(p):
                if p == "gru":
                    rows = table[p].rearrange("(c p r) m -> c p (r m)", c=NC, p=NP)
                    for k in range(2):
                        sp.wait_ge(step, before("net", f"types {k} out") + 1)
                        sp.dma_start(rows[2 * k].rearrange("p (a f) -> p a f", a=2), typed[:, 0:2]).then_inc(tabled[p], 16)
                        sp.dma_start(rows[2 * k + 1].rearrange("p (a f) -> p a f", a=2), typed[:, 2:4]).then_inc(tabled[p], 16)
                else:
                    prev = STAGES[STAGES.index(p) - 1]
                    sp.wait_ge(step, ended(prev))
                    rows = table[p].rearrange("(c p h) f -> p c (h f)", c=NC, p=NP)
                    frm = t1 if p == "conv1" else hs
                    sp.dma_start(rows, frm[:].rearrange("p (c h) f -> p c (h f)", c=NC)).then_inc(tabled[p], 16)

            sp.wait_ge(edges_loaded, 16 * 6)
            sp.wait_ge(setup, 1)
            for k, p in enumerate(PHASES):

                def load(n, u, m, look=True, p=p):
                    cols = bass.ds(n * TG, TG)
                    first = isinstance(n, int) and n < 2
                    ecols = bass.ds(n * (TG * 128), TG * 128)
                    if p == "net":
                        if not first:
                            sp.wait_ge(weights, n * NPAIR + (base_conv[p] - NPAIR))
                            sp.sem_inc(slot_free, 1)
                        sp.dma_start(ea[0:D, u], ea16[:, ecols]).then_inc(ea_in[u], 16)
                    if p in ("conv0", "conv1"):
                        if not first:
                            sp.wait_ge(hid_mm, n * NH + (base_hid[p] - NH))
                            sp.sem_inc(slot_free, 1)
                        for h in range(2):
                            sp.dma_start(ea[64 * h:64 * h + DA, u, 0:HT * 128],
                                         ea48[:, bass.ds(n * (TG * 128) + h * HT * 128, HT * 128)]
                                         ).then_inc(ea_in[u], 16)
                    if not first:
                        sp.wait_ge(gathered[p][u], m * gather_count[p])
                        sp.sem_inc(slot_free, 1)
                    which = typ_i if p == "gru" else dst_i
                    sp.dma_start(idx_a[:, u], which[:, cols]).then_inc(idx_in[u], 16)
                    if p == "react":
                        sp.dma_start(idx_b[:, u], src_i[:, bass.ds(n * TG + LT, TG - LT)]).then_inc(idx_in[u], 16)
                    if p in scal_count:
                        if not first:
                            sp.wait_ge(formed, n * FORM[p] + (base_form[p] - FORM[p]))
                            sp.sem_inc(slot_free, 1)
                        if p == "gru":
                            sp.dma_start(scal[:, u, 0:LG], typ_f[:, bass.ds(n * TG + LOOK_FROM[p], LG)]
                                         ).then_inc(scal_in[u], 16)
                        elif p == "react":
                            sp.dma_start(scal[:, u, 0:TG], wgt[:, cols]).then_inc(scal_in[u], 16)
                        else:
                            sp.dma_start(scal[:, u].rearrange("p (t c) -> p t c", c=3),
                                         unit[:, cols, :]).then_inc(scal_in[u], 16)
                    if not (isinstance(n, int) and n == 0):
                        load_key(n - 1, 1 - u)
                    if p == "net" and not (isinstance(n, int) and n < 3):
                        keep_masks(n - 3, 1 - u)
                    if p in LOOK and look:
                        look_ahead(n, u)

                def look_ahead(n, u, p=p):
                    sp.wait_ge(turned_lo, n + (base_turn[p] + 1))
                    sp.sem_inc(slot_free, 1)
                    lo_load(n + 2, u)
                    sp.wait_ge(picked, n * NL[p] + (base_look[p] + NL[p]))
                    sp.sem_inc(slot_free, 1)
                    hi_load(n + 2, u)

                def load_key(n, u, p=p):
                    if p == "net" and isinstance(n, int) and n == 0:
                        sp.wait_ge(setup, N_SETUP)
                        sp.dma_start(lo_rows, rows_lo).then_inc(rows_keys, 16)
                        sp.dma_start(hi_rows, rows_hi).then_inc(rows_keys, 16)
                        sp.wait_ge(rows_keys, 32)
                    if not (isinstance(n, int) and n < 2):
                        sp.wait_ge(summed, n * NPAIR + (base_pair[p] - NPAIR))
                        sp.sem_inc(slot_free, 1)
                    sp.dma_start(key[:, u], key_of[p][:, bass.ds(n * TG, TG), :]).then_inc(key_in[u], 16)
                    if p == "conv1":
                        sp.dma_start(group_masks[:, u], masks_kept[:, bass.ds(n * (TG * 128), TG * 128)]
                                     ).then_inc(mask_in[u], 16)

                def keep_masks(n, u):
                    sp.wait_ge(masked, n * NPAIR + NPAIR)
                    sp.sem_inc(slot_free, 1)
                    sp.dma_start(masks_kept[:, bass.ds(n * (TG * 128), TG * 128)], group_masks[:, u]
                                 ).then_inc(mask_out[u], 16)

                def lo_load(n, u, p=p):
                    w = LOOK[p][-1] * 128
                    sp.dma_start(lo_t[:, u, 0:w], lo_rows.rearrange("q t -> (q t)")[
                        bass.ds(n * (TG * 128) + LOOK_FROM[p] * 128, w)].partition_broadcast(128)).then_inc(lo_in[u], 16)

                def hi_load(n, u, p=p):
                    w = LOOK[p][-1] * 128
                    sp.dma_start(hi_t[:, u, 0:w], hi_rows.rearrange("q t -> (q t)")[
                        bass.ds(n * (TG * 128) + LOOK_FROM[p] * 128, w)].partition_broadcast(128)).then_inc(hi_in[u], 16)

                if k:
                    sp.wait_ge(acc_done, k)
                if p == "conv0":
                    sp.wait_ge(ones_row, 1)
                load(0, 0, 0, look=False)
                if p != "net":
                    load(1, 1, 0, look=False)
                if p == "gru":
                    for n in range(2):
                        sp.wait_ge(mask_out[n], NG // 2 * 16)
                        lo_load(n, n)
                if p in LOOK:
                    for n in range(2):
                        hi_load(n, n)
                if p == "gru":
                    sp.wait_ge(step, before("net", "h turned"))
                    sp.dma_start(table["react"].rearrange("(c p h) f -> p c (h f)", c=NC, p=NP),
                                 hs[:].rearrange("p (c h) f -> p c (h f)", c=NC)).then_inc(h_out, 16)
                    sp.wait_ge(h_out, 16)
                else:
                    table_out(p)
                if p == "net":
                    load(1, 1, 0)
                if p == "react":
                    sp.wait_ge(tabled[p], 16)
                    sp.wait_ge(h_split, 7)
                if p in LOOK:
                    by_lo = table["react"].rearrange("(l h) f -> l (h f)", h=8)
                    sp.dma_start(h_by_lo[:, 0:LC * 128].rearrange("p (c f) -> p c f", c=LC),
                                 by_lo[0:LC * 128].rearrange("(c p) f -> p c f", c=LC)).then_inc(h_in, 16)
                    for s in range(3):
                        sp.dma_start(h_by_lo[32 * s:32 * s + LREST, LC * 128:], by_lo[LC * 128:]).then_inc(h_in, 16)
                if p == "gru":
                    table_out(p)
                if p in LOOK:
                    for n in range(2):
                        look_ahead(n, n)
                group_loop(sp, load, NG - 2, first=4, done=2)
                load(NG - 2, 0, NG // 2 - 1, look=False)
                load(NG - 1, 1, NG // 2 - 1, look=False)
                load_key(NG - 1, 1)
                if p == "net":
                    for n in range(NG - 3, NG):
                        keep_masks(n, n % 2)
                if p == "gru":
                    sp.wait_ge(turned_lo, NG)
                    for n in range(2):
                        lo_load(n, n, "react")
            sp.wait_ge(step, ended("conv1"))
            sp.dma_start(out.rearrange("(c p h) f -> p c (h f)", c=NC, p=NP),
                         xs[:].rearrange("p (c h) f -> p c (h f)", c=NC)).then_inc(stored, 16)
            sp.wait_ge(stored, 16)

        @block.gpsimd
        def _(pool):
            g = nc.gpsimd
            g.iota(lo_vals[:], [[1, 2 * LO]], base=0, channel_multiplier=0,
                   allow_small_or_imprecise_dtypes=True).then_inc(pool_consts, 1)
            g.iota(hi_vals8[:], [[1, 8], [0, D]], base=0, channel_multiplier=0,
                   allow_small_or_imprecise_dtypes=True).then_inc(pool_consts, 1)
            g.iota(hi_vals4[:], [[1, 4], [0, FA]], base=0, channel_multiplier=0,
                   allow_small_or_imprecise_dtypes=True).then_inc(pool_consts, 1)
            g.iota(part_i[:, 0:1], [[0, 1]], base=0, channel_multiplier=1).then_inc(pool_consts, 1)
            g.iota(part_lo[:, 0:LC], [[128, LC]], base=0, channel_multiplier=1,
                   allow_small_or_imprecise_dtypes=True).then_inc(pool_consts, 1)
            g.iota(type_vals[:], [[0, D], [1, NTYPE]], base=0, channel_multiplier=0,
                   allow_small_or_imprecise_dtypes=True).then_inc(pool_consts, 1)
            g.memset(ones[:], 1.0).then_inc(pool_consts, 1)
            pool.wait_ge(pool_consts, 7)
            g.affine_select(out=ident[:], in_=ones[:], compare_op=ALU.is_equal, fill=0.0, base=0,
                            pattern=[[-1, 128]], channel_multiplier=1).then_inc(pool_consts, 1)
            g.affine_select(out=mask[:].rearrange("p (c h) -> p c h", c=NC),
                            in_=ones[0:NP, 0:NC * 8].rearrange("p (c h) -> p c h", c=NC),
                            compare_op=ALU.is_ge, fill=0.0, base=N - 1,
                            pattern=[[-8 * NP, NC], [-1, 8]], channel_multiplier=-8).then_inc(pool_consts, 1)

            for p in PHASES:
                pool.wait_ge(tabled[p], 64 if p == "gru" else 16)

                def gather(n, u, m, p=p):
                    pool.wait_ge(idx_in[u], m * idx_count[p] + (base_idx[p] + idx_count[p]))
                    if not (isinstance(n, int) and n < 2):
                        if p in CONVS:
                            pool.wait_ge(mult, n * NPAIR + (base_conv[p] - NPAIR))
                        elif p == "react":
                            pool.wait_ge(formed, n * FORM[p] + (base_form[p] - FORM[p]))
                        else:
                            pool.wait_ge(split, n * 4 + (base_split[p] - 4 - 2))
                    pool.sem_inc(rows_free, 1)
                    for t in range(TG - LG if p == "gru" else TG):
                        g.indirect_dma_start(out=rows_a[:, u, t, 0:GCOLS[p]], out_offset=None, in_=table[p],
                                             in_offset=bass.IndirectOffsetOnAxis(ap=idx_a[:, u, t:t + 1], axis=0)
                                             ).then_inc(gathered[p][u], 16)
                    if p == "react":
                        for t in range(TG - LT):
                            g.indirect_dma_start(out=rows_b[:, u, t], out_offset=None, in_=table[p],
                                                 in_offset=bass.IndirectOffsetOnAxis(ap=idx_b[:, u, t:t + 1], axis=0)
                                                 ).then_inc(gathered[p][u], 16)

                group_loop(pool, gather)

        @block.scalar
        def _(act):
            a = nc.scalar

            def at(stage, name):
                act.wait_ge(step, before(stage, name))

            def std(stage):
                at(stage, "std")
                a.activation(st[:, 2], st[:, 1], ACT.Sqrt, bias=eps[0:NP, 0:1], scale=1.0 / D).then_inc(step, 1)

            std("start")
            act.wait_ge(setup, N_SQUARED)
            a.activation(len_b[:], len_a[:], ACT.Sqrt, bias=eps[:, 1:2]).then_inc(lens, 1)

            act.wait_ge(pool_consts, 9)
            for p in PHASES:
                def relu(n, u, c, p=p):
                    if c == 0 and not (isinstance(n, int) and n < 2):
                        act.wait_ge(weights, n * NPAIR + (base_conv[p] - NPAIR))
                    act.wait_ge(hid_mm, n * NH + (base_hid[p] + c + 1))
                    a.activation(hid[:, u, c * HC:(c + 1) * HC], hidden[:, c % 2, 0:HC],
                                 ACT.Relu).then_inc(hid_relu, 1)

                def act_tiles(u, j, p=p):
                    q = 2 * ((u + j) % 2)
                    if p == "conv0":
                        return [(2 * j + 1, away[:, q:q + 2].rearrange("p a b -> p (a b)")[:, 0:2 * LO], 2 * LO)]
                    return [(t, away[:, q + t % 2, 0:LO], LO) for t in (2 * j, 2 * j + 1) if t not in DVE_LO.get(p, ())]

                def distance(n, u, j, p=p):
                    if not (isinstance(n, int) and n == 0 and j < 2):
                        act.wait_ge(lo_ready, n * NPAIR + (base_pair[p] + j - 1))
                    for t, to, lo_n in act_tiles(u, j):
                        i = a.activation(to, lo_vals[:, 0:lo_n], ACT.Abs, bias=key[:, u, t, 0:1], scale=-1.0)
                    i.then_inc(apart, 1)

                def nearest(n, u, j, p=p):
                    act.wait_ge(apart, n * NPAIR + (base_pair[p] + j + 1))
                    if not (isinstance(n, int) and n == 0):
                        act.wait_ge(summed, n * NPAIR + (base_pair[p] + j + 1 - NPAIR))
                    for t, to, lo_n in act_tiles(u, j):
                        i = a.activation(onehot[:, t, 0:lo_n], to, ACT.Relu, bias=ones[:, 0:1], scale=-1.0)
                    i.then_inc(lo_ready, 1)

                def body(n, u, m, ahead=True, p=p):
                    old = not (isinstance(n, int) and n == 0)
                    if old:
                        act.wait_ge(key_in[1 - u], (m - 1 + u) * 16 + (base_key[p] + 16))
                        distance(n - 1, 1 - u, 0)
                    for j in range(NPAIR):
                        if old:
                            if j + 1 < NPAIR:
                                distance(n - 1, 1 - u, j + 1)
                            nearest(n - 1, 1 - u, j)
                        if p in CONVS[1:] and ahead and j < NH:
                            relu(n + 1, 1 - u, j)

                if p in CONVS[1:]:
                    for c in range(NH):
                        relu(0, 0, c)
                if p == "gru":
                    at(p, "gates hid out")
                    act.wait_ge(tabled["gru"], 64)
                    a.activation(gh.rearrange("p (c h) f -> p c (h f)", c=NC), wide[0:NP, :, 0:384],
                                 ACT.Copy).then_inc(step, 1)
                group_loop(act, body, NG - 2)
                body(NG - 2, 0, NG // 2 - 1)
                body(NG - 1, 1, NG // 2 - 1, ahead=False)
                body(NG, 0, NG // 2, ahead=False)
                at(p, "sums")
                act.wait_ge(acc_done, PHASES.index(p) + 1)
                if p == "conv0":
                    a.activation(sums[0:4 * FA, 0:2 * LO].rearrange("p (a b) -> p a b", a=2), acc[0:4 * FA, :, 0:LO],
                                 ACT.Copy).then_inc(step, 1)
                    at(p, "std")
                    a.activation(bn[:, 5], bn[:, 4], ACT.Sqrt, bias=eps[0:NP, 0:1]).then_inc(step, 1)
                else:
                    a.activation(sums[:, 0:LO + 1], acc[:, 0, 0:LO + 1], ACT.Copy).then_inc(step, 1)
                if p == "net":
                    std(p)
                    at(p, "h cols")
                    a.activation(hcols[:], hidden[:, 0, 0:NC * NP], ACT.Copy).then_inc(step, 1)
                    at(p, "types 0 out")
                    a.activation(typed, wide[0:NP], ACT.Copy).then_inc(step, 1)
                    at(p, "types 1 out")
                    act.wait_ge(tabled["gru"], 32)
                    a.activation(typed, wide[0:NP], ACT.Copy).then_inc(step, 1)
                if p == "gru":
                    at(p, "sigmoid")
                    a.activation(t0[:], t0[:], ACT.Sigmoid).then_inc(step, 1)
                    at(p, "tanh")
                    a.activation(t1[:, :, 0:D], t1[:, :, 0:D], ACT.Tanh).then_inc(step, 1)
                if p in ("gru", "react"):
                    std(p)
                if p == "conv1":
                    at(p, "std")
                    a.activation(bn[:, 5, 0:NS], bn[:, 4, 0:NS], ACT.Sqrt, bias=eps[0:NP, 0:1]).then_inc(step, 1)

        @block.tensor
        def _(pe):
            m = nc.tensor

            def at(stage, name):
                pe.wait_ge(step, before(stage, name))

            pe.wait_ge(pool_consts, 9)
            pe.wait_ge(setup, N_SETUP)
            pe.wait_ge(consts_loaded, 16 * N_CONST)
            for k, p in enumerate(PHASES):
                H, F = HI[p], SUMF[p]
                NB = 2 if p == "conv0" else 1
                W = {"net": (net_sb[:],) * 2, "conv0": (w2_sb[:, 0, 0], w2_sb[:, 0, 1]),
                     "conv1": (w2_sb[:, 1, 0], w2_sb[:, 1, 1])}.get(p)
                nw = IN[p] * OUTF[p] if p in CONVS else 0
                pe.wait_ge(step, ended(STAGES[k]))
                for b in range(NB):
                    m.matmul(acc[0:H * F, b, 0:LO + 1], zeros[:, 0:H * F], zeros[:], start=True, stop=False)

                def gates_of(name, frm, w, k2):
                    at("gru", name)
                    for c in range(NC):
                        m.matmul(wide[0:NP, c, 0:384], frm[:, c * NP:(c + 1) * NP], w[:], start=True, stop=False)
                        mm = m.matmul(wide[0:NP, c, 0:384], ones[0:1, 0:NP], gate_b[:, k2], start=False, stop=True)
                    mm.then_inc(step, 1)

                if p == "gru":
                    gates_of("gates hid", hcols, hh_sb, 1)

                def hid_chunk(n, u, c, mth, p=p):
                    if c == 0:
                        pe.wait_ge(ea_in[u], mth * ea_count[p] + (base_ea[p] + ea_count[p]))
                    if not (isinstance(n, int) and n == 0 and c < 2):
                        pe.wait_ge(hid_relu, n * NH + (base_hid[p] + c - 1))
                    m.matmul(hidden[:, c % 2, 0:HC], w1_sb[:, CONVS.index(p) - 1],
                             ea[:, u, c * HC:(c + 1) * HC], start=True, stop=True).then_inc(hid_mm, 1)

                def conv_pair(n, u, j, mth, p=p, W=W, nw=nw):
                    if p == "net":
                        if j == 0:
                            pe.wait_ge(ea_in[u], mth * 16 + (base_ea[p] + 16))
                        lhs = ea
                    else:
                        lhs = hid
                        c = max((t % HT * 128 + 127) // HC for t in (2 * j, 2 * j + 1))
                        pe.wait_ge(hid_relu, n * NH + (base_hid[p] + c + 1))
                    if not (isinstance(n, int) and n == 0 and j < 2):
                        pe.wait_ge(mult, n * NPAIR + (base_conv[p] + j - 1))
                    for s in range(2):
                        t = 2 * j + s
                        col = (t if p == "net" else t % HT) * 128
                        mm = m.matmul(wide[:, 2 * ((u + j) % 2) + s, 0:nw], lhs[:, u, col:col + 128], W[t // HT],
                                      start=True, stop=True)
                    mm.then_inc(weights, 1)

                def sum_pair(n, j, p=p, H=H, F=F, NB=NB):
                    pe.wait_ge(spreadd, n * NPAIR + (base_pair[p] + j + 1))
                    pe.wait_ge(lo_ready, n * NPAIR + (base_pair[p] + j + 1))
                    for t in (2 * j, 2 * j + 1):
                        for s in range(3):
                            for b in range(NB):
                                mm = m.matmul(acc[0:H * F, b, 0:LO], spread[:, (3 * t + s) * H * F:(3 * t + s + 1) * H * F],
                                              onehot[:, t, b * LO:(b + 1) * LO], start=False, stop=False)
                    mm.then_inc(summed, 1)

                def look_up(n, u, b, p=p):
                    if b == 0:
                        pe.wait_ge(turned_lo, n + (base_turn[p] + 1))
                    if not (isinstance(n, int) and n * NL[p] + b < 2):
                        pe.wait_ge(picked, n * NL[p] + (base_look[p] + b - 1))
                    c0, c1 = LOOK[p][b] * 128, LOOK[p][b + 1] * 128
                    bank = (u * NL[p] + b) % 2
                    for s in range(3):
                        for c in range(LC):
                            m.matmul(hidden[:, bank, 0:c1 - c0], h_parts[:, s, c * 128:(c + 1) * 128],
                                     onehot_t[u][:, c, c0:c1], start=(s == 0 and c == 0), stop=False)
                    mm = m.matmul(hidden[:, bank, 0:c1 - c0], h_rest[:], onehot_t[u][:, LC, c0:c1], start=False,
                                  stop=True)
                    mm.then_inc(looked, 1)

                def choose_rows(n, u, b, p=p):
                    pe.wait_ge(picked, n * NL[p] + (base_look[p] + b + 1))
                    if b == 0 and not (isinstance(n, int) and n < 2):
                        pe.wait_ge(formed, n * FORM[p] + (base_form[p] - FORM[p]))
                    right = by_type_sb if p == "gru" else choose
                    w = D * NTYPE if p == "gru" else D
                    for t in range(LOOK[p][b], LOOK[p][b + 1]):
                        c = (t - LOOK[p][b]) * 128
                        mm = m.matmul(wide[:, u, t * w:(t + 1) * w], picked_rows[:, (u * NL[p] + b) % 2, c:c + 128],
                                      right[:], start=True, stop=True)
                    mm.then_inc(chosen, 1)

                def body(n, u, mth, new=True, ahead=True, p=p):
                    for j in range(NPAIR):
                        if p in CONVS[1:] and ahead and j < NH:
                            hid_chunk(n + 1, 1 - u, j, mth + u)
                        if p in CONVS and new and j + 2 < NPAIR:
                            conv_pair(n, u, j + 2, mth)
                        if p in CONVS and ahead and j + 2 >= NPAIR:
                            conv_pair(n + 1, 1 - u, j + 2 - NPAIR, mth + u)
                        if p == "react":
                            if j == 0 and new:
                                choose_rows(n, u, NL[p] - 1)
                            if j in (3, 4, 6) and ahead:
                                choose_rows(n + 1, 1 - u, {3: 0, 4: 1, 6: 2}[j])
                            if j in (0, 1, 3, 4) and ahead:
                                look_up(n + 1, 1 - u, {0: 0, 1: 1, 3: 2, 4: 3}[j])
                        if p == "gru" and ahead:
                            if j == 0:
                                look_up(n + 1, 1 - u, 0)
                            if j == 5:
                                choose_rows(n + 1, 1 - u, 0)
                        if not (isinstance(n, int) and n == 0):
                            sum_pair(n - 1, j)

                if p in CONVS[1:]:
                    for c in range(NH):
                        hid_chunk(0, 0, c, 0)
                if p in CONVS:
                    conv_pair(0, 0, 0, 0)
                    conv_pair(0, 0, 1, 0)
                if p in LOOK:
                    pe.wait_ge(h_split, 7 if p == "gru" else 14)
                    if p == "gru":
                        at(p, "sums")
                    for b in range(NL[p]):
                        look_up(0, 0, b)
                        if p == "gru" or b < NL[p] - 1:
                            choose_rows(0, 0, b)
                group_loop(pe, body, NG - 2)
                body(NG - 2, 0, NG // 2 - 1)
                body(NG - 1, 1, NG // 2 - 1, ahead=False)
                body(NG, 0, NG // 2, new=False, ahead=False)
                for b in range(NB):
                    mm = m.matmul(acc[0:H * F, b, 0:LO + 1], zeros[:, 0:H * F], zeros[:], start=False, stop=True)
                mm.then_inc(acc_done, 1)

                if p in ("net", "react", "conv1"):
                    at(p, "turned")
                    for c in range(NC):
                        mm = m.transpose(wide[0:NP, 0, c * 128:(c + 1) * 128], sums[:, c * NP:(c + 1) * NP], ident[:])
                    mm.then_inc(step, 1)
                if p == "net":
                    at(p, "h turned")
                    for c in range(NC):
                        mm = m.transpose(hidden[:, 0, c * NP:(c + 1) * NP],
                                         hs[:, 8 * c:8 * c + 8].rearrange("p h f -> p (h f)"), ident[0:NP, 0:NP])
                    mm.then_inc(step, 1)
                    for k2 in range(2):
                        at(p, f"types {k2}")
                        for q in range(4):
                            c = 2 * k2 + q // 2
                            mm = m.matmul(wide[0:NP, q, :], hcols[:, c * NP:(c + 1) * NP],
                                          types_sb[:, (q % 2) * 512:(q % 2 + 1) * 512], start=True, stop=True)
                        mm.then_inc(step, 1)
                if p == "gru":
                    gates_of("gates in", sums, ih_sb, 0)
                if p == "conv0":
                    at(p, "turned")
                    for q in range(8):
                        c, b = q // 2, q % 2
                        mm = m.transpose(wide[0:NP, q // 4, (q % 4) * 4 * FA:(q % 4 + 1) * 4 * FA],
                                         sums[0:4 * FA, bass.ds(2 * c * NP + b, NP, step=2)], ident[0:4 * FA, 0:4 * FA])
                    mm.then_inc(step, 1)
                if p in ("conv0", "conv1"):
                    at(p, "all s")
                    m.matmul(hidden[0:NP, 0, 0:NS], ones[0:NP, 0:NP], bn[:, 0, 0:NS], start=True, stop=True).then_inc(step, 1)
                    at(p, "all sq")
                    w = NS + NV if p == "conv0" else NS
                    m.matmul(hidden[0:NP, 1, 0:w], ones[0:NP, 0:NP], bn[:, 2, 0:w], start=True, stop=True).then_inc(step, 1)

        @block.vector
        def _(dve):
            v = nc.vector

            def at(stage, name):
                dve.wait_ge(step, before(stage, name))

            n_set = [0]

            def then(ins):
                n_set[0] += 1
                ins.then_inc(setup, 1)
                dve.wait_ge(setup, n_set[0])

            def norm(stage):
                at(stage, "mean")
                v.tensor_reduce(st[:, 0], xs[:], AX.X, ALU.add).then_inc(step, 1)
                at(stage, "scale")
                v.tensor_scalar(st[:, 3], st[:, 0], 1.0 / D, None, ALU.mult).then_inc(step, 1)
                at(stage, "center")
                v.tensor_tensor(t0[:, :, 0:D], xs[:], bc(st[:, 3], [1, NC * 8], [0, D]), ALU.subtract).then_inc(step, 1)
                at(stage, "square")
                v.tensor_tensor(t1[:, :, 0:D], t0[:, :, 0:D], t0[:, :, 0:D], ALU.mult).then_inc(step, 1)
                at(stage, "var")
                v.tensor_reduce(st[:, 1], t1[:, :, 0:D], AX.X, ALU.add).then_inc(step, 1)
                at(stage, "rstd")
                v.reciprocal(st[:, 4], st[:, 2]).then_inc(step, 1)
                at(stage, "norm")
                v.tensor_tensor(t1[:, :, 0:D], t0[:, :, 0:D], bc(st[:, 4], [1, NC * 8], [0, D]), ALU.mult).then_inc(step, 1)
                at(stage, "relu")
                v.tensor_scalar(hs[:], t1[:, :, 0:D], 0.0, None, ALU.max).then_inc(step, 1)

            v.memset(eps[:, 1:2], 0.0)
            v.memset(zeros[:], 0.0)
            v.memset(sums[:], 0.0)
            v.memset(t1[:], 0.0)
            v.memset(ea[:], 1.0)
            v.memset(msg[:], 1.0)
            then(v.memset(eps[:, 0:1], EPS))
            dve.wait_ge(x_loaded, 16)
            norm("start")
            dve.wait_ge(edges_loaded, 16 * 6)
            then(v.tensor_scalar(rows_bits, rows_i, 3, None, ALU.arith_shift_right))
            then(v.tensor_copy(rows_lo, rows_bits))
            then(v.tensor_scalar(rows_bits, rows_i, 7, None, ALU.bitwise_and))
            then(v.tensor_copy(rows_hi, rows_bits))
            dve.wait_ge(pool_consts, 9)
            then(v.tensor_scalar(part_i[:, 1:2], part_i[:, 0:1], 4, None, ALU.arith_shift_right))
            then(v.tensor_copy(part_hi[:], part_i[:, 1:2]))
            then(v.tensor_scalar(part_i[:, 1:2], part_i[:, 0:1], 31, None, ALU.bitwise_and))
            then(v.tensor_copy(part_lo[:, LC:], part_i[:, 1:2]))
            then(v.tensor_scalar(part_lo[:, LC:], part_lo[:, LC:], 128.0 * LC, None, ALU.add))
            assert n_set[0] == N_ROWS
            then(v.tensor_reduce(choose[:], bc(ident[:, 0:1], [1, D], [D, 8]), AX.X, ALU.add))
            for idx, keys, shift in ((src_i, key_src8, 3), (src_i, key_src4, 2), (dst_i, key_dst8, 3)):
                then(v.tensor_scalar(bits[:], idx[:], shift, None, ALU.arith_shift_right))
                then(v.tensor_copy(keys[:, :, 0], bits[:]))
                then(v.tensor_scalar(bits[:], idx[:], (1 << shift) - 1, None, ALU.bitwise_and))
                then(v.tensor_copy(keys[:, :, 1], bits[:]))
            then(v.tensor_copy(typ_f, typ_i[:]))
            then(v.scalar_tensor_tensor(out=typ_i[:], in0=src_i[:], scalar=float(NTYPE), in1=typ_i[:],
                                        op0=ALU.mult, op1=ALU.add))
            then(v.tensor_tensor(len_b[:], unit[:, :, 1], unit[:, :, 1], ALU.mult))
            then(v.tensor_tensor(len_a[:], unit[:, :, 0], unit[:, :, 0], ALU.mult))
            then(v.tensor_tensor(len_a[:], len_a[:], len_b[:], ALU.add))
            then(v.tensor_tensor(len_b[:], unit[:, :, 2], unit[:, :, 2], ALU.mult))
            then(v.tensor_tensor(len_a[:], len_a[:], len_b[:], ALU.add))
            assert n_set[0] == N_SQUARED
            dve.wait_ge(lens, 1)
            then(v.tensor_scalar(len_a[:], len_b[:], 1e-12, None, ALU.add))
            then(v.reciprocal(len_b[:], len_a[:]))
            then(v.tensor_tensor(unit[:], unit[:], bc(len_b[:], [1, T], [0, 3]), ALU.mult))
            then(v.memset(h_by_lo, 0.0))
            assert n_set[0] == N_SETUP
            dve.wait_ge(consts_loaded, 16 * N_CONST)

            for k, p in enumerate(PHASES):
                H, F = HI[p], SUMF[p]
                I, O = IN.get(p), OUTF.get(p)
                lo_n = 2 * LO if p == "conv0" else LO
                hi_vals = hi_vals4 if p == "conv0" else hi_vals8
                first_in = 12 if p == "conv1" else 0

                def form(n, u, m, k, p=p):
                    if k:
                        dve.wait_ge(formed, n * FORM[p] + (base_form[p] + k))
                    elif p != "conv0":
                        dve.wait_ge(scal_in[u], m * 16 + (base_scal[p] + 16))
                        if p in LOOK:
                            dve.wait_ge(chosen, n * NL[p] + (base_look[p] + NL[p]))
                        if p != "gru":
                            dve.wait_ge(gathered[p][u], m * gather_count[p] + gather_count[p])
                    if p == "gru":
                        if k == 0:
                            for t in range(LG):
                                i = v.scalar_tensor_tensor(
                                    out=by_type_masked[:, t], in0=type_vals[:], scalar=scal[:, u, t:t + 1],
                                    in1=wide[:, u, t * D * NTYPE:(t + 1) * D * NTYPE].rearrange("p (m k) -> p m k", m=D),
                                    op0=ALU.is_equal, op1=ALU.mult)
                        if k == 1:
                            i = v.tensor_reduce(rows_a[:, u, LOOK_FROM[p]:TG, 0:D], by_type_masked, AX.X, ALU.add)
                    if p == "react":
                        xj = rows_a[:, u, :, 0:D]
                        wg = scal[:, u, 0:TG]
                        three = lambda ap: ap.rearrange("p (t f) -> p t f", f=D)
                        by_source = ((slice(0, LT), three(wide[:, u, 0:LT * D])), (slice(LT, TG), rows_b[:, u]))
                        if k == 0:
                            for ts, xi in by_source:
                                i = v.tensor_tensor(three(ra)[:, ts], xi, xj[:, ts], ALU.mult)
                        if k == 1:
                            i = v.tensor_tensor(three(ra), three(ra), bc(wg, [1, TG], [0, D]), ALU.mult)
                        if k == 2:
                            i = v.tensor_scalar(three(rb[:]), xj, KH, KD, ALU.mult, ALU.add)
                        if k == 3:
                            for ts, xi in by_source:
                                i = v.scalar_tensor_tensor(out=three(rb[:])[:, ts], in0=xi, scalar=KE,
                                                           in1=three(rb[:])[:, ts], op0=ALU.mult, op1=ALU.add)
                        if k == 4:
                            i = v.reciprocal(rb[:], rb[:])
                        if k == 5:
                            i = v.tensor_tensor(msg[:, :, 0:D], three(ra), three(rb[:]), ALU.mult)
                    if p == "conv0":
                        t0_, t1_ = HALVES[p][k]
                        if k == 0:
                            dve.wait_ge(scal_in[u], m * 16 + (base_scal[p] + 16))
                        dve.wait_ge(reduced, n * NPAIR + (base_conv[p] + t1_ // 2))
                        i = v.tensor_tensor(msg[:, t0_:t1_, NV + NS:NV + NS + 12].rearrange("p t (j c) -> p t j c", c=3),
                                            bc(msg[:, t0_, 0:NV], [NV + FA, t1_ - t0_], [1, NV], [0, 3]),
                                            bc(scal[:, u, 3 * t0_:3 * t0_ + 1], [3, t1_ - t0_], [0, NV], [1, 3]), ALU.mult)
                    if p == "conv1":
                        vs = vsh[:].rearrange("p (t i c) -> p t i c", t=TG, c=3)
                        if k == 0:
                            i = v.tensor_tensor(vs, rows_a[:, u, :, 0:12].rearrange("p t (i c) -> p t i c", c=3),
                                                bc(scal[:, u], [3, TG], [0, NV], [1, 3]), ALU.mult)
                        if k == 1:
                            i = v.tensor_reduce(rows_a[:, u, :, 28:32], vs, AX.X, ALU.add)
                    i.then_inc(formed, 1)

                def multiply(n, u, m, j, p=p, I=I, O=O, first_in=first_in):
                    if j == 0:
                        dve.wait_ge(gathered[p][u], m * gather_count[p] + gather_count[p])
                        if p == "conv1":
                            dve.wait_ge(formed, n * FORM[p] + (base_form[p] + FORM[p]))
                    dve.wait_ge(weights, n * NPAIR + (base_conv[p] + j + 1))
                    if not (isinstance(n, int) and n == 0 and j < 2):
                        dve.wait_ge(reduced, n * NPAIR + (base_conv[p] + j - 1))
                    q = (u + j) % 2
                    v.tensor_tensor(prod[:, q, :, 0:I * O].rearrange("p s (o i) -> p s o i", i=I),
                                    wide[:, 2 * q:2 * q + 2, 0:I * O].rearrange("p s (o i) -> p s o i", i=I),
                                    bc(rows_a[:, u, 2 * j, first_in:first_in + I], [32, 2], [0, O], [1, I]),
                                    ALU.mult).then_inc(mult, 1)

                def reduce(n, u, j, p=p, I=I, O=O):
                    dve.wait_ge(mult, n * NPAIR + (base_conv[p] + j + 1))
                    q = (u + j) % 2
                    v.tensor_reduce(msg[:, 2 * j:2 * j + 2, 0:O],
                                    prod[:, q, :, 0:I * O].rearrange("p s (o i) -> p s o i", i=I),
                                    AX.X, ALU.add).then_inc(reduced, 1)

                def mask_of(u, t, p=p):
                    return group_masks[:, u, t * 128:(t + 1) * 128] if p in MASKS else himask[:, (2 * u + t) % 4]

                def masks(n, u, m, j, p=p, H=H, F=F, lo_n=lo_n, hi_vals=hi_vals, mask_of=mask_of):
                    if not (isinstance(n, int) and n == 0):
                        dve.wait_ge(summed, n * NPAIR + (base_pair[p] + j + 1 - NPAIR))
                    if p == "net" and j == 0 and not (isinstance(n, int) and n < 2):
                        dve.wait_ge(mask_out[u], m * 16)
                    if p != "conv1":
                        for t in (2 * j, 2 * j + 1):
                            hm = v.tensor_scalar(mask_of(u, t)[:, 0:H * F], hi_vals[:].rearrange("p h f -> p (h f)"),
                                                 key[:, u, t, 1:2], None, ALU.is_equal)
                        hm.then_inc(masked, 1)
                    for t in (2 * j, 2 * j + 1):
                        if t in DVE_LO.get(p, ()):
                            v.tensor_scalar(onehot[:, t, 0:lo_n], lo_vals[:, 0:lo_n], key[:, u, t, 0:1], None,
                                            ALU.is_equal)

                def spread_pair(n, u, m, j, p=p, H=H, F=F, mask_of=mask_of):
                    for h, (t0_, _) in enumerate(HALVES[p]):
                        if 2 * j == t0_:
                            dve.wait_ge(split, n * SPLIT[p] + (base_split[p] + 4 * h + 4))
                    if p != "conv1":
                        dve.wait_ge(masked, n * NPAIR + (base_pair[p] + j + 1))
                    elif j == 0:
                        dve.wait_ge(mask_in[u], m * 16 + 16)
                    if F == D:
                        t = 2 * j
                        mask_step = mask_of(u, 1).offset - mask_of(u, 0).offset
                        sp_ = v.tensor_tensor(bc(spread[:, t * 3 * H * F:t * 3 * H * F + 1], [H * F, 6], [F, H], [1, F]),
                                              bc(parts[:, u, t * 3 * F:t * 3 * F + 1], [F, 6], [0, H], [1, F]),
                                              bc(mask_of(u, t)[:, 0:1], [mask_step, 2], [0, 3], [1, H * F]), ALU.mult)
                    else:
                        for t in (2 * j, 2 * j + 1):
                            sp_ = v.tensor_tensor(bc(spread[:, t * 3 * H * F:t * 3 * H * F + 1], [H * F, 3], [F, H], [1, F]),
                                                  bc(parts[:, u, t * 3 * F:t * 3 * F + 1], [F, 3], [0, H], [1, F]),
                                                  bc(mask_of(u, t)[:, 0:1], [0, 3], [F, H], [1, F]), ALU.mult)
                    sp_.then_inc(spreadd, 1)

                def split_step(n, u, m, half, i, p=p, F=F):
                    t0_, t1_ = HALVES[p][half]
                    part = lambda k: parts[:, u, t0_ * 3 * F:t1_ * 3 * F].rearrange("p (t k f) -> p t k f", k=3, f=F)[:, :, k]
                    left = rest[:, 0:(t1_ - t0_) * F].rearrange("p (t f) -> p t f", f=F)
                    value = dict(gru=rows_a[:, u, t0_:t1_, 0:F], conv0=msg[:, t0_:t1_, NV:NV + FA]
                                 ).get(p, msg[:, t0_:t1_, 0:F])
                    if i:
                        dve.wait_ge(split, n * SPLIT[p] + (base_split[p] + 4 * half + i))
                    elif p == "gru":
                        dve.wait_ge(formed, n * FORM[p] + (base_form[p] + FORM[p]))
                        dve.wait_ge(gathered[p][u], m * gather_count[p] + gather_count[p])
                    elif p == "react":
                        dve.wait_ge(formed, n * FORM[p] + (base_form[p] + FORM[p]))
                    elif p == "conv0":
                        dve.wait_ge(formed, n * FORM[p] + (base_form[p] + half + 1))
                    else:
                        dve.wait_ge(reduced, n * NPAIR + (base_conv[p] + t1_ // 2))
                    if i == 0:
                        x_ = v.tensor_copy(part(0), value)
                    if i == 1:
                        x_ = v.tensor_tensor(left, value, part(0), ALU.subtract)
                    if i == 2:
                        x_ = v.tensor_copy(part(1), left)
                    if i == 3:
                        x_ = v.tensor_tensor(part(2), left, part(1), ALU.subtract)
                    x_.then_inc(split, 1)

                def turn_lo(n, u, loads, c, p=p):
                    if c == 0:
                        dve.wait_ge(lo_in[u], loads * 16 + (base_turn[p] * 8 + 16))
                        if p == "react" or not (isinstance(n, int) and n < 2):
                            dve.wait_ge(looked, base_look[p] if isinstance(n, int) and n < 2
                                        else n * NL[p] + (base_look[p] - NL[p]))
                    w = LOOK[p][-1] * 128
                    i = v.tensor_scalar(onehot_t[u][:, c, 0:w], lo_t[:, u, 0:w], part_lo[:, c:c + 1], None, ALU.is_equal)
                    if c == LC:
                        i.then_inc(turned_lo, 1)

                def pick(n, u, loads, b, p=p):
                    if b == 0:
                        dve.wait_ge(hi_in[u], loads * 16 + (base_turn[p] * 8 + 16))
                    dve.wait_ge(looked, n * NL[p] + (base_look[p] + b + 1))
                    if not (isinstance(n, int) and n * NL[p] + b < 2):
                        dve.wait_ge(chosen, n * NL[p] + (base_look[p] + b - 1))
                    c0, c1 = LOOK[p][b] * 128, LOOK[p][b + 1] * 128
                    bank = (u * NL[p] + b) % 2
                    v.scalar_tensor_tensor(out=picked_rows[:, bank, 0:c1 - c0], in0=hi_t[:, u, c0:c1],
                                           scalar=part_hi[:], in1=hidden[:, bank, 0:c1 - c0], op0=ALU.is_equal,
                                           op1=ALU.mult).then_inc(picked, 1)

                def body(n, u, m, new=True, ahead=True, two_ahead=True, p=p, form=form, multiply=multiply, reduce=reduce,
                         masks=masks, spread_pair=spread_pair, split_step=split_step):
                    old = not (isinstance(n, int) and n == 0)
                    m_old = m - 1 + u
                    if old:
                        dve.wait_ge(key_in[1 - u], m_old * 16 + (base_key[p] + 16))
                    if p == "conv1" and new:
                        form(n, u, m, 0)
                    for j in range(NPAIR):
                        if old:
                            masks(n - 1, 1 - u, m_old, j)
                        if p == "conv1" and new and j == 0:
                            form(n, u, m, 1)
                            if old:
                                spread_pair(n - 1, 1 - u, m_old, j)
                        if p in CONVS and new:
                            multiply(n, u, m, j)
                        if p == "react":
                            if j in (1, 3, 4) and new:
                                form(n, u, m, {1: 0, 3: 2, 4: 4}[j])
                            if j == 0 and two_ahead:
                                turn_lo(n + 2, u, m + 1, 0)
                            if j in (2, 3, 5) and ahead:
                                pick(n + 1, 1 - u, m + u, {2: 0, 3: 1, 5: 2}[j])
                            if j == 6 and ahead:
                                pick(n + 1, 1 - u, m + u, 3)
                            if j in (5, 6) and new:
                                split_step(n, u, m, 0, {5: 0, 6: 2}[j])
                        if old and not (p == "conv1" and new and j == 0):
                            spread_pair(n - 1, 1 - u, m_old, j)
                        if p == "react":
                            if j in (2, 3, 4) and new:
                                form(n, u, m, {2: 1, 3: 3, 4: 5}[j])
                            if j in (0, 1, 2) and two_ahead:
                                turn_lo(n + 2, u, m + 1, j + 1)
                            if j in (5, 6) and new:
                                split_step(n, u, m, 0, {5: 1, 6: 3}[j])
                        if p == "gru":
                            if j == 0 and two_ahead:
                                turn_lo(n + 2, u, m + 1, 0)
                                turn_lo(n + 2, u, m + 1, 1)
                            if j == 1 and two_ahead:
                                turn_lo(n + 2, u, m + 1, 2)
                                turn_lo(n + 2, u, m + 1, 3)
                            if j in (0, 1) and new:
                                form(n, u, m, j)
                            if j == 2 and ahead:
                                pick(n + 1, 1 - u, m + u, 0)
                            if j >= 3 and new:
                                split_step(n, u, m, 0, j - 3)
                        if p == "conv0":
                            if j == 0 and old:
                                form(n - 1, 1 - u, m_old, 1)
                            if j == 4 and new:
                                form(n, u, m, 0)
                        if p in CONVS:
                            if j == 6 and new:
                                split_step(n, u, m, 0, 2)
                            if new:
                                reduce(n, u, j)
                            if j < 4 and old:
                                split_step(n - 1, 1 - u, m_old, 1, j)
                            if j >= 4 and new:
                                split_step(n, u, m, 0, {4: 0, 5: 1, 6: 3}[j])

                if p in LOOK:
                    if p == "gru":
                        for n in range(2):
                            for c in range(LC + 1):
                                turn_lo(n, n, 0, c)
                    first = 0 if p == "gru" else 7

                    def h_step(k, ins):
                        ins.then_inc(h_split, 1)
                        dve.wait_ge(h_split, first + k + 1)

                    dve.wait_ge(h_in, 64 if p == "gru" else 128)
                    h_step(0, v.tensor_copy(h_parts[:, 0], h_by_lo))
                    h_step(1, v.tensor_tensor(h_left, h_by_lo, h_parts[:, 0], ALU.subtract))
                    h_step(2, v.tensor_copy(h_parts[:, 1], h_left))
                    h_step(3, v.tensor_tensor(h_parts[:, 2], h_left, h_parts[:, 1], ALU.subtract))
                    for s in range(3):
                        if s == 2:
                            rows_ = slice(64, 128)
                        else:
                            rows_ = slice(32 * s, 32 * s + 32)
                        h_step(4 + s, v.tensor_copy(h_rest[rows_], h_parts[rows_, s, LC * 128:]))
                    for b in range(NL[p]):
                        pick(0, 0, 0, b)
                group_loop(dve, body, NG - 2, first=4 if p == "net" else 2)
                body(NG - 2, 0, NG // 2 - 1, two_ahead=False)
                body(NG - 1, 1, NG // 2 - 1, ahead=False, two_ahead=False)
                body(NG, 0, NG // 2, new=False, ahead=False, two_ahead=False)
                if p == "gru":
                    for n in range(2):
                        for c in range(LC + 1):
                            turn_lo(n, n, 0, c, "react")

                if p == "react":
                    dve.wait_ge(looked, base_look[p] + NG * NL[p])
                    v.memset(ea[:, :, 0:HT * 128], 1.0).then_inc(ones_row, 1)

                turned = wide[0:NP, 0].rearrange("p (n f) -> p n f", f=D)
                T0, T1 = t0[:, :, 0:D], t1[:, :, 0:D]
                nodes = lambda ap: bc(ap, [1, NC * 8], [0, D])
                feats = lambda ap, w=NS: bc(ap, [0, NC * 8], [1, w])
                if p == "net":
                    at(p, "add")
                    v.tensor_tensor(xs[:], xs[:], turned, ALU.add).then_inc(step, 1)
                    norm(p)
                if p == "gru":
                    at(p, "rz")
                    gates_in = wide[0:NP, :, 0:384].rearrange("p c (h f) -> p c h f", h=8)
                    chunks = lambda ap: ap.rearrange("p (c h) f -> p c h f", c=NC)
                    v.tensor_tensor(chunks(t0[:]), gates_in[:, :, :, 0:32], chunks(gh[:, :, 0:32]), ALU.add).then_inc(step, 1)
                    at(p, "reset")
                    v.tensor_tensor(T1, T0, gh[:, :, 32:48], ALU.mult).then_inc(step, 1)
                    at(p, "new in")
                    v.tensor_tensor(chunks(T1), chunks(T1), gates_in[:, :, :, 32:48], ALU.add).then_inc(step, 1)
                    at(p, "diff")
                    v.tensor_tensor(gi[:, :, 0:16], hs[:], T1, ALU.subtract).then_inc(step, 1)
                    at(p, "update")
                    v.tensor_tensor(gi[:, :, 0:16], gi[:, :, 0:16], t0[:, :, 16:32], ALU.mult).then_inc(step, 1)
                    at(p, "blend")
                    v.tensor_tensor(T1, T1, gi[:, :, 0:16], ALU.add).then_inc(step, 1)
                    at(p, "add")
                    v.tensor_tensor(xs[:], xs[:], T1, ALU.add).then_inc(step, 1)
                    norm(p)
                if p == "react":
                    at(p, "f1")
                    v.tensor_scalar(T0, hs[:], -1.0 / KK, 1.0, ALU.mult, ALU.add).then_inc(step, 1)
                    at(p, "f2")
                    v.tensor_scalar(T1, hs[:], 1.0 / KC, -1.0, ALU.mult, ALU.add).then_inc(step, 1)
                    at(p, "f3")
                    v.tensor_tensor(T0, T0, hs[:], ALU.mult).then_inc(step, 1)
                    at(p, "f4")
                    v.tensor_tensor(T0, T0, T1, ALU.mult).then_inc(step, 1)
                    at(p, "f5")
                    v.tensor_tensor(xs[:], xs[:], T0, ALU.add).then_inc(step, 1)
                    at(p, "const")
                    v.tensor_scalar(xs[:], xs[:], KB, None, ALU.add).then_inc(step, 1)
                    at(p, "add")
                    v.tensor_tensor(xs[:], xs[:], turned, ALU.add).then_inc(step, 1)
                    norm(p)
                if p == "conv0":
                    S, V = oa[:, :, 0:NS], oa[:, :, NS:NS + 12]
                    at(p, "node major")
                    v.tensor_copy(oa[:].rearrange("p (b n) f -> p b (n f)", b=2),
                                  wide[0:NP, 0:2, 0:16 * FA]).then_inc(step, 1)
                    at(p, "count")
                    v.tensor_scalar(st[:, 0], oa[:, :, FA - 1], 1.0, None, ALU.max).then_inc(step, 1)
                    at(p, "inv count")
                    v.reciprocal(st[:, 5], st[:, 0]).then_inc(step, 1)
                    at(p, "quarter")
                    v.tensor_scalar(st[:, 1], st[:, 5], NS ** -0.5, None, ALU.mult).then_inc(step, 1)
                    at(p, "average")
                    v.tensor_tensor(oa[:, :, 0:28], oa[:, :, 0:28], bc(st[:, 1], [1, NC * 8], [0, 28]),
                                    ALU.mult).then_inc(step, 1)
                    at(p, "average v")
                    v.tensor_scalar(V, V, 3.0 ** 0.5, None, ALU.mult).then_inc(step, 1)
                    at(p, "sum s")
                    v.tensor_reduce(bn[:, 0, 0:NS], bc(oa[:, 0, 0:1], [1, NS], [FA, NC * 8]), AX.X,
                                    ALU.add).then_inc(step, 1)
                if p == "conv1":
                    at(p, "average")
                    v.tensor_tensor(T0, turned, nodes(st[:, 5]), ALU.mult).then_inc(step, 1)
                    at(p, "norm 20")
                    v.tensor_scalar(T0, T0, (NS + NV) ** -0.5, None, ALU.mult).then_inc(step, 1)
                    at(p, "sum s")
                    v.tensor_reduce(bn[:, 0, 0:NS], bc(t0[:, 0, 0:1], [1, NS], [32, NC * 8]), AX.X,
                                    ALU.add).then_inc(step, 1)
                    S = T0
                if p in ("conv0", "conv1"):
                    at(p, "mean s")
                    v.tensor_scalar(bn[:, 1, 0:NS], hidden[0:NP, 0, 0:NS], 1.0 / N, None, ALU.mult).then_inc(step, 1)
                    at(p, "centered")
                    v.tensor_tensor(T0, S, feats(bn[:, 1, 0:NS]), ALU.subtract).then_inc(step, 1)
                    at(p, "masked")
                    v.tensor_tensor(T0, T0, nodes(mask[:]), ALU.mult).then_inc(step, 1)
                    at(p, "squares")
                    v.tensor_tensor(T1, T0, T0, ALU.mult).then_inc(step, 1)
                    if p == "conv0":
                        at(p, "squares v")
                        v.tensor_tensor(t1[:, :, NS:NS + 12], V, V, ALU.mult).then_inc(step, 1)
                    at(p, "sum sq s")
                    v.tensor_reduce(bn[:, 2, 0:NS], bc(t1[:, 0, 0:1], [1, NS], [32, NC * 8]), AX.X,
                                    ALU.add).then_inc(step, 1)
                    if p == "conv0":
                        at(p, "sum sq v")
                        v.tensor_reduce(bn[:, 2, NS:NS + NV], bc(t1[:, 0, NS:NS + 1], [3, NV], [32, NC * 8], [1, 3]),
                                        AX.XY, ALU.add).then_inc(step, 1)
                    at(p, "var s")
                    v.tensor_scalar(bn[:, 4, 0:NS], hidden[0:NP, 1, 0:NS], 1.0 / N, None, ALU.mult).then_inc(step, 1)
                    if p == "conv0":
                        at(p, "var v")
                        v.tensor_scalar(bn[:, 4, NS:], hidden[0:NP, 1, NS:NS + NV], 1.0 / (3 * N), None,
                                        ALU.mult).then_inc(step, 1)
                    w = NS + NV if p == "conv0" else NS
                    g0 = 0 if p == "conv0" else 2 * NS + NV
                    b0 = g0 + w
                    at(p, "rstd")
                    v.reciprocal(bn[:, 6, 0:w], bn[:, 5, 0:w]).then_inc(step, 1)
                    at(p, "gain")
                    v.tensor_tensor(bn[:, 7, 0:w], bn[:, 6, 0:w], norms[:, g0:g0 + w], ALU.mult).then_inc(step, 1)
                    at(p, "scaled")
                    v.tensor_tensor(T0, T0, feats(bn[:, 7, 0:NS]), ALU.mult).then_inc(step, 1)
                    at(p, "shift")
                    to = t1[:, :, 12:28] if p == "conv0" else T1
                    v.tensor_tensor(to, T0, feats(norms[:, b0:b0 + NS]), ALU.add).then_inc(step, 1)
                    if p == "conv0":
                        at(p, "scaled v")
                        v.tensor_tensor(t1[:, :, 0:12].rearrange("p n (j c) -> p n j c", c=3),
                                        V.rearrange("p n (j c) -> p n j c", c=3),
                                        bc(bn[:, 7, NS:NS + NV], [0, NC * 8], [1, NV], [0, 3]), ALU.mult).then_inc(step, 1)
                    else:
                        at(p, "add")
                        v.tensor_tensor(xs[:], xs[:], T1, ALU.add).then_inc(step, 1)


def kernel(**inputs):
    import numpy as np
    import concourse.bacc as bacc
    from concourse.bass_utils import run_bass_kernel_spmd

    a = {k: np.asarray(v) for k, v in inputs.items()}

    def edges(v, fill):
        full = np.full((128 * T,) + v.shape[1:], fill, v.dtype)
        full[:E] = v
        return full.reshape((128, T) + v.shape[1:])

    def columns(v):
        return np.ascontiguousarray(edges(v, 0).transpose(2, 1, 0)).reshape(v.shape[1], T * 128)

    def diagonal(w):
        r, c = w.shape
        full = np.zeros((8, r, 8, c), w.dtype)
        for h in range(8):
            full[h, :, h, :] = w
        return full.reshape(8 * r, 8 * c)

    def with_bias(w, b):
        full = np.zeros((128, w.shape[1]), w.dtype)
        full[:len(w)] = w
        full[len(w)] = b
        return full

    def hidden_weights(w, b):
        full = np.zeros((2, 64, 2, 64), w.dtype)
        for h in range(2):
            full[h, :, h, :DA] = with_bias(w, b)[:64]
            full[h, DA, h, DA] = 1
        return full.reshape(128, 128)

    def for_halves(w):
        return np.stack([w, np.concatenate([w[64:], w[:64]])], 1)

    def out_major(w, i, o):
        return w.reshape(w.shape[0], i, o).transpose(0, 2, 1).reshape(w.shape[0], i * o)

    x = np.zeros((NPAD, D), a["x"].dtype)
    x[:N] = a["x"]
    f0 = with_bias(a["L3_gnn_fc0_w2"], a["L3_gnn_fc0_b2"])
    f1 = with_bias(a["L3_gnn_fc1_w2"], a["L3_gnn_fc1_b2"])
    emb = a["L1_gnn_edge_emb"].reshape(NTYPE, D, D).transpose(2, 0, 1).reshape(D, NTYPE * D)
    arrays = {
        "x": x,
        "src": edges(a["src"], PADNODE),
        "dst": edges(a["dst"], PADNODE),
        "etype": edges(a["edge_type_8"], 0),
        "weight": edges(a["edge_weight"], 0),
        "vec": edges(a["edge_attr_3"], 0).reshape(128, T * 3),
        "ea16": columns(a["edge_attr_16"]),
        "ea48": columns(a["edge_attr_48"]),
        "net_w": with_bias(a["L0_gnn_kernel"], a["L0_gnn_bias"]),
        "types_w": diagonal(emb),
        "ih_w": diagonal(a["L1_gnn_w_ih"].T),
        "hh_w": diagonal(a["L1_gnn_w_hh"].T),
        "ih_b": np.tile(a["L1_gnn_b_ih"], 8)[None, :],
        "hh_b": np.tile(a["L1_gnn_b_hh"], 8)[None, :],
        "w1": np.stack([hidden_weights(a[f"L3_gnn_fc{k}_w1"], a[f"L3_gnn_fc{k}_b1"]) for k in range(2)]),
        "w2": np.stack([
            for_halves(np.concatenate([out_major(f0[:, NS * NS:], NS, NV), out_major(f0[:, :NS * NS], NS, NS)], 1)),
            for_halves(out_major(f1, NS + NV, NS))]),
        "by_type": np.tile(a["L1_gnn_edge_emb"].reshape(NTYPE, D, D).transpose(2, 1, 0).reshape(D, D * NTYPE), (8, 1)),
        "src_rows": edges(a["src"], PADNODE).T.reshape(128, T),
        "gs0": a["L3_gnn_bn0_gs"], "bs0": a["L3_gnn_bn0_bs"], "gv0": a["L3_gnn_bn0_gv"],
        "gs1": a["L3_gnn_bn1_gs"], "bs1": a["L3_gnn_bn1_bs"],
    }
    nc = bacc.Bacc("TRN2", target_bir_lowering=False, num_devices=1)
    feed, args = {}, []
    for name, v in arrays.items():
        v = np.ascontiguousarray(v)
        feed[f"in_{name}"] = v
        args.append(nc.dram_tensor(f"in_{name}", v.shape, mybir.dt.from_np(v.dtype), kind="ExternalInput").ap())
    args.append(nc.dram_tensor("out_x", (NPAD, D), F32, kind="ExternalOutput").ap())
    gnn_kernel(nc, *args)
    r = run_bass_kernel_spmd(nc, [feed], core_ids=[0])
    return r.results[0]["out_x"][:N]
```
